# Optimizing a Trainium2 kernel written in Bass

```python
import numpy as np
import jax
import jax.numpy as jnp

def _softmax(x, axis=-1):
    return jax.nn.softmax(x, axis=axis)

def _gelu(x):
    return jax.nn.gelu(x, approximate=True)

def _silu(x):
    return jax.nn.silu(x)

def _sigmoid(x):
    return jax.nn.sigmoid(x)

def _layernorm(x, axis=-1, eps=1e-05):
    m = jnp.mean(x, axis=axis, keepdims=True)
    v = jnp.var(x, axis=axis, keepdims=True)
    return (x - m) / jnp.sqrt(v + eps)

def _scatter_add(tgt, idx, src, axis=0):
    return tgt.at[idx].add(src)

def _segment_sum(src, seg, n):
    return jax.ops.segment_sum(src, seg, n)
kernel_name = 'mk_recurrent_d1_jaxref_r4_a7c597'

def setup_inputs(seed: int=0):
    np.random.seed(seed)
    _w = jnp.asarray

    def _L0_attn_setup():
        import jax, jax.numpy as jnp
        import numpy as np
        DIM = 1024
        N_HEADS = 32
        N_KV_HEADS = 8
        HEAD_DIM = DIM // N_HEADS
        N_REP = N_HEADS // N_KV_HEADS
        THETA = 10000.0
        B, S = (4, 256)

        def _rope_cos_sin(seq_len):
            freqs = 1.0 / THETA ** (jnp.arange(0, HEAD_DIM, 2, dtype=jnp.float32) / HEAD_DIM)
            t = jnp.arange(seq_len, dtype=jnp.float32)
            ang = jnp.outer(t, freqs)
            return (jnp.cos(ang), jnp.sin(ang))

        def _apply_rope(x, cos, sin):
            xr = x[..., 0::2]
            xi = x[..., 1::2]
            c = cos[None, :, None, :]
            s = sin[None, :, None, :]
            out_r = xr * c - xi * s
            out_i = xr * s + xi * c
            return jnp.stack([out_r, out_i], axis=-1).reshape(x.shape)
        key = jax.random.key(seed)
        ks = jax.random.split(key, 5)
        sc = 1.0 / np.sqrt(DIM).astype(np.float32)
        x = jax.random.normal(ks[0], (B, S, DIM), jnp.float32)
        wq = jax.random.normal(ks[1], (DIM, N_HEADS * HEAD_DIM), jnp.float32) * sc
        wk = jax.random.normal(ks[2], (DIM, N_KV_HEADS * HEAD_DIM), jnp.float32) * sc
        wv = jax.random.normal(ks[3], (DIM, N_KV_HEADS * HEAD_DIM), jnp.float32) * sc
        wo = jax.random.normal(ks[4], (N_HEADS * HEAD_DIM, DIM), jnp.float32) * sc
        return {'x': x, 'wq': wq, 'wk': wk, 'wv': wv, 'wo': wo}
    _L0_attn_in = _L0_attn_setup()

    def _L0_ffn_setup():
        import jax, jax.numpy as jnp
        import numpy as np
        HIDDEN = 1024
        INTER = 2752
        GROUP = 128
        B, S = (4, 512)
        NIB = jnp.uint32(15)

        def _pack_rows(nib):
            r = nib.reshape(-1, 8, nib.shape[-1])
            shifts = (jnp.arange(8, dtype=jnp.uint32) * 4)[None, :, None]
            return jnp.sum(r << shifts, axis=1, dtype=jnp.uint32)

        def _pack_cols(nib):
            r = nib.reshape(nib.shape[0], -1, 8)
            shifts = (jnp.arange(8, dtype=jnp.uint32) * 4)[None, None, :]
            return jnp.sum(r << shifts, axis=2, dtype=jnp.uint32)

        def _dequant(qw, qz, sc, g_idx):
            shifts = jnp.arange(8, dtype=jnp.uint32) * 4
            wq = qw[:, None, :] >> shifts[None, :, None] & NIB
            wq = wq.reshape(-1, qw.shape[1]).astype(jnp.float32)
            zq = qz[:, :, None] >> shifts[None, None, :] & NIB
            zq = zq.reshape(qz.shape[0], -1).astype(jnp.float32) + 1.0
            return sc[g_idx] * (wq - zq[g_idx])
        key = jax.random.key(seed)
        ks = jax.random.split(key, 7)
        n_groups = HIDDEN // GROUP
        n_groups_d = INTER // GROUP
        x = jax.random.normal(ks[0], (B, S, HIDDEN), jnp.float32)
        nib_w_gu = jax.random.randint(ks[1], (HIDDEN, 2 * INTER), 0, 16).astype(jnp.uint32)
        nib_z_gu = jax.random.randint(ks[2], (n_groups, 2 * INTER), 0, 15).astype(jnp.uint32)
        qweight_gu = _pack_rows(nib_w_gu)
        qzeros_gu = _pack_cols(nib_z_gu)
        scales_gu = jax.random.uniform(ks[3], (n_groups, 2 * INTER), jnp.float32, 0.005, 0.02)
        g_idx_gu = jnp.arange(HIDDEN, dtype=jnp.int32) // GROUP
        nib_w_d = jax.random.randint(ks[4], (INTER, HIDDEN), 0, 16).astype(jnp.uint32)
        nib_z_d = jax.random.randint(ks[5], (n_groups_d, HIDDEN), 0, 15).astype(jnp.uint32)
        qweight_down = _pack_rows(nib_w_d)
        qzeros_down = _pack_cols(nib_z_d)
        scales_down = jax.random.uniform(ks[6], (n_groups_d, HIDDEN), jnp.float32, 0.005, 0.02)
        g_idx_down = jnp.arange(INTER, dtype=jnp.int32) // GROUP
        return {'x': x, 'qweight_gu': qweight_gu, 'qzeros_gu': qzeros_gu, 'scales_gu': scales_gu, 'g_idx_gu': g_idx_gu, 'qweight_down': qweight_down, 'qzeros_down': qzeros_down, 'scales_down': scales_down, 'g_idx_down': g_idx_down}
    _L0_ffn_in = _L0_ffn_setup()
    _d = {'L0_attn_x': _L0_attn_in['x'], 'L0_attn_wq': _L0_attn_in['wq'], 'L0_attn_wk': _L0_attn_in['wk'], 'L0_attn_wv': _L0_attn_in['wv'], 'L0_attn_wo': _L0_attn_in['wo'], 'L0_ffn_qweight_gu': _L0_ffn_in['qweight_gu'], 'L0_ffn_qzeros_gu': _L0_ffn_in['qzeros_gu'], 'L0_ffn_scales_gu': _L0_ffn_in['scales_gu'], 'L0_ffn_g_idx_gu': _L0_ffn_in['g_idx_gu'], 'L0_ffn_qweight_down': _L0_ffn_in['qweight_down'], 'L0_ffn_qzeros_down': _L0_ffn_in['qzeros_down'], 'L0_ffn_scales_down': _L0_ffn_in['scales_down'], 'L0_ffn_g_idx_down': _L0_ffn_in['g_idx_down']}
    _x0 = _d['L0_attn_x']
    _d['L0_attn_x'] = jax.random.normal(jax.random.fold_in(jax.random.key(seed), 1), (2, 1024, 1024), dtype=_x0.dtype)
    del _x0
    return _d

def reference(L0_attn_x, L0_attn_wq, L0_attn_wk, L0_attn_wv, L0_attn_wo, L0_ffn_qweight_gu, L0_ffn_qzeros_gu, L0_ffn_scales_gu, L0_ffn_g_idx_gu, L0_ffn_qweight_down, L0_ffn_qzeros_down, L0_ffn_scales_down, L0_ffn_g_idx_down):

    def _L0_attn_ref(x, wq, wk, wv, wo):
        import jax, jax.numpy as jnp
        import numpy as np
        DIM = 1024
        N_HEADS = 32
        N_KV_HEADS = 8
        HEAD_DIM = DIM // N_HEADS
        N_REP = N_HEADS // N_KV_HEADS
        THETA = 10000.0
        B, S = (4, 256)

        def _rope_cos_sin(seq_len):
            freqs = 1.0 / THETA ** (jnp.arange(0, HEAD_DIM, 2, dtype=jnp.float32) / HEAD_DIM)
            t = jnp.arange(seq_len, dtype=jnp.float32)
            ang = jnp.outer(t, freqs)
            return (jnp.cos(ang), jnp.sin(ang))

        def _apply_rope(x, cos, sin):
            xr = x[..., 0::2]
            xi = x[..., 1::2]
            c = cos[None, :, None, :]
            s = sin[None, :, None, :]
            out_r = xr * c - xi * s
            out_i = xr * s + xi * c
            return jnp.stack([out_r, out_i], axis=-1).reshape(x.shape)
        bsz, seq_len, _ = x.shape
        q = (x @ wq).reshape(bsz, seq_len, N_HEADS, HEAD_DIM)
        k = (x @ wk).reshape(bsz, seq_len, N_KV_HEADS, HEAD_DIM)
        v = (x @ wv).reshape(bsz, seq_len, N_KV_HEADS, HEAD_DIM)
        cos, sin = _rope_cos_sin(seq_len)
        q = _apply_rope(q, cos, sin)
        k = _apply_rope(k, cos, sin)
        k = jnp.repeat(k, N_REP, axis=2)
        v = jnp.repeat(v, N_REP, axis=2)
        scores = jnp.einsum('bqhd,bkhd->bhqk', q, k) / np.float32(np.sqrt(HEAD_DIM))
        mask = jnp.triu(jnp.full((seq_len, seq_len), -jnp.inf, dtype=scores.dtype), k=1)
        scores = scores + mask
        attn = jax.nn.softmax(scores.astype(jnp.float32), axis=-1).astype(q.dtype)
        out = jnp.einsum('bhqk,bkhd->bqhd', attn, v).reshape(bsz, seq_len, N_HEADS * HEAD_DIM)
        return out @ wo

    def _L0_ffn_ref(x, qweight_gu, qzeros_gu, scales_gu, g_idx_gu, qweight_down, qzeros_down, scales_down, g_idx_down):
        import jax, jax.numpy as jnp
        import numpy as np
        HIDDEN = 1024
        INTER = 2752
        GROUP = 128
        B, S = (4, 512)
        NIB = jnp.uint32(15)

        def _pack_rows(nib):
            r = nib.reshape(-1, 8, nib.shape[-1])
            shifts = (jnp.arange(8, dtype=jnp.uint32) * 4)[None, :, None]
            return jnp.sum(r << shifts, axis=1, dtype=jnp.uint32)

        def _pack_cols(nib):
            r = nib.reshape(nib.shape[0], -1, 8)
            shifts = (jnp.arange(8, dtype=jnp.uint32) * 4)[None, None, :]
            return jnp.sum(r << shifts, axis=2, dtype=jnp.uint32)

        def _dequant(qw, qz, sc, g_idx):
            shifts = jnp.arange(8, dtype=jnp.uint32) * 4
            wq = qw[:, None, :] >> shifts[None, :, None] & NIB
            wq = wq.reshape(-1, qw.shape[1]).astype(jnp.float32)
            zq = qz[:, :, None] >> shifts[None, None, :] & NIB
            zq = zq.reshape(qz.shape[0], -1).astype(jnp.float32) + 1.0
            return sc[g_idx] * (wq - zq[g_idx])
        w_gu = _dequant(qweight_gu, qzeros_gu, scales_gu, g_idx_gu)
        inter = jnp.einsum('bsh,hf->bsf', x, w_gu)
        gate, up = (inter[..., :INTER], inter[..., INTER:])
        h = jax.nn.silu(gate) * up
        w_d = _dequant(qweight_down, qzeros_down, scales_down, g_idx_down)
        return jnp.einsum('bsf,fh->bsh', h, w_d)
    x = L0_attn_x
    xn = _layernorm(x, axis=-1)
    s = _L0_attn_ref(xn, L0_attn_wq, L0_attn_wk, L0_attn_wv, L0_attn_wo)
    g = _silu(_L0_ffn_ref(xn, L0_ffn_qweight_gu, L0_ffn_qzeros_gu, L0_ffn_scales_gu, L0_ffn_g_idx_gu, L0_ffn_qweight_down, L0_ffn_qzeros_down, L0_ffn_scales_down, L0_ffn_g_idx_down))
    x = x + s * g
    return x

_drawn_inputs = setup_inputs


def setup_inputs(seed=0):
    import zlib

    import numpy as np

    out = dict(_drawn_inputs(seed))
    spreads = {}
    factors = {}
    for name, (base, spread) in spreads.items():
        noise = np.random.default_rng([zlib.crc32(name.encode()), seed]).standard_normal(out[name].shape)
        drawn = base * np.exp(spread * noise) if base else spread * noise
        out[name] = jnp.asarray(drawn.astype(out[name].dtype))
    for name, factor in factors.items():
        out[name] = (out[name] * factor).astype(out[name].dtype)
    return out
```

```python
from contextlib import ExitStack

import numpy as np

import concourse.bass as bass
from concourse import mybir

ALU = mybir.AluOpType
ACT = mybir.ActivationFunctionType
AX_X = mybir.AxisListType.X
F32 = mybir.dt.float32
F16 = mybir.dt.float16
BF16 = mybir.dt.bfloat16
I32 = mybir.dt.int32
U32 = mybir.dt.uint32

P = 128
B, S, D = 2, 1024, 1024
T = B * S
TT = T // P
ST = S // P
KT = D // P
HEADS, KV, HD = 32, 8, 32
REP = HEADS // KV
GROUPS = B * KV
QKV = (HEADS + 2 * KV) * HD
QK = HEADS + KV
HALF = HD // 2
STACK = 3 * HD
VH = HD + 1
VW = VH + HD
EPS = 1e-5
THETA = 10000.0
BANK = 512
FULL = 1024

INTER = 2752
G_GU, G_D = 8, 21
NIB = 8
FTILES = (INTER + P - 1) // P
FLAST = INTER - (FTILES - 1) * P
CHUNK = 2
CHUNKS = FTILES // CHUNK
TC = T // BANK

W_SCALE = 64.0
H_SCALE = 1.0 / 16.0
MASKED = -1e30


def at(m, u, off, unroll=2):
    k = u + off
    return m + k // unroll, k % unroll


def inside(m, u, n, unroll=2):
    return not isinstance(m, int) or 0 <= unroll * m + u < n


def wait_alone(eng, sem, count, seen):
    eng.wait_ge(sem, count)
    eng.sem_inc(seen, 1)


def make_masks(pool, ident, identb, maskb, zeros_done, masks_done):
    pool.memset(ident[:, :], 1.0)
    pool.memset(identb[:, :], 1.0)
    pool.memset(maskb[:, :], 0.0).then_inc(zeros_done, 1)
    pool.wait_ge(zeros_done, 1)
    pool.affine_select(out=ident[:, :], in_=ident[:, :], pattern=[[-1, P]], compare_op=ALU.is_equal,
                       fill=0.0, base=0, channel_multiplier=1)
    pool.affine_select(out=identb[:, :], in_=identb[:, :], pattern=[[-1, P]], compare_op=ALU.is_equal,
                       fill=0.0, base=0, channel_multiplier=1)
    pool.affine_select(out=maskb[:, :], in_=maskb[:, :], pattern=[[-1, P]], compare_op=ALU.is_ge,
                       fill=MASKED, base=0, channel_multiplier=1).then_inc(masks_done, 1)


def project_qkv(nc, x, wq, wk, wv, rope, qk_d, v_d, xT, ident, identb, maskb):
    with ExitStack() as ctx:
        def sb(name, shape, dt):
            return ctx.enter_context(nc.sbuf_tensor(name, shape, dt))

        def sem(name):
            return ctx.enter_context(nc.semaphore(name))

        xin = sb("xin", [P, 2, D], F32)
        xn = sb("xn", [P, 2, D], F32)
        xh = sb("xh", [P, 2, D], F16)
        xl = sb("xl", [P, 2, D], F16)
        bn = sb("bn", [P, 2, 6], F32)
        mv = sb("mv", [P, 2, 2], F32)
        std = sb("std", [P, 2, 1], F32)
        rstd = sb("rstd", [P, 2, 1], F32)
        eps = sb("eps", [P, 1], F32)
        xTc = sb("xTc", [P, 2, 2, KT, P], F16)
        w_in = sb("w_in", [P, 2, QKV], F32)
        w = sb("w", [P, 2, KT, QKV], F16)
        cs = sb("cs", [P, TT, 2, HALF], F32)
        rot_t = sb("rot_t", [P, 4, QK, HALF], F32)
        rot = sb("rot", [P, QK, 2, HALF], F32)
        stack = sb("stack", [P, 2, QK, STACK], F16)
        v = sb("v", [P, 2, KV, VW], F16)
        qkv_ps = [ctx.enter_context(nc.psum_tensor(f"qkv_ps{i}", [P, QKV], F32)) for i in range(2)]
        tr_ps = [ctx.enter_context(nc.psum_tensor(f"tr_ps{i}", [P, KT, P], F16)) for i in range(2)]

        x_loaded = [sem(f"x_loaded{i}") for i in range(2)]
        w_loaded = [sem(f"w_loaded{i}") for i in range(2)]
        cs_loaded = sem("cs_loaded")
        whi_done = sem("whi_done")
        wlo_done = sem("wlo_done")
        zeros_done = sem("zeros_done")
        masks_done = sem("masks_done")
        ones_set = sem("ones_set")
        eps_set = sem("eps_set")
        bn_done = sem("bn_done")
        bn_seen = sem("bn_seen")
        hi_seen = sem("hi_seen")
        mv_done = sem("mv_done")
        std_done = sem("std_done")
        rstd_done = sem("rstd_done")
        xn_done = sem("xn_done")
        xh_done = sem("xh_done")
        xl_done = sem("xl_done")
        xh_turned = sem("xh_turned")
        xl_turned = sem("xl_turned")
        xTh_done = sem("xTh_done")
        xTl_done = sem("xTl_done")
        xT_kept = sem("xT_kept")
        qkv_done = sem("qkv_done")
        mult_done = sem("mult_done")
        rot_done = sem("rot_done")
        v_done = sem("v_done")
        vlo_done = sem("vlo_done")
        hi_done = sem("hi_done")
        dup_done = sem("dup_done")
        lo_done = sem("lo_done")
        stored = [sem(f"stored{i}") for i in range(2)]
        qk_v = qk_d.rearrange("b g p t c -> b t p g c")
        v_v = v_d.rearrange("b g p t c -> b t p g c")

        w_parts = [(wq.rearrange("(p s) n -> p s n", s=KT), 0, HEADS * HD),
                   (wk.rearrange("(p s) n -> p s n", s=KT), HEADS * HD, KV * HD),
                   (wv.rearrange("(p s) n -> p s n", s=KT), QK * HD, KV * HD)]
        x_v = x.rearrange("b (t p) d -> (b t) p d", p=P)

        block = ctx.enter_context(nc.Block())

        @block.sync
        def _(sp):
            def load_x(m, u):
                if not inside(m, u, TT):
                    return
                if not isinstance(m, int) or m >= 1:
                    sp.wait_ge(xn_done, 2 * m + u - 1)
                sp.dma_start(xin[:, u, :], x_v[2 * m + u]).then_inc(x_loaded[u], 16)

            load_x(0, 0)
            load_x(0, 1)
            sp.dma_start(cs[:, :, :, :], rope.rearrange("p (t c f) -> p t c f", t=TT, c=2)).then_inc(cs_loaded, 16)
            for s in range(KT):
                if s >= 2:
                    sp.wait_ge(wlo_done, s - 1)
                for w_dram, c0, n in w_parts:
                    sp.dma_start(w_in[:, s % 2, c0:c0 + n], w_dram[:, s, :]).then_inc(w_loaded[s % 2], 16)
            load_x(1, 0)
            load_x(1, 1)

            def step(b, m, u, ahead):
                n = b * ST + 2 * m + u
                sp.wait_ge(lo_done, n + 1)
                sp.wait_ge(dup_done, n + 1)
                sp.wait_ge(vlo_done, n + 1)
                sp.dma_start(qk_v[b, 2 * m + u, :, :, 0:REP * STACK],
                             stack[:, u, 0:HEADS, :].rearrange("p (g r) c -> p g (r c)", r=REP)
                             ).then_inc(stored[u], 16)
                sp.dma_start(qk_v[b, 2 * m + u, :, :, REP * STACK:],
                             stack[:, u, HEADS:QK, :]).then_inc(stored[u], 16)
                sp.dma_start(v_v[b, 2 * m + u], v[:, u, :, :]).then_inc(stored[u], 16)

            half = ST // 2
            with sp.Fori(0, half) as m:
                for u in range(2):
                    load_x(m + 2, u)
                    step(0, m, u, True)
            with sp.Fori(0, half - 2) as m:
                for u in range(2):
                    load_x(m + 2 + half, u)
                    step(1, m, u, True)
            for m in range(half - 2, half):
                for u in range(2):
                    step(1, m, u, False)
            for u in range(2):
                sp.wait_ge(stored[u], 16 * 3 * TT // 2)

        @block.gpsimd
        def _(pool):
            pool.memset(v[:, :, :, HD:VH], 1.0).then_inc(ones_set, 1)
            make_masks(pool, ident, identb, maskb, zeros_done, masks_done)

            def low(m, u):
                if not inside(m, u, TT):
                    return
                n = 2 * m + u
                pool.wait_ge(xh_done, n + 1)
                if not isinstance(m, int) or m >= 1:
                    pool.wait_ge(xl_turned, n - 1)
                pool.tensor_tensor(xl[:, u, :], xn[:, u, :], xh[:, u, :], ALU.subtract).then_inc(xl_done, 1)

            def keep(m, u):
                if not inside(m, u, TT):
                    return
                n = 2 * m + u
                pool.wait_ge(xTh_done, n + 1)
                pool.wait_ge(xTl_done, n + 1)
                for part in range(2):
                    last = pool.tensor_copy(xT[:, part, :, bass.ds(n * P, P)], xTc[:, u, part, :, :])
                last.then_inc(xT_kept, 1)

            def dup(m, u):
                if not inside(m, u, TT):
                    return
                n = 2 * m + u
                wait_alone(pool, hi_done, n + 1, hi_seen)
                pool.tensor_copy(stack[:, u, 0:HEADS, HD:2 * HD], stack[:, u, 0:HEADS, 0:HD])
                pool.tensor_copy(stack[:, u, HEADS:QK, 2 * HD:STACK],
                                 stack[:, u, HEADS:QK, 0:HD]).then_inc(dup_done, 1)

            def step(m, u):
                low(*at(m, u, 2))
                keep(*at(m, u, 1))
                dup(m, u)

            step(-1, 0)
            step(-1, 1)
            step(0, 0)
            step(0, 1)
            with pool.Fori(1, TT // 2 - 1) as m:
                step(m, 0)
                step(m, 1)
            step(TT // 2 - 1, 0)
            step(TT // 2 - 1, 1)

        @block.scalar
        def _(act):
            def deviation(m, u):
                n = 2 * m + u
                act.wait_ge(mv_done, n + 1)
                act.activation(std[:, u, :], mv[:, u, 1:2], ACT.Sqrt, bias=eps[:, :]).then_inc(std_done, 1)

            def norm(m, u):
                if not inside(m, u, TT):
                    return
                n = 2 * m + u
                deviation(m, u)
                act.wait_ge(xn_done, n + 1)
                if not isinstance(m, int) or m >= 1:
                    act.wait_ge(xh_turned, n - 1)
                    act.wait_ge(xl_done, n - 1)
                act.activation(xh[:, u, :], xn[:, u, :], ACT.Copy).then_inc(xh_done, 1)

            def turned(m, u):
                if not inside(m, u, TT):
                    return
                n = 2 * m + u
                act.wait_ge(xh_turned, n + 1)
                if not isinstance(m, int) or m >= 1:
                    act.wait_ge(qkv_done, n - 1)
                    act.wait_ge(xT_kept, n - 1)
                act.activation(xTc[:, u, 0, :, :], tr_ps[0][:, :, :], ACT.Copy).then_inc(xTh_done, 1)

            def post(m, u):
                if not inside(m, u, TT):
                    return
                n = 2 * m + u
                act.wait_ge(mult_done, n + 1)
                if not isinstance(m, int) or m >= 1:
                    act.wait_ge(stored[u], 48 * m)
                act.activation(v[:, u, :, 0:HD],
                               qkv_ps[u][:, QK * HD:QKV].rearrange("p (h c) -> p h c", h=KV),
                               ACT.Copy, scale=1.0 / W_SCALE).then_inc(v_done, 1)
                act.wait_ge(rot_done, n + 1)
                act.activation(stack[:, u, :, 0:HD], rot[:, :, :, :].rearrange("p h c f -> p h (c f)"),
                               ACT.Copy).then_inc(hi_done, 1)

            def step(m, u):
                norm(*at(m, u, 2))
                turned(*at(m, u, 1))
                post(m, u)

            act.wait_ge(eps_set, 1)
            act.wait_ge(ones_set, 1)
            norm(0, 0)
            for s in range(KT):
                act.wait_ge(w_loaded[s % 2], 48 * (s // 2 + 1))
                act.activation(w[:, 0, s, :], w_in[:, s % 2, :], ACT.Copy, scale=W_SCALE).then_inc(whi_done, 1)
            turned(0, 0)
            norm(0, 1)
            step(0, 0)
            step(0, 1)
            with act.Fori(1, TT // 2 - 1) as m:
                step(m, 0)
                step(m, 1)
            step(TT // 2 - 1, 0)
            step(TT // 2 - 1, 1)

        @block.vector
        def _(dve):
            def norm(m, u):
                if not inside(m, u, TT):
                    return
                n = 2 * m + u
                dve.wait_ge(x_loaded[u], 16 * (m + 1))
                for h in range(2):
                    last = dve.bn_stats(bn[:, h, :], xin[:, u, h * BANK:(h + 1) * BANK])
                last.then_inc(bn_done, 1)
                wait_alone(dve, bn_done, n + 1, bn_seen)
                dve.bn_aggr(mv[:, u, :], bn[:, :, :]).then_inc(mv_done, 1)
                dve.wait_ge(std_done, n + 1)
                dve.reciprocal(rstd[:, u, :], std[:, u, :]).then_inc(rstd_done, 1)
                dve.wait_ge(rstd_done, n + 1)
                if not isinstance(m, int) or m >= 1:
                    dve.wait_ge(xl_done, n - 1)
                dve.tensor_scalar(xn[:, u, :], xin[:, u, :], mv[:, u, 0:1], rstd[:, u, :],
                                  ALU.subtract, ALU.mult).then_inc(xn_done, 1)

            def turned(m, u):
                if not inside(m, u, TT):
                    return
                n = 2 * m + u
                dve.wait_ge(xl_turned, n + 1)
                if not isinstance(m, int) or m >= 1:
                    dve.wait_ge(qkv_done, n - 1)
                    dve.wait_ge(xT_kept, n - 1)
                dve.tensor_copy(xTc[:, u, 1, :, :], tr_ps[1][:, :, :]).then_inc(xTl_done, 1)

            def post(m, u):
                if not inside(m, u, TT):
                    return
                n = 2 * m + u
                dve.wait_ge(qkv_done, n + 1)
                pairs = qkv_ps[u][:, 0:QK * HD].rearrange("p (h f c) -> p c h f", h=QK, c=2)
                trig = cs[:, bass.ds(n, 1), :, :].rearrange("p t c f -> p c t f")
                for k, (c, q) in enumerate([(0, 0), (1, 1), (0, 1), (1, 0)]):
                    last = dve.tensor_tensor(rot_t[:, k, :, :], pairs[:, c, :, :],
                                             trig[:, q, :, :].to_broadcast([P, QK, HALF]), ALU.mult)
                last.then_inc(mult_done, 1)
                dve.wait_ge(mult_done, n + 1)
                if not isinstance(m, int) or 2 * m + u >= 1:
                    dve.wait_ge(hi_done, n)
                dve.tensor_tensor(rot[:, :, 0, :], rot_t[:, 0, :, :], rot_t[:, 1, :, :], ALU.subtract)
                dve.tensor_tensor(rot[:, :, 1, :], rot_t[:, 2, :, :], rot_t[:, 3, :, :],
                                  ALU.add).then_inc(rot_done, 1)
                dve.wait_ge(v_done, n + 1)
                dve.scalar_tensor_tensor(v[:, u, :, VH:VW],
                                         qkv_ps[u][:, QK * HD:QKV].rearrange("p (h c) -> p h c", h=KV),
                                         1.0 / W_SCALE, v[:, u, :, 0:HD], ALU.mult, ALU.subtract
                                         ).then_inc(vlo_done, 1)
                dve.wait_ge(hi_done, n + 1)
                full = rot[:, :, :, :].rearrange("p h c f -> p h (c f)")
                dve.tensor_tensor(stack[:, u, 0:HEADS, 2 * HD:STACK], full[:, 0:HEADS, :],
                                  stack[:, u, 0:HEADS, 0:HD], ALU.subtract)
                dve.tensor_tensor(stack[:, u, HEADS:QK, HD:2 * HD], full[:, HEADS:QK, :],
                                  stack[:, u, HEADS:QK, 0:HD], ALU.subtract).then_inc(lo_done, 1)

            def step(m, u):
                norm(*at(m, u, 2))
                turned(*at(m, u, 1))
                post(m, u)

            dve.memset(eps[:, :], EPS).then_inc(eps_set, 1)
            norm(0, 0)
            for s in range(KT):
                dve.wait_ge(whi_done, s + 1)
                dve.scalar_tensor_tensor(w[:, 1, s, :], w_in[:, s % 2, :], W_SCALE, w[:, 0, s, :],
                                         ALU.mult, ALU.subtract).then_inc(wlo_done, 1)
            turned(0, 0)
            norm(0, 1)
            dve.wait_ge(cs_loaded, 16)
            step(0, 0)
            step(0, 1)
            with dve.Fori(1, TT // 2 - 1) as m:
                step(m, 0)
                step(m, 1)
            step(TT // 2 - 1, 0)
            step(TT // 2 - 1, 1)

        @block.tensor
        def _(pe):
            def turn(m, u):
                if not inside(m, u, TT):
                    return
                n = 2 * m + u
                for part, (src, done, free, out) in enumerate([(xh, xh_done, xTh_done, xh_turned),
                                                               (xl, xl_done, xTl_done, xl_turned)]):
                    pe.wait_ge(done, n + 1)
                    if not isinstance(m, int) or n >= 1:
                        pe.wait_ge(free, n)
                    cols = src[:, u, :].rearrange("p (d s) -> p s d", s=KT)
                    for s in range(KT):
                        last = pe.transpose(tr_ps[part][:, s, :], cols[:, s, :], ident[:, :])
                    last.then_inc(out, 1)

            def products(m, u):
                if not inside(m, u, TT):
                    return
                n = 2 * m + u
                pe.wait_ge(xTh_done, n + 1)
                pe.wait_ge(xTl_done, n + 1)
                if not isinstance(m, int) or m >= 1:
                    pe.wait_ge(vlo_done, n - 1)
                    pe.wait_ge(mult_done, n - 1)
                for s in range(KT):
                    for k, (xp, wp) in enumerate([(0, 0), (0, 1), (1, 0)]):
                        for c in range(QKV // BANK):
                            cols = slice(c * BANK, (c + 1) * BANK)
                            last = pe.matmul(qkv_ps[u][:, cols], xTc[:, u, xp, s, :], w[:, wp, s, cols],
                                             start=(s == 0 and k == 0), stop=(s == KT - 1 and k == 2))
                last.then_inc(qkv_done, 1)

            pe.wait_ge(masks_done, 1)
            turn(0, 0)
            pe.wait_ge(whi_done, KT)
            pe.wait_ge(wlo_done, KT)
            for u in range(2):
                turn(*at(0, u, 1))
                products(0, u)
            with pe.Fori(1, TT // 2 - 1) as m:
                for u in range(2):
                    turn(*at(m, u, 1))
                    products(m, u)
            turn(TT // 2 - 1, 1)
            products(TT // 2 - 1, 0)
            products(TT // 2 - 1, 1)


def attend(nc, qk_d, v_d, o_d, ident, identb, maskb):
    NH = B * HEADS
    R = 2 * REP
    POOL_TILES = [0, 1, 2, 3, 7]
    DVE_TILES = [4, 5, 6]
    TB = BANK // P
    SC = [(t, max(c, t * P), c + BANK) for t in range(ST) for c in range(t * P // BANK * BANK, S, BANK)]
    MX = [(t, c, min(c + BANK, (t + 1) * P)) for t in range(ST) for c in range(0, (t + 1) * P, BANK)]
    NC = len(SC)
    SC_BANKS, MX_BANKS = 3, 2
    WIDE = BANK // VW
    OW = WIDE * VW + (ST - WIDE) * VH
    with ExitStack() as ctx:
        def sb(name, shape, dt):
            return ctx.enter_context(nc.sbuf_tensor(name, shape, dt))

        def sem(name):
            return ctx.enter_context(nc.semaphore(name))

        qkn = sb("qkn", [P, 2, ST, (REP + 1) * STACK], F16)
        vn = sb("vn", [P, 2, ST, VW], F16)
        qT = sb("qT", [P, REP, S], F16)
        kT = sb("kT", [P, 2, S], F16)
        probs = sb("probs", [P, 2, ST, S], F32)
        p_hi = probs[:, :, :, :].bitcast(BF16).rearrange("p u t (s c) -> p u t s c", c=2)[:, :, :, :, 1]
        p_lo = sb("p_lo", [P, 2, ST, S], F16)
        shift = sb("shift", [P, 2, ST], F16)
        part = sb("part", [P, 2, ST - TB], F16)
        sums = sb("sums", [P, 2, OW], F32)
        rsum = sb("rsum", [P, ST], F32)
        o_sum = sb("o_sum", [P, WIDE, HD], F32)
        o = sb("o", [P, 2, ST, REP * HD], F32)
        sc_ps = [ctx.enter_context(nc.psum_tensor(f"sc_ps{i}", [P, BANK], F32)) for i in range(SC_BANKS)]
        mx_ps = [ctx.enter_context(nc.psum_tensor(f"mx_ps{i}", [P, BANK], F32)) for i in range(MX_BANKS)]
        o_ps = [ctx.enter_context(nc.psum_tensor(f"o_ps{i}", [P, BANK], F32)) for i in range(2)]
        tr_ps = ctx.enter_context(nc.psum_tensor("tr_ps", [P, S], F16))

        qk_loaded = [sem(f"qk_loaded{i}") for i in range(2)]
        v_loaded = [sem(f"v_loaded{i}") for i in range(2)]
        ones_set = sem("ones_set_a")
        k_done = sem("k_done")
        q_done = sem("q_done")
        mx_ready = sem("mx_ready")
        mx_taken = sem("mx_taken")
        shift_turned = sem("shift_turned")
        shift_done = sem("shift_done")
        q_turned = sem("q_turned")
        k_turned = sem("k_turned")
        sc_ready = sem("sc_ready")
        exp_done = sem("exp_done")
        lo_pool = sem("lo_pool")
        lo_dve = sem("lo_dve")
        p_used = sem("p_used")
        o_copied = sem("o_copied")
        shift_ready = sem("shift_ready")
        rsum_done = sem("rsum_done")
        o_added = sem("o_added")
        o_done = sem("o_done")
        o_stored = [sem(f"o_stored{i}") for i in range(2)]

        block = ctx.enter_context(nc.Block())

        def head(m, r):
            return R * m + r

        def low(eng, m, r, t, done):
            if not exists(m, r):
                return
            eng.wait_ge(exp_done, NC * head(m, r) + chunks_to(t))
            eng.tensor_tensor(p_lo[:, r % 2, t, t * P:], probs[:, r % 2, t, t * P:],
                              p_hi[:, r % 2, t, t * P:], ALU.subtract).then_inc(done, 1)

        def chunks_to(t):
            return sum(c[0] <= t for c in SC)

        def exists(m, r):
            return inside(m, r, NH, R)

        def steps(eng, step):
            for r in range(-3, 0):
                step(*at(0, 0, r, R))
            for r in range(R):
                step(0, r)
            with eng.Fori(1, NH // R - 1) as m:
                for r in range(R):
                    step(m, r)
            for r in range(R + 2):
                step(*at(NH // R - 1, 0, r, R))

        @block.sync
        def _(sp):
            def load_qk(g, u):
                sp.dma_start(qkn[:, u, :, :], qk_d.rearrange("b g p t c -> (b g) p t c")[g]
                             ).then_inc(qk_loaded[u], 16)

            def load_v(g, u):
                sp.dma_start(vn[:, u, :, :], v_d.rearrange("b g p t c -> (b g) p t c")[g]
                             ).then_inc(v_loaded[u], 16)

            def store(g, u):
                sp.wait_ge(o_done, REP * (g + 1))
                sp.dma_start(o_d.rearrange("b g p t c -> (b g) p t c")[g], o[:, u, :, :]
                             ).then_inc(o_stored[u], 16)

            for g in range(2):
                load_qk(g, g)
                load_v(g, g)
            with sp.Fori(0, GROUPS // 2 - 1) as m:
                for u in range(2):
                    g = 2 * m + u
                    sp.wait_ge(q_turned, REP * (g + 1))
                    load_qk(g + 2, u)
                    sp.wait_ge(p_used, ST * REP * (g + 1))
                    load_v(g + 2, u)
                    store(g, u)
            for u in range(2):
                store(GROUPS - 2 + u, u)
            for u in range(2):
                sp.wait_ge(o_stored[u], 16 * GROUPS // 2)

        @block.tensor
        def _(pe):
            def turn_key(m, r):
                if r % REP or not exists(m, r):
                    return
                h, u = head(m, r), r // REP
                if not isinstance(m, int) or h >= 2:
                    pe.wait_ge(shift_done, h - 1)
                pe.wait_ge(qk_loaded[u], 16 * (m + 1))
                for t in range(ST):
                    last = pe.transpose(tr_ps[0:STACK, t * P:(t + 1) * P],
                                        qkn[:, u, t, REP * STACK:], ident[:, :])
                last.then_inc(k_turned, 1)

            def turn(m, r):
                if not exists(m, r):
                    return
                h, u, q = head(m, r), r // REP, r % REP
                if q == 0:
                    pe.wait_ge(k_done, 2 * m + u + 1)
                elif not isinstance(m, int) or h >= 2:
                    pe.wait_ge(shift_done, h - 1)
                else:
                    pe.wait_ge(q_done, h)
                for t in range(ST):
                    last = pe.transpose(tr_ps[0:STACK, t * P:(t + 1) * P],
                                        qkn[:, u, t, q * STACK:(q + 1) * STACK], ident[:, :])
                last.then_inc(q_turned, 1)

            def turn_shifts(m, r):
                if not exists(m, r):
                    return
                h = head(m, r)
                pe.wait_ge(shift_ready, h + 1)
                pe.wait_ge(q_done, min(h + 2, NH) if isinstance(m, int) else h + 2)
                for t in range(ST):
                    last = pe.transpose(tr_ps[STACK:STACK + 1, t * P:(t + 1) * P], shift[:, r % 2, t:t + 1],
                                        ident[:, :])
                last.then_inc(shift_turned, 1)

            def maxima(m, r, slot):
                if not exists(m, r):
                    return
                h, u, q = head(m, r), r // REP, r % REP
                if slot == 0:
                    pe.wait_ge(q_done, h + 1)
                    pe.wait_ge(k_done, 2 * m + u + 1)
                for i, (t, c, e) in enumerate(MX):
                    if t != slot:
                        continue
                    if not isinstance(m, int) or NC * h + i >= MX_BANKS:
                        pe.wait_ge(mx_taken, NC * h + i + 1 - MX_BANKS)
                    bank = mx_ps[i % MX_BANKS]
                    last = pe.matmul(bank[:, 0:e - c], qT[0:STACK, q, t * P:(t + 1) * P], kT[0:STACK, u, c:e],
                                     start=True, stop=(e <= t * P))
                    if e > t * P:
                        last = pe.matmul(bank[:, t * P - c:e - c], identb[:, :], maskb[:, :],
                                         start=False, stop=True)
                    last.then_inc(mx_ready, 1)

            def scores(m, r, slot):
                if not exists(m, r):
                    return
                h, u, q = head(m, r), r // REP, r % REP
                if slot == 0:
                    pe.wait_ge(shift_done, h + 1)
                for i, (t, c, e) in enumerate(SC):
                    if t != slot:
                        continue
                    if not isinstance(m, int) or NC * h + i >= SC_BANKS:
                        pe.wait_ge(exp_done, NC * h + i + 1 - SC_BANKS)
                    bank = sc_ps[i % SC_BANKS]
                    last = pe.matmul(bank[:, 0:e - c], kT[0:STACK + 1, u, t * P:(t + 1) * P],
                                     qT[0:STACK + 1, q, c:e], start=True, stop=(c > t * P))
                    if c == t * P:
                        last = pe.matmul(bank[:, 0:P], maskb[:, :], identb[:, :], start=False, stop=True)
                    last.then_inc(sc_ready, 1)

            def outputs(m, r, k):
                if not exists(m, r):
                    return
                h, u = head(m, r), r // REP
                if k == 0:
                    if r % REP == 0:
                        pe.wait_ge(v_loaded[u], 16 * (m + 1))
                    if not isinstance(m, int) or h >= 2:
                        pe.wait_ge(o_copied, h - 1)
                if k in POOL_TILES:
                    pe.wait_ge(lo_pool, len(POOL_TILES) * h + POOL_TILES.index(k) + 1)
                else:
                    pe.wait_ge(lo_dve, len(DVE_TILES) * h + DVE_TILES.index(k) + 1)
                bank = o_ps[r % 2]
                for t in range(k, ST):
                    hi, lo = p_hi[:, r % 2, k, t * P:(t + 1) * P], p_lo[:, r % 2, k, t * P:(t + 1) * P]
                    c = min(t, WIDE) * VW + max(t - WIDE, 0) * VH
                    if t < WIDE:
                        pe.matmul(bank[:, c:c + VW], hi, vn[:, u, k, :], start=(k + t == 0), stop=False)
                    else:
                        pe.matmul(bank[:, c:c + VH], hi, vn[:, u, k, 0:VH], start=False, stop=False)
                        pe.matmul(bank[:, c:c + HD], hi, vn[:, u, k, VH:VW], start=False, stop=False)
                    last = pe.matmul(bank[:, c:c + VH], lo, vn[:, u, k, 0:VH], start=False,
                                     stop=(k == ST - 1))
                last.then_inc(p_used, 1)

            pe.wait_ge(ones_set, 1)

            def step(m, r):
                for t in range(ST):
                    scores(m, r, t)
                    if t == 1:
                        turn_shifts(*at(m, r, 1, R))
                    if t == 3:
                        turn_key(*at(m, r, 3, R))
                    if t == 5:
                        turn(*at(m, r, 3, R))
                    maxima(*at(m, r, 2, R), t)
                    outputs(*at(m, r, -1, R), t)

            steps(pe, step)

        @block.scalar
        def _(act):
            def key(m, r):
                if r % REP or not exists(m, r):
                    return
                h, u = head(m, r), r // REP
                act.wait_ge(k_turned, 2 * m + u + 1)
                if not isinstance(m, int) or m >= 1:
                    act.wait_ge(sc_ready, NC * (h - REP))
                act.activation(kT[0:STACK, u, :], tr_ps[0:STACK, :], ACT.Copy).then_inc(k_done, 1)

            def queries(m, r):
                if not exists(m, r):
                    return
                h = head(m, r)
                act.wait_ge(q_turned, h + 1)
                if not isinstance(m, int) or h >= REP:
                    act.wait_ge(sc_ready, NC * (h - REP + 1))
                act.activation(qT[0:STACK, r % REP, :], tr_ps[0:STACK, :], ACT.Copy).then_inc(q_done, 1)

            def exps(m, r, slot):
                if not exists(m, r):
                    return
                h = head(m, r)
                if not isinstance(m, int) or h >= 2:
                    act.wait_ge(p_used, ST * (h - 2) + slot + 1)
                for i, (t, c, e) in enumerate(SC):
                    if t == slot:
                        act.wait_ge(sc_ready, NC * h + i + 1)
                        act.activation(probs[:, r % 2, t, c:e], sc_ps[i % SC_BANKS][:, 0:e - c], ACT.Exp,
                                       scale=float(1.0 / np.sqrt(HD))).then_inc(exp_done, 1)

            def shifts(m, r):
                if not exists(m, r):
                    return
                h = head(m, r)
                act.wait_ge(shift_turned, h + 1)
                act.activation(qT[STACK:STACK + 1, r % REP, :], tr_ps[STACK:STACK + 1, :], ACT.Copy
                               ).then_inc(shift_done, 1)

            def copy_sums(m, r):
                if not exists(m, r):
                    return
                h = head(m, r)
                act.wait_ge(p_used, ST * (h + 1))
                if not isinstance(m, int) or h >= 2:
                    act.wait_ge(o_done, h - 1)
                act.activation(sums[:, r % 2, :], o_ps[r % 2][:, 0:OW], ACT.Copy).then_inc(o_copied, 1)

            def step(m, r):
                for t in range(ST):
                    exps(m, r, t)
                    if t == 0:
                        copy_sums(*at(m, r, -2, R))
                    if t == 2:
                        shifts(*at(m, r, 1, R))
                    if t == 4:
                        key(*at(m, r, 3, R))
                    if t == 6:
                        queries(*at(m, r, 3, R))

            steps(act, step)

        @block.vector
        def _(dve):
            dve.memset(kT[STACK:STACK + 1, :, :], 1.0).then_inc(ones_set, 1)

            def maxima(m, r, slot):
                if not exists(m, r):
                    return
                h = head(m, r)
                for i, (t, c, e) in enumerate(MX):
                    if t != slot:
                        continue
                    dve.wait_ge(mx_ready, NC * h + i + 1)
                    if i == 0 and (not isinstance(m, int) or h >= 2):
                        dve.wait_ge(shift_turned, h - 1)
                    out = shift[:, r % 2, t:t + 1] if t < TB else part[:, c // BANK, t - TB:t - TB + 1]
                    dve.tensor_reduce(out, mx_ps[i % MX_BANKS][:, 0:e - c], AX_X, ALU.max,
                                      negate=True).then_inc(mx_taken, 1)
                if slot == ST - 1:
                    dve.wait_ge(mx_taken, NC * (h + 1))
                    dve.tensor_tensor(shift[:, r % 2, TB:ST], part[:, 0, :], part[:, 1, :], ALU.min
                                      ).then_inc(shift_ready, 1)

            def normalise(m, r):
                if not exists(m, r):
                    return
                h, u, q = head(m, r), r // REP, r % REP
                apart = sums[:, r % 2, 0:WIDE * VW].rearrange("p (t c) -> p t c", c=VW)
                rest = sums[:, r % 2, WIDE * VW:]
                dve.wait_ge(o_copied, h + 1)
                dve.reciprocal(rsum[:, 0:WIDE], apart[:, :, HD])
                dve.reciprocal(rsum[:, WIDE:ST], rest[:, HD:VH]).then_inc(rsum_done, 1)
                dve.tensor_tensor(o_sum[:, :, :], apart[:, :, 0:HD], apart[:, :, VH:VW], ALU.add
                                  ).then_inc(o_added, 1)
                if q == 0 and (not isinstance(m, int) or m >= 1):
                    dve.wait_ge(o_stored[u], 16 * m)
                o_q = o[:, u, :, q * HD:(q + 1) * HD]
                dve.wait_ge(rsum_done, h + 1)
                dve.tensor_scalar(o_q[:, WIDE, :], rest[:, 0:HD], rsum[:, WIDE:ST], None, ALU.mult)
                dve.wait_ge(o_added, h + 1)
                dve.tensor_tensor(o_q[:, 0:WIDE, :], o_sum[:, :, :],
                                  rsum[:, 0:WIDE].unsqueeze(2).to_broadcast([P, WIDE, HD]), ALU.mult
                                  ).then_inc(o_done, 1)

            def step(m, r):
                for t in range(ST):
                    maxima(*at(m, r, 2, R), t)
                    if t == 1:
                        normalise(*at(m, r, -2, R))
                    elif t < ST // 2:
                        low(dve, *at(m, r, -1, R), DVE_TILES[max(t - 1, 0)], lo_dve)

            steps(dve, step)

        @block.gpsimd
        def _(pool):
            def step(m, r):
                for t in POOL_TILES:
                    low(pool, m, r, t, lo_pool)

            steps(pool, step)


def project_out(nc, o_d, wo, s_d, ident):
    with ExitStack() as ctx:
        def sb(name, shape, dt):
            return ctx.enter_context(nc.sbuf_tensor(name, shape, dt))

        def sem(name):
            return ctx.enter_context(nc.semaphore(name))

        a = sb("a", [P, 2, D], F32)
        ah = sb("ah", [P, 2, D], F16)
        al = sb("al", [P, 2, D], F16)
        aT = sb("aT", [P, 2, 2, KT, P], F16)
        w_in = sb("wo_in", [P, 2, D], F32)
        w = sb("wo", [P, 2, KT, D], F16)
        s_out = sb("s_out", [P, 2, D], F32)
        out_ps = [ctx.enter_context(nc.psum_tensor(f"out_ps{i}", [P, FULL], F32)) for i in range(2)]
        tr_ps = [ctx.enter_context(nc.psum_tensor(f"tro_ps{i}", [P, KT, P], F16)) for i in range(2)]

        a_loaded = [sem(f"a_loaded{i}") for i in range(2)]
        w_loaded = [sem(f"wo_loaded{i}") for i in range(2)]
        whi_done = sem("wohi_done")
        wlo_done = sem("wolo_done")
        ah_done = sem("ah_done")
        al_done = sem("al_done")
        ah_turned = sem("ah_turned")
        al_turned = sem("al_turned")
        aTh_done = sem("aTh_done")
        aTl_done = sem("aTl_done")
        out_ready = sem("out_ready")
        out_done = sem("out_done")
        stored = [sem(f"s_stored{i}") for i in range(2)]
        w_v = wo.rearrange("(s p) n -> p s n", p=P)
        o_v = o_d.rearrange("b g p t c -> b t p g c")
        s_v = s_d.rearrange("(t p) n -> t p n", p=P)

        block = ctx.enter_context(nc.Block())

        @block.sync
        def _(sp):
            def load(b, m, u, wait):
                n = b * ST + 2 * m + u
                if wait:
                    sp.wait_ge(al_done, n - 1)
                sp.dma_start(a[:, u, :].rearrange("p (g c) -> p g c", g=KV), o_v[b, 2 * m + u]
                             ).then_inc(a_loaded[u], 16)

            load(0, 0, 0, False)
            load(0, 0, 1, False)
            for s in range(KT):
                if s >= 2:
                    sp.wait_ge(wlo_done, s - 1)
                sp.dma_start(w_in[:, s % 2, :], w_v[:, s, :]).then_inc(w_loaded[s % 2], 16)
            with sp.Fori(1, ST // 2) as m:
                load(0, m, 0, True)
                load(0, m, 1, True)
            with sp.Fori(0, ST // 2) as m:
                load(1, m, 0, True)
                load(1, m, 1, True)

        @block.gpsimd
        def _(pool):
            with pool.Fori(0, TT // 2) as m:
                for u in range(2):
                    pool.wait_ge(out_done, 2 * m + u + 1)
                    pool.dma_start(s_v[2 * m + u], s_out[:, u, :]).then_inc(stored[u], 16)
            for u in range(2):
                pool.wait_ge(stored[u], 16 * TT // 2)

        @block.scalar
        def _(act):
            def high(m, u):
                if not inside(m, u, TT):
                    return
                n = 2 * m + u
                act.wait_ge(a_loaded[u], 16 * (m + 1))
                if not isinstance(m, int) or m >= 1:
                    act.wait_ge(ah_turned, n - 1)
                    act.wait_ge(al_done, n - 1)
                act.activation(ah[:, u, :], a[:, u, :], ACT.Copy).then_inc(ah_done, 1)

            def turned(m, u):
                if not inside(m, u, TT):
                    return
                n = 2 * m + u
                act.wait_ge(ah_turned, n + 1)
                if not isinstance(m, int) or m >= 1:
                    act.wait_ge(out_ready, n - 1)
                act.activation(aT[:, u, 0, :, :], tr_ps[0][:, :, :], ACT.Copy).then_inc(aTh_done, 1)

            def post(m, u):
                if not inside(m, u, TT):
                    return
                n = 2 * m + u
                act.wait_ge(out_ready, n + 1)
                if not isinstance(m, int) or m >= 1:
                    act.wait_ge(stored[u], 16 * m)
                act.activation(s_out[:, u, :], out_ps[u][:, :], ACT.Copy, scale=1.0 / W_SCALE
                               ).then_inc(out_done, 1)

            def step(m, u):
                high(*at(m, u, 2))
                turned(*at(m, u, 1))
                post(m, u)

            high(0, 0)
            for s in range(KT):
                act.wait_ge(w_loaded[s % 2], 16 * (s // 2 + 1))
                act.activation(w[:, 0, s, :], w_in[:, s % 2, :], ACT.Copy, scale=W_SCALE).then_inc(whi_done, 1)
            step(-1, 1)
            step(0, 0)
            step(0, 1)
            with act.Fori(1, TT // 2 - 1) as m:
                step(m, 0)
                step(m, 1)
            step(TT // 2 - 1, 0)
            step(TT // 2 - 1, 1)

        @block.vector
        def _(dve):
            def low(m, u):
                if not inside(m, u, TT):
                    return
                n = 2 * m + u
                dve.wait_ge(ah_done, n + 1)
                if not isinstance(m, int) or m >= 1:
                    dve.wait_ge(al_turned, n - 1)
                dve.tensor_tensor(al[:, u, :], a[:, u, :], ah[:, u, :], ALU.subtract).then_inc(al_done, 1)

            def turned(m, u):
                if not inside(m, u, TT):
                    return
                n = 2 * m + u
                dve.wait_ge(al_turned, n + 1)
                if not isinstance(m, int) or m >= 1:
                    dve.wait_ge(out_ready, n - 1)
                dve.tensor_copy(aT[:, u, 1, :, :], tr_ps[1][:, :, :]).then_inc(aTl_done, 1)

            def step(m, u):
                low(*at(m, u, 2))
                turned(*at(m, u, 1))

            low(0, 0)
            for s in range(KT):
                dve.wait_ge(whi_done, s + 1)
                dve.scalar_tensor_tensor(w[:, 1, s, :], w_in[:, s % 2, :], W_SCALE, w[:, 0, s, :],
                                         ALU.mult, ALU.subtract).then_inc(wlo_done, 1)
            step(-1, 1)
            step(0, 0)
            step(0, 1)
            with dve.Fori(1, TT // 2 - 1) as m:
                step(m, 0)
                step(m, 1)
            step(TT // 2 - 1, 0)
            step(TT // 2 - 1, 1)

        @block.tensor
        def _(pe):
            def turn(m, u):
                if not inside(m, u, TT):
                    return
                n = 2 * m + u
                for part, (src, done, free, out) in enumerate([(ah, ah_done, aTh_done, ah_turned),
                                                               (al, al_done, aTl_done, al_turned)]):
                    pe.wait_ge(done, n + 1)
                    if not isinstance(m, int) or n >= 1:
                        pe.wait_ge(free, n)
                    for s in range(KT):
                        last = pe.transpose(tr_ps[part][:, s, :], src[:, u, s * P:(s + 1) * P], ident[:, :])
                    last.then_inc(out, 1)

            def products(m, u):
                n = 2 * m + u
                pe.wait_ge(aTh_done, n + 1)
                pe.wait_ge(aTl_done, n + 1)
                if not isinstance(m, int) or m >= 1:
                    pe.wait_ge(out_done, n - 1)
                for s in range(KT):
                    for k, (xp, wp) in enumerate([(0, 0), (0, 1), (1, 0)]):
                        for c in range(D // BANK):
                            cols = slice(c * BANK, (c + 1) * BANK)
                            last = pe.matmul(out_ps[u][:, cols], aT[:, u, xp, s, :], w[:, wp, s, cols],
                                             start=(s == 0 and k == 0), stop=(s == KT - 1 and k == 2))
                last.then_inc(out_ready, 1)

            turn(0, 0)
            pe.wait_ge(whi_done, KT)
            pe.wait_ge(wlo_done, KT)
            for u in range(2):
                turn(*at(0, u, 1))
                products(0, u)
            with pe.Fori(1, TT // 2 - 1) as m:
                for u in range(2):
                    turn(*at(m, u, 1))
                    products(m, u)
            turn(TT // 2 - 1, 1)
            products(TT // 2 - 1, 0)
            products(TT // 2 - 1, 1)


def quant_tables(nc, scales_gu, zeros_gu, scales_d, zeros_d, g_idx_gu, lanes, sc_d, z_d, scd, zd, sel_gu):
    PIECE = 1376
    WORDS = PIECE // NIB
    R_GU, R_D = 64 + G_GU, 64 + G_D
    with ExitStack() as ctx:
        def sb(name, shape, dt):
            return ctx.enter_context(nc.sbuf_tensor(name, shape, dt))

        def sem(name):
            return ctx.enter_context(nc.semaphore(name))

        sc = sb("tb_sc", [R_D, 2, PIECE], F32)
        rest = sb("tb_rest", [R_D, PIECE], F32)
        hi = sb("tb_hi", [R_D, 2, PIECE], BF16)
        mid = sb("tb_mid", [R_D, PIECE], BF16)
        lo = sb("tb_lo", [R_D, PIECE], BF16)
        zw = sb("tb_zw", [G_D, 2, WORDS], U32)
        zn = sb("tb_zn", [G_D, NIB, WORDS], U32)
        zt = sb("tb_zt", [R_D, 2, PIECE], BF16)
        idx = sb("tb_idx", [R_GU, D], I32)
        idf = sb("tb_idf", [R_GU, 2, D], F32)

        loaded = [sem(f"tb_loaded{i}") for i in range(2)]
        idx_loaded = sem("tb_idx_loaded")
        zeroed = sem("tb_zeroed")
        stepped = sem("tb_stepped")
        built = sem("tb_built")
        stored = [sem(f"tb_stored{i}") for i in range(2)]

        pieces = [(scales_gu[:, c:c + PIECE], zeros_gu[:, c // NIB:(c + PIECE) // NIB], G_GU, PIECE)
                  for c in range(0, 2 * INTER, PIECE)] + [(scales_d, zeros_d, G_D, D)]
        N = len(pieces)

        def store(sp, n):
            sp.wait_ge(built, n + 1)
            c = slice(n * PIECE, (n + 1) * PIECE)
            sp.dma_start(sc_d[:, c], hi[0:R_GU, n % 2, :]).then_inc(stored[n % 2], 16)
            sp.dma_start(z_d[:, c], zt[0:R_GU, n % 2, :]).then_inc(stored[n % 2], 16)

        block = ctx.enter_context(nc.Block())

        @block.sync
        def _(sp):
            sp.dma_start(idx[:, :], g_idx_gu.rearrange("(a i) -> a i", a=1).broadcast_to([R_GU, D])
                         ).then_inc(idx_loaded, 16)
            sp.wait_ge(zeroed, 1)
            for n, (s_ap, z_ap, g, cols) in enumerate(pieces):
                u = n % 2
                if n >= 2:
                    sp.wait_ge(built, n - 1)
                for r in range(3):
                    sp.dma_start(sc[32 * r:32 * r + g, u, 0:cols], s_ap).then_inc(loaded[u], 16)
                sp.dma_start(zw[0:g, u, 0:cols // NIB], z_ap).then_inc(loaded[u], 16)
                if n >= 1:
                    store(sp, n - 1)
            for u in range(2):
                sp.wait_ge(stored[u], 32 * ((N - 1) // 2))

        @block.vector
        def _(dve):
            count = [0]

            def link(ins):
                count[0] += 1
                ins.then_inc(stepped, 1)
                dve.wait_ge(stepped, count[0])

            dve.memset(zt[:, :, :], 0.0)
            dve.memset(zd[:, :], 0.0)
            dve.memset(sc[:, :, :], 0.0).then_inc(zeroed, 1)
            dve.wait_ge(idx_loaded, 16)
            link(dve.tensor_scalar(idf[:, 0, :], idx[:, :], 0.0, float(G_GU), ALU.is_lt, ALU.mult))
            link(dve.tensor_tensor(idf[:, 1, :], idf[:, 0, :], idx[:, :], ALU.add))
            link(dve.tensor_scalar(idf[:, 0, :], idf[:, 1, :], 0.0, float(G_GU - 1), ALU.max, ALU.min))
            link(dve.tensor_scalar(sel_gu[0:R_GU, :], idf[:, 0, :], lanes[0:R_GU, 0:1], None, ALU.is_equal))

            for n, (_, _, g, cols) in enumerate(pieces):
                u = n % 2
                dve.wait_ge(loaded[u], 64 * (n // 2 + 1))
                if n >= 2 and n < N - 1:
                    dve.wait_ge(stored[u], 32 * (n // 2))
                last = n == N - 1
                rows = 64 + g
                hi_t = scd[0:rows, 0:cols] if last else hi[0:rows, u, 0:cols]
                z_t = zd[0:g, 0:cols] if last else zt[0:g, u, 0:cols]
                x = sc[0:rows, u, 0:cols]
                r, md, l = rest[0:rows, 0:cols], mid[0:rows, 0:cols], lo[0:rows, 0:cols]
                link(dve.tensor_scalar(hi_t, x, W_SCALE, None, ALU.mult))
                link(dve.scalar_tensor_tensor(r, x, W_SCALE, hi_t, ALU.mult, ALU.subtract))
                link(dve.tensor_copy(md, r))
                link(dve.tensor_tensor(l, r, md, ALU.subtract))
                hold = scd if last else hi[:, u, :]
                dve.tensor_copy(hold[32:64, 0:cols], mid[32:64, 0:cols])
                link(dve.tensor_copy(hold[64:rows, 0:cols], lo[64:rows, 0:cols]))
                for k in range(NIB):
                    z_n = dve.tensor_scalar(zn[0:g, k, 0:cols // NIB], zw[0:g, u, 0:cols // NIB], 4 * k, 15,
                                            ALU.logical_shift_right, ALU.bitwise_and)
                link(z_n)
                link(dve.tensor_scalar(z_t.rearrange("g (c k) -> g k c", k=NIB), zn[0:g, :, 0:cols // NIB],
                                       1.0, None, ALU.add))
                dve.tensor_copy(rest[0:1, 0:1], rest[0:1, 0:1]).then_inc(built, 1)


def feed_forward(nc, x, qw_gu, qw_d, g_idx_d, lanes, sc_d, z_d, scd, zd, sel_gu, xT, s_d, out):
    R_GU, R_D = 64 + G_GU, 64 + G_D
    ROUNDS = NIB // 2
    PER = ROUNDS + 2
    DN = 2 * TT
    with ExitStack() as ctx:
        def sb(name, shape, dt):
            return ctx.enter_context(nc.sbuf_tensor(name, shape, dt))

        def sem(name):
            return ctx.enter_context(nc.semaphore(name))

        acc = sb("acc", [P, TT, D], F32)
        hT = sb("hT", [P, 2, CHUNK, T], F16)
        wg = sb("wg", [P, 2, 2, KT, 2 * P], F16)
        wd = sb("wd", [P, 2, CHUNK, D], F16)
        qwg = sb("qwg", [P, 2, 2, P], U32)
        qwd = sb("qwd", [P, 2, BANK], U32)
        nib = sb("nib", [P, BANK], U32)
        dif = sb("dif", [P, BANK], F32)
        wf = sb("wf", [P, 2, BANK], F32)
        h = sb("h", [P, 2, BANK], F32)
        zt = sb("zt", [R_GU, 2, 2, P], BF16)
        st = sb("st", [R_GU, 2, 2, P], BF16)
        idx = sb("idx", [R_D, 2, P], I32)
        idf = sb("idf", [R_D, 2, P], F32)
        sel = sb("sel", [R_D, 2, P], BF16)
        x_in = sb("x_in", [P, 2, BANK], F32)
        s_in = sb("s_in", [P, 2, BANK], F32)
        gate_ps = [ctx.enter_context(nc.psum_tensor(f"gate_ps{i}", [P, BANK], F32)) for i in range(2)]
        up_ps = [ctx.enter_context(nc.psum_tensor(f"up_ps{i}", [P, BANK], F32)) for i in range(2)]
        dn_ps = [ctx.enter_context(nc.psum_tensor(f"dn_ps{i}", [P, BANK], F32)) for i in range(2)]
        z_ps = ctx.enter_context(nc.psum_tensor("z_ps", [P, BANK], F32))
        s_ps = ctx.enter_context(nc.psum_tensor("s_ps", [P, BANK], F32))

        gu_loaded = [sem(f"gu_loaded{i}") for i in range(2)]
        dn_loaded = [sem(f"dn_loaded{i}") for i in range(2)]
        idx_loaded = [sem(f"idx_loaded{i}") for i in range(2)]
        acc_zeroed = sem("acc_zeroed")
        sel_step = sem("sel_step")
        sel_done = sem("sel_done")
        zs_ready = sem("zs_ready")
        nib_done = sem("nib_done")
        dif_done = sem("dif_done")
        wf_done = sem("wf_done")
        whi_done = sem("fwhi_done")
        wlo_done = sem("fwlo_done")
        gu_ready = sem("gu_ready")
        silu_done = sem("silu_done")
        h_done = sem("h_done")
        hhi_done = sem("hhi_done")
        hlo_done = sem("hlo_done")
        dn_ready = sem("dn_ready")
        dn_taken = sem("dn_taken")
        g_done = sem("g_done")
        xs_loaded = [sem(f"xs_loaded{i}") for i in range(2)]
        prod_done = sem("prod_done")
        sum_done = sem("sum_done")
        out_stored = sem("out_stored")

        qwg_v = qw_gu.rearrange("p (h f) -> p h f", h=2)
        z_v = z_d.rearrange("p (h f) -> p h f", h=2)
        sc_v = sc_d.rearrange("p (h f) -> p h f", h=2)
        x_v = x.rearrange("b (t p) d -> (b t) p d", p=P)
        s_v = s_d.rearrange("(t p) d -> t p d", p=P)
        out_v = out.rearrange("b (t p) d -> (b t) p d", p=P)

        def width(j):
            return FLAST if isinstance(j, int) and j == FTILES - 1 else P

        def first_round(j, kind):
            if kind == "g":
                return 0 if isinstance(j, int) and j == 0 else ROUNDS + PER * (j - 1)
            return ROUNDS + PER * j + (0 if isinstance(j, int) and j == FTILES - 1 else ROUNDS)

        def places(j):
            nxt = [("g", k) for k in range(ROUNDS)] if not (isinstance(j, int) and j == FTILES - 1) else []
            return (nxt + [("d", 0), ("d", 1)] + [None] * 8)[:8]

        def store(sp, k):
            t, n = k // 2, k % 2
            cols = slice(n * BANK, (n + 1) * BANK)
            sp.wait_ge(sum_done, k + 1)
            sp.dma_start(out_v[t][:, cols], acc[:, t, cols]).then_inc(out_stored, 16)

        block = ctx.enter_context(nc.Block())

        @block.sync
        def _(sp):
            def load_gu(j, u):
                w = width(j)
                f = bass.ds(j * P, w)
                sp.dma_start(qwg[:, u, :, 0:w], qwg_v[:, :, f]).then_inc(gu_loaded[u], 16)
                sp.dma_start(zt[:, u, :, 0:w], z_v[:, :, f]).then_inc(gu_loaded[u], 16)
                sp.dma_start(st[:, u, :, 0:w], sc_v[:, :, f]).then_inc(gu_loaded[u], 16)

            def load_dn(j, u):
                w = width(j)
                rows = qw_d[bass.ds(j * (P // NIB), w // NIB), :]
                for n in range(2):
                    sp.dma_start(qwd[0:w, n, :],
                                 rows[:, n * BANK:(n + 1) * BANK].unsqueeze(1).broadcast_to([w // NIB, NIB, BANK])
                                 ).then_inc(dn_loaded[n], 16)
                sp.dma_start(idx[:, u, 0:w],
                             g_idx_d.rearrange("(a i) -> a i", a=1)[:, bass.ds(j * P, w)].broadcast_to([R_D, w])
                             ).then_inc(idx_loaded[u], 16)

            def step(j, u):
                if not isinstance(j, int) or j + 2 < FTILES:
                    sp.wait_ge(wf_done, first_round(j, "g") + ROUNDS)
                    load_gu(j + 2, u)
                if not isinstance(j, int) or j + 1 < FTILES:
                    sp.wait_ge(wf_done, first_round(j, "d") + 2)
                    load_dn(j + 1, 1 - u)

            load_gu(0, 0)
            load_gu(1, 1)
            load_dn(0, 0)
            step(0, 0)
            step(1, 1)
            with sp.Fori(1, CHUNKS - 2) as c:
                for u in range(2):
                    step(CHUNK * c + u, u)
            for j in range(CHUNK * (CHUNKS - 2), FTILES):
                step(j, j % 2)
            for k in range(DN):
                t, n, u = k // 2, k % 2, k % 2
                cols = slice(n * BANK, (n + 1) * BANK)
                if k >= 2:
                    sp.wait_ge(sum_done, k - 1)
                sp.dma_start(x_in[:, u, :], x_v[t][:, cols]).then_inc(xs_loaded[u], 16)
                sp.dma_start(s_in[:, u, :], s_v[t][:, cols]).then_inc(xs_loaded[u], 16)
                if k >= 2:
                    store(sp, k - 2)
            store(sp, DN - 2)
            store(sp, DN - 1)
            sp.wait_ge(out_stored, 16 * DN)

        @block.tensor
        def _(pe):
            def rebuild(j, u, place):
                if place is None:
                    return
                kind, k = place
                if kind == "g":
                    n, w, s_u = first_round(j + 1, "g") + k, width(j + 1), 1 - u
                    if k == 0:
                        slot_load = gu_loaded[s_u]
                        pe.wait_ge(slot_load, 48 * ((j + 1 - s_u) // 2 + 1))
                    if not isinstance(n, int) or n >= 1:
                        pe.wait_ge(wf_done, n)
                    for b in range(2):
                        rows = sel_gu[0:R_GU, :].rearrange("g (p s) -> g s p", s=KT)[:, 2 * k + b, :]
                        for src, dst in ((zt, z_ps), (st, s_ps)):
                            last = pe.matmul(dst[:, b * 2 * P:b * 2 * P + 2 * w], rows, src[:, s_u, :, 0:w],
                                             start=True, stop=True)
                else:
                    n, w = first_round(j, "d") + k, width(j)
                    pe.wait_ge(wf_done, n)
                    if k == 0:
                        pe.wait_ge(sel_done, j + 1)
                    for src, dst in ((zd, z_ps), (scd, s_ps)):
                        last = pe.matmul(dst[0:w, :], sel[:, u, 0:w], src[0:R_D, k * BANK:(k + 1) * BANK],
                                         start=True, stop=True)
                last.then_inc(zs_ready, 1)

            def gate_up(j, u):
                w = width(j)
                for t in range(TC):
                    e = TC * j + t
                    if t == 0:
                        pe.wait_ge(whi_done, first_round(j, "g") + ROUNDS)
                        pe.wait_ge(wlo_done, first_round(j, "g") + ROUNDS)
                    if not isinstance(j, int) or e >= 2:
                        pe.wait_ge(h_done, e - 1)
                    for s in range(KT):
                        if s % (KT // 2) == 0:
                            rebuild(j, u, places(j)[2 * t + s // (KT // 2)])
                        for k, (wp, xp) in enumerate([(0, 0), (0, 1), (1, 0)]):
                            for g, ps in ((0, gate_ps), (1, up_ps)):
                                last = pe.matmul(ps[t % 2][0:w, :], wg[:, u, wp, s, g * w:(g + 1) * w],
                                                 xT[:, xp, s, t * BANK:(t + 1) * BANK],
                                                 start=(s == 0 and k == 0), stop=(s == KT - 1 and k == 2))
                    last.then_inc(gu_ready, 1)

            def down(c):
                j = CHUNK * c + CHUNK - 1
                pe.wait_ge(whi_done, first_round(j, "d") + 2)
                pe.wait_ge(wlo_done, first_round(j, "d") + 2)
                for t in range(TT):
                    if t % (TT // TC) == 0:
                        pe.wait_ge(hlo_done, TC * j + t // (TT // TC) + 1)
                        pe.wait_ge(hhi_done, TC * j + t // (TT // TC) + 1)
                    for n in range(2):
                        i = DN * c + 2 * t + n
                        if not isinstance(c, int) or i >= 2:
                            pe.wait_ge(dn_taken, i - 1)
                        for e in range(CHUNK):
                            w = width(CHUNK * c + e)
                            for k, (hp, wp) in enumerate([(0, 0), (0, 1), (1, 0)]):
                                last = pe.matmul(dn_ps[n][:, :], hT[0:w, hp, e, t * P:(t + 1) * P],
                                                 wd[0:w, wp, e, n * BANK:(n + 1) * BANK],
                                                 start=(e == 0 and k == 0), stop=(e == CHUNK - 1 and k == 2))
                        last.then_inc(dn_ready, 1)

            for k in range(ROUNDS):
                rebuild(-1, 1, ("g", k))
            for u in range(2):
                gate_up(u, u)
            down(0)
            with pe.Fori(1, CHUNKS - 1) as c:
                for u in range(2):
                    gate_up(CHUNK * c + u, u)
                down(c)
            for u in range(2):
                gate_up(CHUNK * (CHUNKS - 1) + u, u)
            down(CHUNKS - 1)

        @block.vector
        def _(dve):
            def select(j, u):
                w = width(j)
                steps = [lambda: dve.tensor_scalar(idf[:, 0, 0:w], idx[:, u, 0:w], 0.0, float(G_D),
                                                   ALU.is_lt, ALU.mult),
                         lambda: dve.tensor_tensor(idf[:, 1, 0:w], idf[:, 0, 0:w], idx[:, u, 0:w], ALU.add),
                         lambda: dve.tensor_scalar(idf[:, 0, 0:w], idf[:, 1, 0:w], 0.0, float(G_D - 1),
                                                   ALU.max, ALU.min)]
                dve.wait_ge(idx_loaded[u], 16 * ((j - u) // 2 + 1))
                for k, op in enumerate(steps):
                    op().then_inc(sel_step, 1)
                    dve.wait_ge(sel_step, 3 * j + k + 1)
                dve.tensor_scalar(sel[:, u, 0:w], idf[:, 0, 0:w], lanes[0:R_D, 0:1], None, ALU.is_equal
                                  ).then_inc(sel_done, 1)

            def rebuild(j, u, place):
                if place is None:
                    return
                kind, k = place
                if kind == "g":
                    n, w, s_u = first_round(j + 1, "g") + k, width(j + 1), 1 - u
                    p, view = P, [slice(b * 2 * P, b * 2 * P + 2 * w) for b in range(2)]
                    if k == 0:
                        dve.wait_ge(gu_loaded[s_u], 48 * ((j + 1 - s_u) // 2 + 1))
                    for b in range(2):
                        last = dve.tensor_scalar(nib[:, view[b]].rearrange("p (h f) -> p h f", h=2),
                                                 qwg[:, s_u, :, 0:w], 4 * (2 * k + b), 15,
                                                 ALU.logical_shift_right, ALU.bitwise_and)
                    if w == P:
                        view = [slice(0, BANK)]
                else:
                    n, p, view = first_round(j, "d") + k, width(j), [slice(0, BANK)]
                    dve.wait_ge(dn_loaded[k], 16 * (j + 1))
                    last = dve.tensor_scalar(nib[0:p, :], qwd[0:p, k, :], lanes[0:p, 1:2].bitcast(U32), 15,
                                             ALU.logical_shift_right, ALU.bitwise_and)
                last.then_inc(nib_done, 1)
                dve.wait_ge(zs_ready, n + 1)
                dve.wait_ge(nib_done, n + 1)
                for v in view:
                    last = dve.tensor_tensor(dif[0:p, v], nib[0:p, v], z_ps[0:p, v], ALU.subtract)
                last.then_inc(dif_done, 1)
                dve.wait_ge(dif_done, n + 1)
                if not isinstance(n, int) or n >= 2:
                    dve.wait_ge(wlo_done, n - 1)
                for v in view:
                    last = dve.tensor_tensor(wf[0:p, k % 2, v], dif[0:p, v], s_ps[0:p, v], ALU.mult)
                last.then_inc(wf_done, 1)

            def gated(j, t):
                w, e = width(j), TC * j + t
                dve.wait_ge(silu_done, e + 1)
                dve.scalar_tensor_tensor(h[0:w, t % 2, :], up_ps[t % 2][0:w, :], H_SCALE / W_SCALE,
                                         h[0:w, t % 2, :], ALU.mult, ALU.mult).then_inc(h_done, 1)

            def tile(j, u):
                select(j, u)
                for t in range(TC):
                    for half in range(2):
                        rebuild(j, u, places(j)[2 * t + half])
                    gated(j, t)

            def add(c, t, n):
                i = DN * c + 2 * t + n
                cols = slice(n * BANK, (n + 1) * BANK)
                dve.wait_ge(dn_ready, i + 1)
                dve.tensor_tensor(acc[:, t, cols], acc[:, t, cols], dn_ps[n][:, :], ALU.add).then_inc(dn_taken, 1)

            def weigh(k):
                t, n, u = k // 2, k % 2, k % 2
                cols = slice(n * BANK, (n + 1) * BANK)
                dve.wait_ge(g_done, k + 1)
                dve.wait_ge(xs_loaded[u], 32 * (k // 2 + 1))
                dve.tensor_tensor(acc[:, t, cols], acc[:, t, cols], s_in[:, u, :], ALU.mult).then_inc(prod_done, 1)

            for k in range(ROUNDS):
                rebuild(-1, 1, ("g", k))
            for u in range(2):
                tile(u, u)
            dve.wait_ge(acc_zeroed, 1)
            for k in range(DN):
                add(0, k // 2, k % 2)
            with dve.Fori(1, CHUNKS - 1) as c:
                for u in range(2):
                    tile(CHUNK * c + u, u)
                dve.wait_ge(dn_taken, DN * c)
                for k in range(DN):
                    add(c, k // 2, k % 2)
            for u in range(2):
                tile(CHUNK * (CHUNKS - 1) + u, u)
            dve.wait_ge(dn_taken, DN * (CHUNKS - 1))
            for k in range(DN + 2):
                if k < DN:
                    add(CHUNKS - 1, k // 2, k % 2)
                if k >= 2:
                    weigh(k - 2)

        @block.scalar
        def _(act):
            def high(j, u, place):
                if place is None:
                    return
                kind, k = place
                if kind == "g":
                    n, w = first_round(j + 1, "g") + k, width(j + 1)
                    act.wait_ge(wf_done, n + 1)
                    act.activation(wg[:, 1 - u, 0, 2 * k:2 * k + 2, 0:2 * w],
                                   wf[:, k % 2, :].rearrange("p (s f) -> p s f", s=2)[:, :, 0:2 * w],
                                   ACT.Copy).then_inc(whi_done, 1)
                else:
                    n, w = first_round(j, "d") + k, width(j)
                    act.wait_ge(wf_done, n + 1)
                    act.activation(wd[0:w, 0, u, k * BANK:(k + 1) * BANK], wf[0:w, k % 2, :],
                                   ACT.Copy).then_inc(whi_done, 1)

            def gated(j, u, t):
                w, e = width(j), TC * j + t
                act.wait_ge(gu_ready, e + 1)
                if not isinstance(e, int) or e >= 2:
                    act.wait_ge(hlo_done, e - 1)
                act.activation(h[0:w, t % 2, :], gate_ps[t % 2][0:w, :], ACT.Silu, scale=1.0 / W_SCALE
                               ).then_inc(silu_done, 1)
                act.wait_ge(h_done, e + 1)
                act.activation(hT[0:w, 0, u, t * BANK:(t + 1) * BANK], h[0:w, t % 2, :], ACT.Copy
                               ).then_inc(hhi_done, 1)

            def tile(j, u):
                for t in range(TC):
                    for half in range(2):
                        high(j, u, places(j)[2 * t + half])
                    gated(j, u, t)

            for k in range(ROUNDS):
                high(-1, 1, ("g", k))
            for u in range(2):
                tile(u, u)
            with act.Fori(1, CHUNKS - 1) as c:
                for u in range(2):
                    tile(CHUNK * c + u, u)
            for u in range(2):
                tile(CHUNK * (CHUNKS - 1) + u, u)
            for k in range(DN):
                t, n = k // 2, k % 2
                cols = slice(n * BANK, (n + 1) * BANK)
                act.wait_ge(dn_taken, DN * (CHUNKS - 1) + k + 1)
                act.activation(acc[:, t, cols], acc[:, t, cols], ACT.Silu, scale=1.0 / (W_SCALE * H_SCALE)
                               ).then_inc(g_done, 1)

        @block.gpsimd
        def _(pool):
            def low(j, u, place):
                if place is None:
                    return
                kind, k = place
                if kind == "g":
                    n, w = first_round(j + 1, "g") + k, width(j + 1)
                    s = slice(2 * k, 2 * k + 2)
                    pool.wait_ge(whi_done, n + 1)
                    pool.tensor_tensor(wg[:, 1 - u, 1, s, 0:2 * w],
                                       wf[:, k % 2, :].rearrange("p (s f) -> p s f", s=2)[:, :, 0:2 * w],
                                       wg[:, 1 - u, 0, s, 0:2 * w], ALU.subtract).then_inc(wlo_done, 1)
                else:
                    n, w = first_round(j, "d") + k, width(j)
                    cols = slice(k * BANK, (k + 1) * BANK)
                    pool.wait_ge(whi_done, n + 1)
                    pool.tensor_tensor(wd[0:w, 1, u, cols], wf[0:w, k % 2, :], wd[0:w, 0, u, cols],
                                       ALU.subtract).then_inc(wlo_done, 1)

            def gated(j, u, t):
                w, e = width(j), TC * j + t
                cols = slice(t * BANK, (t + 1) * BANK)
                pool.wait_ge(hhi_done, e + 1)
                pool.tensor_tensor(hT[0:w, 1, u, cols], h[0:w, t % 2, :], hT[0:w, 0, u, cols],
                                   ALU.subtract).then_inc(hlo_done, 1)

            def tile(j, u):
                for t in range(TC):
                    for half in range(2):
                        low(j, u, places(j)[2 * t + half])
                    gated(j, u, t)

            pool.memset(acc[:, :, :], 0.0).then_inc(acc_zeroed, 1)
            for k in range(ROUNDS):
                low(-1, 1, ("g", k))
            for u in range(2):
                tile(u, u)
            with pool.Fori(1, CHUNKS - 1) as c:
                for u in range(2):
                    tile(CHUNK * c + u, u)
            for u in range(2):
                tile(CHUNK * (CHUNKS - 1) + u, u)
            for k in range(DN):
                t, n, u = k // 2, k % 2, k % 2
                cols = slice(n * BANK, (n + 1) * BANK)
                pool.wait_ge(prod_done, k + 1)
                pool.tensor_tensor(acc[:, t, cols], acc[:, t, cols], x_in[:, u, :], ALU.add).then_inc(sum_done, 1)


def build(nc, x, wq, wk, wv, wo, qw_gu, qz_gu, sc_gu, gi_gu, qw_d, qz_d, sc_dn, gi_d, rope, lanes_in, out):
    qk_d = nc.dram_tensor("qk_scratch", (B, KV, P, ST, (REP + 1) * STACK), F16, kind="Internal").ap()
    v_d = nc.dram_tensor("v_scratch", (B, KV, P, ST, VW), F16, kind="Internal").ap()
    o_d = nc.dram_tensor("o_scratch", (B, KV, P, ST, REP * HD), F32, kind="Internal").ap()
    s_d = nc.dram_tensor("s_scratch", (T, D), F32, kind="Internal").ap()
    sc_d = nc.dram_tensor("scale_scratch", (64 + G_GU, 2 * INTER), BF16, kind="Internal").ap()
    z_d = nc.dram_tensor("zero_scratch", (64 + G_GU, 2 * INTER), BF16, kind="Internal").ap()
    with ExitStack() as ctx:
        def sb(name, shape, dt):
            return ctx.enter_context(nc.sbuf_tensor(name, shape, dt))

        xT = sb("xT", [P, 2, KT, T], F16)
        ident = sb("ident", [P, P], F16)
        with ExitStack() as attn:
            identb = attn.enter_context(nc.sbuf_tensor("identb", [P, P], BF16))
            maskb = attn.enter_context(nc.sbuf_tensor("maskb", [P, P], BF16))
            project_qkv(nc, x, wq, wk, wv, rope, qk_d, v_d, xT, ident, identb, maskb)
            attend(nc, qk_d, v_d, o_d, ident, identb, maskb)
        project_out(nc, o_d, wo, s_d, ident)
        lanes = sb("lanes", [P, 2], I32)
        scd = sb("scd", [64 + G_D, D], BF16)
        zd = sb("zd", [64 + G_D, D], BF16)
        sel_gu = sb("sel_gu", [64 + G_GU, D], BF16)
        with nc.semaphore("lanes_loaded") as lanes_loaded, nc.Block() as block:
            @block.sync
            def _(sp):
                sp.dma_start(lanes[:, :], lanes_in).then_inc(lanes_loaded, 16)
                sp.wait_ge(lanes_loaded, 16)
        quant_tables(nc, sc_gu, qz_gu, sc_dn, qz_d, gi_gu, lanes, sc_d, z_d, scd, zd, sel_gu)
        feed_forward(nc, x, qw_gu, qw_d, gi_d, lanes, sc_d, z_d, scd, zd, sel_gu, xT, s_d, out)


def rope_table():
    f32 = np.float32
    freqs = (f32(1.0) / np.power(f32(THETA), np.arange(0, HD, 2, dtype=f32) / f32(HD))).astype(f32)
    ang = np.outer(np.arange(S, dtype=f32), freqs).astype(f32)
    both = np.stack([np.cos(ang), np.sin(ang)], axis=1).astype(f32) / f32(W_SCALE)
    both = np.tile(both.reshape(ST, P, 2, HALF), (B, 1, 1, 1))
    return np.ascontiguousarray(both.transpose(1, 0, 2, 3).reshape(P, -1))


def lane_table():
    p = np.arange(P)
    return np.stack([p % 32, 4 * (p % NIB)], axis=1).astype(np.int32)


def kernel(L0_attn_x, L0_attn_wq, L0_attn_wk, L0_attn_wv, L0_attn_wo, L0_ffn_qweight_gu, L0_ffn_qzeros_gu,
           L0_ffn_scales_gu, L0_ffn_g_idx_gu, L0_ffn_qweight_down, L0_ffn_qzeros_down, L0_ffn_scales_down,
           L0_ffn_g_idx_down):
    import concourse.bacc as bacc
    from concourse.bass_utils import run_bass_kernel_spmd

    given = {"x": L0_attn_x, "wq": L0_attn_wq, "wk": L0_attn_wk, "wv": L0_attn_wv, "wo": L0_attn_wo,
             "qw_gu": L0_ffn_qweight_gu, "qz_gu": L0_ffn_qzeros_gu, "sc_gu": L0_ffn_scales_gu,
             "gi_gu": L0_ffn_g_idx_gu, "qw_d": L0_ffn_qweight_down, "qz_d": L0_ffn_qzeros_down,
             "sc_dn": L0_ffn_scales_down, "gi_d": L0_ffn_g_idx_down, "rope": rope_table(), "lanes": lane_table()}
    nc = bacc.Bacc("TRN2", target_bir_lowering=False, num_devices=1)
    arrays, args = {}, []
    for name, a in given.items():
        a = np.ascontiguousarray(a)
        arrays[f"in_{name}"] = a
        args.append(nc.dram_tensor(f"in_{name}", a.shape, mybir.dt.from_np(a.dtype), kind="ExternalInput").ap())
    out = nc.dram_tensor("out", (B, S, D), F32, kind="ExternalOutput").ap()
    build(nc, *args, out)
    r = run_bass_kernel_spmd(nc, [arrays], core_ids=[0])
    return r.results[0]["out"]
```

```python
from contextlib import ExitStack

import numpy as np

import concourse.bass as bass
from concourse import mybir

ALU = mybir.AluOpType
ACT = mybir.ActivationFunctionType
AX_X = mybir.AxisListType.X
F32 = mybir.dt.float32
F16 = mybir.dt.float16
BF16 = mybir.dt.bfloat16
I32 = mybir.dt.int32
U32 = mybir.dt.uint32

P = 128
B, S, D = 2, 1024, 1024
T = B * S
TT = T // P
ST = S // P
KT = D // P
HEADS, KV, HD = 32, 8, 32
REP = HEADS // KV
GROUPS = B * KV
QKV = (HEADS + 2 * KV) * HD
QK = HEADS + KV
HALF = HD // 2
STACK = 3 * HD
VH = HD + 1
VW = VH + HD
EPS = 1e-5
THETA = 10000.0
BANK = 512
FULL = 1024

INTER = 2752
G_GU, G_D = 8, 21
NIB = 8
FTILES = (INTER + P - 1) // P
FLAST = INTER - (FTILES - 1) * P
CHUNK = 2
CHUNKS = FTILES // CHUNK
TC = T // BANK
STAGE = 4

W_SCALE = 64.0
H_SCALE = 1.0 / 16.0
MASKED = -1e30


def at(m, u, off, unroll=2):
    k = u + off
    return m + k // unroll, k % unroll


def inside(m, u, n, unroll=2):
    return not isinstance(m, int) or 0 <= unroll * m + u < n


def wait_alone(eng, sem, count, seen):
    eng.wait_ge(sem, count)
    eng.sem_inc(seen, 1)


def make_masks(pool, ident, identb, maskb, zeros_done, masks_done):
    pool.memset(ident[:, :], 1.0)
    pool.memset(identb[:, :], 1.0)
    pool.memset(maskb[:, :], 0.0).then_inc(zeros_done, 1)
    pool.wait_ge(zeros_done, 1)
    pool.affine_select(out=ident[:, :], in_=ident[:, :], pattern=[[-1, P]], compare_op=ALU.is_equal,
                       fill=0.0, base=0, channel_multiplier=1)
    pool.affine_select(out=identb[:, :], in_=identb[:, :], pattern=[[-1, P]], compare_op=ALU.is_equal,
                       fill=0.0, base=0, channel_multiplier=1)
    pool.affine_select(out=maskb[:, :], in_=maskb[:, :], pattern=[[-1, P]], compare_op=ALU.is_ge,
                       fill=MASKED, base=0, channel_multiplier=1).then_inc(masks_done, 1)


def project_qkv(nc, x, wq, wk, wv, rope, qk_d, v_d, xT, ident, identb, maskb):
    with ExitStack() as ctx:
        def sb(name, shape, dt):
            return ctx.enter_context(nc.sbuf_tensor(name, shape, dt))

        def sem(name):
            return ctx.enter_context(nc.semaphore(name))

        xin = sb("xin", [P, 2, D], F32)
        xn = sb("xn", [P, 2, D], F32)
        xh = sb("xh", [P, 2, D], F16)
        xl = sb("xl", [P, 2, D], F16)
        bn = sb("bn", [P, 2, 6], F32)
        mv = sb("mv", [P, 2, 2], F32)
        std = sb("std", [P, 2, 1], F32)
        rstd = sb("rstd", [P, 2, 1], F32)
        eps = sb("eps", [P, 1], F32)
        xTc = sb("xTc", [P, 2, 2, KT, P], F16)
        w_in = sb("w_in", [P, STAGE, QKV], F32)
        w = sb("w", [P, 2, KT, QKV], F16)
        cs = sb("cs", [P, TT, 2, HALF], F32)
        rot_t = sb("rot_t", [P, 4, QK, HALF], F32)
        rot = sb("rot", [P, QK, 2, HALF], F32)
        stack = sb("stack", [P, 2, QK, STACK], F16)
        v = sb("v", [P, 2, KV, VW], F16)
        qkv_ps = [ctx.enter_context(nc.psum_tensor(f"qkv_ps{i}", [P, QKV], F32)) for i in range(2)]
        tr_ps = [ctx.enter_context(nc.psum_tensor(f"tr_ps{i}", [P, KT, P], F16)) for i in range(2)]

        x_loaded = [sem(f"x_loaded{i}") for i in range(2)]
        w_loaded = [sem(f"w_loaded{i}") for i in range(STAGE)]
        cs_loaded = sem("cs_loaded")
        whi_done = sem("whi_done")
        wlo_done = sem("wlo_done")
        zeros_done = sem("zeros_done")
        masks_done = sem("masks_done")
        ones_set = sem("ones_set")
        eps_set = sem("eps_set")
        bn_done = sem("bn_done")
        bn_seen = sem("bn_seen")
        hi_seen = sem("hi_seen")
        mv_done = sem("mv_done")
        std_done = sem("std_done")
        rstd_done = sem("rstd_done")
        xn_done = sem("xn_done")
        xh_done = sem("xh_done")
        xl_done = sem("xl_done")
        xh_turned = sem("xh_turned")
        xl_turned = sem("xl_turned")
        xTh_done = sem("xTh_done")
        xTl_done = sem("xTl_done")
        xT_kept = sem("xT_kept")
        qkv_done = sem("qkv_done")
        mult_done = sem("mult_done")
        rot_done = sem("rot_done")
        v_done = sem("v_done")
        vlo_done = sem("vlo_done")
        hi_done = sem("hi_done")
        dup_done = sem("dup_done")
        lo_done = sem("lo_done")
        stored = [sem(f"stored{i}") for i in range(2)]
        qk_v = qk_d.rearrange("b g p t c -> b t p g c")
        v_v = v_d.rearrange("b g p t c -> b t p g c")

        w_parts = [(wq.rearrange("(p s) n -> p s n", s=KT), 0, HEADS * HD),
                   (wk.rearrange("(p s) n -> p s n", s=KT), HEADS * HD, KV * HD),
                   (wv.rearrange("(p s) n -> p s n", s=KT), QK * HD, KV * HD)]
        x_v = x.rearrange("b (t p) d -> (b t) p d", p=P)

        block = ctx.enter_context(nc.Block())

        @block.sync
        def _(sp):
            def load_x(m, u):
                if not inside(m, u, TT):
                    return
                if not isinstance(m, int) or m >= 1:
                    sp.wait_ge(xn_done, 2 * m + u - 1)
                sp.dma_start(xin[:, u, :], x_v[2 * m + u]).then_inc(x_loaded[u], 16)

            load_x(0, 0)
            load_x(0, 1)
            for s in range(KT):
                if s >= STAGE:
                    sp.wait_ge(wlo_done, s - STAGE + 1)
                for w_dram, c0, n in w_parts:
                    sp.dma_start(w_in[:, s % STAGE, c0:c0 + n], w_dram[:, s, :]).then_inc(w_loaded[s % STAGE], 16)
                if s >= KT - 2:
                    load_x(1, s - KT + 2)
            sp.dma_start(cs[:, :, :, :], rope.rearrange("p (t c f) -> p t c f", t=TT, c=2)).then_inc(cs_loaded, 16)

            def step(b, m, u, ahead):
                n = b * ST + 2 * m + u
                sp.wait_ge(lo_done, n + 1)
                sp.wait_ge(dup_done, n + 1)
                sp.wait_ge(vlo_done, n + 1)
                sp.dma_start(qk_v[b, 2 * m + u, :, :, 0:REP * STACK],
                             stack[:, u, 0:HEADS, :].rearrange("p (g r) c -> p g (r c)", r=REP)
                             ).then_inc(stored[u], 16)
                sp.dma_start(qk_v[b, 2 * m + u, :, :, REP * STACK:],
                             stack[:, u, HEADS:QK, :]).then_inc(stored[u], 16)
                sp.dma_start(v_v[b, 2 * m + u], v[:, u, :, :]).then_inc(stored[u], 16)

            half = ST // 2
            with sp.Fori(0, half) as m:
                for u in range(2):
                    load_x(m + 2, u)
                    step(0, m, u, True)
            with sp.Fori(0, half - 2) as m:
                for u in range(2):
                    load_x(m + 2 + half, u)
                    step(1, m, u, True)
            for m in range(half - 2, half):
                for u in range(2):
                    step(1, m, u, False)
            for u in range(2):
                sp.wait_ge(stored[u], 16 * 3 * TT // 2)

        @block.gpsimd
        def _(pool):
            pool.memset(v[:, :, :, HD:VH], 1.0).then_inc(ones_set, 1)
            make_masks(pool, ident, identb, maskb, zeros_done, masks_done)

            def low(m, u):
                if not inside(m, u, TT):
                    return
                n = 2 * m + u
                pool.wait_ge(xh_done, n + 1)
                if not isinstance(m, int) or m >= 1:
                    pool.wait_ge(xl_turned, n - 1)
                pool.tensor_tensor(xl[:, u, :], xn[:, u, :], xh[:, u, :], ALU.subtract).then_inc(xl_done, 1)

            def keep(m, u):
                if not inside(m, u, TT):
                    return
                n = 2 * m + u
                pool.wait_ge(xTh_done, n + 1)
                pool.wait_ge(xTl_done, n + 1)
                for part in range(2):
                    last = pool.tensor_copy(xT[:, part, :, bass.ds(n * P, P)], xTc[:, u, part, :, :])
                last.then_inc(xT_kept, 1)

            def dup(m, u):
                if not inside(m, u, TT):
                    return
                n = 2 * m + u
                wait_alone(pool, hi_done, n + 1, hi_seen)
                pool.tensor_copy(stack[:, u, 0:HEADS, HD:2 * HD], stack[:, u, 0:HEADS, 0:HD])
                pool.tensor_copy(stack[:, u, HEADS:QK, 2 * HD:STACK],
                                 stack[:, u, HEADS:QK, 0:HD]).then_inc(dup_done, 1)

            def step(m, u):
                low(*at(m, u, 2))
                keep(*at(m, u, 1))
                dup(m, u)

            for m in range(2):
                low(m, 0)
                low(m, 1)
                if m == 0:
                    keep(0, 0)
                    keep(0, 1)
            dup(0, 0)
            keep(1, 0)
            dup(0, 1)
            with pool.Fori(1, TT // 2 - 1) as m:
                step(m, 0)
                step(m, 1)
            step(TT // 2 - 1, 0)
            step(TT // 2 - 1, 1)

        @block.scalar
        def _(act):
            def deviation(m, u):
                n = 2 * m + u
                act.wait_ge(mv_done, n + 1)
                act.activation(std[:, u, :], mv[:, u, 1:2], ACT.Sqrt, bias=eps[:, :]).then_inc(std_done, 1)

            def norm(m, u):
                if not inside(m, u, TT):
                    return
                n = 2 * m + u
                deviation(m, u)
                act.wait_ge(xn_done, n + 1)
                if not isinstance(m, int) or m >= 1:
                    act.wait_ge(xh_turned, n - 1)
                    act.wait_ge(xl_done, n - 1)
                act.activation(xh[:, u, :], xn[:, u, :], ACT.Copy).then_inc(xh_done, 1)

            def turned(m, u):
                if not inside(m, u, TT):
                    return
                n = 2 * m + u
                act.wait_ge(xh_turned, n + 1)
                if not isinstance(m, int) or m >= 1:
                    act.wait_ge(qkv_done, n - 1)
                    act.wait_ge(xT_kept, n - 1)
                act.activation(xTc[:, u, 0, :, :], tr_ps[0][:, :, :], ACT.Copy).then_inc(xTh_done, 1)

            def post(m, u):
                if not inside(m, u, TT):
                    return
                n = 2 * m + u
                act.wait_ge(mult_done, n + 1)
                if not isinstance(m, int) or m >= 1:
                    act.wait_ge(stored[u], 48 * m)
                act.activation(v[:, u, :, 0:HD],
                               qkv_ps[u][:, QK * HD:QKV].rearrange("p (h c) -> p h c", h=KV),
                               ACT.Copy, scale=1.0 / W_SCALE).then_inc(v_done, 1)
                act.wait_ge(rot_done, n + 1)
                act.activation(stack[:, u, :, 0:HD], rot[:, :, :, :].rearrange("p h c f -> p h (c f)"),
                               ACT.Copy).then_inc(hi_done, 1)

            def step(m, u):
                norm(*at(m, u, 2))
                turned(*at(m, u, 1))
                post(m, u)

            act.wait_ge(eps_set, 1)
            act.wait_ge(ones_set, 1)
            norm(0, 0)
            norm(0, 1)
            for s in range(KT):
                act.wait_ge(w_loaded[s % STAGE], 48 * (s // STAGE + 1))
                act.activation(w[:, 0, s, :], w_in[:, s % STAGE, :], ACT.Copy, scale=W_SCALE
                               ).then_inc(whi_done, 1)
                if s < 2:
                    turned(0, s)
                if s >= KT - 2:
                    norm(1, s - KT + 2)
            turned(1, 0)
            post(0, 0)
            post(0, 1)
            with act.Fori(1, TT // 2 - 1) as m:
                step(m, 0)
                step(m, 1)
            step(TT // 2 - 1, 0)
            step(TT // 2 - 1, 1)

        @block.vector
        def _(dve):
            def norm(m, u):
                if not inside(m, u, TT):
                    return
                n = 2 * m + u
                dve.wait_ge(x_loaded[u], 16 * (m + 1))
                for h in range(2):
                    last = dve.bn_stats(bn[:, h, :], xin[:, u, h * BANK:(h + 1) * BANK])
                last.then_inc(bn_done, 1)
                wait_alone(dve, bn_done, n + 1, bn_seen)
                dve.bn_aggr(mv[:, u, :], bn[:, :, :]).then_inc(mv_done, 1)
                dve.wait_ge(std_done, n + 1)
                dve.reciprocal(rstd[:, u, :], std[:, u, :]).then_inc(rstd_done, 1)
                dve.wait_ge(rstd_done, n + 1)
                if not isinstance(m, int) or m >= 1:
                    dve.wait_ge(xl_done, n - 1)
                dve.tensor_scalar(xn[:, u, :], xin[:, u, :], mv[:, u, 0:1], rstd[:, u, :],
                                  ALU.subtract, ALU.mult).then_inc(xn_done, 1)

            def turned(m, u):
                if not inside(m, u, TT):
                    return
                n = 2 * m + u
                dve.wait_ge(xl_turned, n + 1)
                if not isinstance(m, int) or m >= 1:
                    dve.wait_ge(qkv_done, n - 1)
                    dve.wait_ge(xT_kept, n - 1)
                dve.tensor_copy(xTc[:, u, 1, :, :], tr_ps[1][:, :, :]).then_inc(xTl_done, 1)

            def post(m, u):
                if not inside(m, u, TT):
                    return
                n = 2 * m + u
                dve.wait_ge(qkv_done, n + 1)
                pairs = qkv_ps[u][:, 0:QK * HD].rearrange("p (h f c) -> p c h f", h=QK, c=2)
                trig = cs[:, bass.ds(n, 1), :, :].rearrange("p t c f -> p c t f")
                for k, (c, q) in enumerate([(0, 0), (1, 1), (0, 1), (1, 0)]):
                    last = dve.tensor_tensor(rot_t[:, k, :, :], pairs[:, c, :, :],
                                             trig[:, q, :, :].to_broadcast([P, QK, HALF]), ALU.mult)
                last.then_inc(mult_done, 1)
                dve.wait_ge(mult_done, n + 1)
                if not isinstance(m, int) or 2 * m + u >= 1:
                    dve.wait_ge(hi_done, n)
                dve.tensor_tensor(rot[:, :, 0, :], rot_t[:, 0, :, :], rot_t[:, 1, :, :], ALU.subtract)
                dve.tensor_tensor(rot[:, :, 1, :], rot_t[:, 2, :, :], rot_t[:, 3, :, :],
                                  ALU.add).then_inc(rot_done, 1)
                dve.wait_ge(v_done, n + 1)
                dve.scalar_tensor_tensor(v[:, u, :, VH:VW],
                                         qkv_ps[u][:, QK * HD:QKV].rearrange("p (h c) -> p h c", h=KV),
                                         1.0 / W_SCALE, v[:, u, :, 0:HD], ALU.mult, ALU.subtract
                                         ).then_inc(vlo_done, 1)
                dve.wait_ge(hi_done, n + 1)
                full = rot[:, :, :, :].rearrange("p h c f -> p h (c f)")
                dve.tensor_tensor(stack[:, u, 0:HEADS, 2 * HD:STACK], full[:, 0:HEADS, :],
                                  stack[:, u, 0:HEADS, 0:HD], ALU.subtract)
                dve.tensor_tensor(stack[:, u, HEADS:QK, HD:2 * HD], full[:, HEADS:QK, :],
                                  stack[:, u, HEADS:QK, 0:HD], ALU.subtract).then_inc(lo_done, 1)

            def step(m, u):
                norm(*at(m, u, 2))
                turned(*at(m, u, 1))
                post(m, u)

            dve.memset(eps[:, :], EPS).then_inc(eps_set, 1)
            norm(0, 0)
            norm(0, 1)
            for s in range(KT):
                dve.wait_ge(whi_done, s + 1)
                dve.scalar_tensor_tensor(w[:, 1, s, :], w_in[:, s % STAGE, :], W_SCALE, w[:, 0, s, :],
                                         ALU.mult, ALU.subtract).then_inc(wlo_done, 1)
                if s < 2:
                    turned(0, s)
                if s >= KT - 2:
                    norm(1, s - KT + 2)
            turned(1, 0)
            dve.wait_ge(cs_loaded, 16)
            post(0, 0)
            post(0, 1)
            with dve.Fori(1, TT // 2 - 1) as m:
                step(m, 0)
                step(m, 1)
            step(TT // 2 - 1, 0)
            step(TT // 2 - 1, 1)

        @block.tensor
        def _(pe):
            def turn(m, u):
                if not inside(m, u, TT):
                    return
                n = 2 * m + u
                for part, (src, done, free, out) in enumerate([(xh, xh_done, xTh_done, xh_turned),
                                                               (xl, xl_done, xTl_done, xl_turned)]):
                    pe.wait_ge(done, n + 1)
                    if not isinstance(m, int) or n >= 1:
                        pe.wait_ge(free, n)
                    cols = src[:, u, :].rearrange("p (d s) -> p s d", s=KT)
                    for s in range(KT):
                        last = pe.transpose(tr_ps[part][:, s, :], cols[:, s, :], ident[:, :])
                    last.then_inc(out, 1)

            def operands(m, u):
                n = 2 * m + u
                pe.wait_ge(xTh_done, n + 1)
                pe.wait_ge(xTl_done, n + 1)
                if not isinstance(m, int) or m >= 1:
                    pe.wait_ge(vlo_done, n - 1)
                    pe.wait_ge(mult_done, n - 1)

            def contract(u, s):
                for k, (xp, wp) in enumerate([(0, 0), (0, 1), (1, 0)]):
                    for c in range(QKV // BANK):
                        cols = slice(c * BANK, (c + 1) * BANK)
                        last = pe.matmul(qkv_ps[u][:, cols], xTc[:, u, xp, s, :], w[:, wp, s, cols],
                                         start=(s == 0 and k == 0), stop=(s == KT - 1 and k == 2))
                if s == KT - 1:
                    last.then_inc(qkv_done, 1)

            def products(m, u):
                operands(m, u)
                for s in range(KT):
                    contract(u, s)

            pe.wait_ge(masks_done, 1)
            turn(0, 0)
            turn(0, 1)
            operands(0, 0)
            for s in range(KT):
                pe.wait_ge(whi_done, s + 1)
                pe.wait_ge(wlo_done, s + 1)
                contract(0, s)
                if s == KT // 2:
                    operands(0, 1)
                if s >= KT // 2:
                    contract(1, s - KT // 2)
            turn(1, 0)
            for s in range(KT // 2, KT):
                contract(1, s)
            with pe.Fori(1, TT // 2 - 1) as m:
                for u in range(2):
                    turn(*at(m, u, 1))
                    products(m, u)
            turn(TT // 2 - 1, 1)
            products(TT // 2 - 1, 0)
            products(TT // 2 - 1, 1)


def attend(nc, qk_d, v_d, o_d, wo, ident, identb, maskb, o, o_stored, a, a_loaded, w_in, w_loaded):
    NH = B * HEADS
    R = 2 * REP
    POOL_TILES = [0, 1, 2, 3, 5]
    DVE_TILES = [4, 6, 7]
    TB = BANK // P
    SC = [(t, max(c, t * P), c + BANK) for t in range(ST) for c in range(t * P // BANK * BANK, S, BANK)]
    MX = [(t, c, min(c + BANK, (t + 1) * P)) for t in range(ST) for c in range(0, (t + 1) * P, BANK)]
    NC = len(SC)
    SC_BANKS, MX_BANKS = 3, 3
    WIDE = BANK // VW
    START = [sum(S - k * P for k in range(t)) - t * P for t in range(ST)]
    COLS = START[-1] + S
    OW = WIDE * VW + (ST - WIDE) * VH
    with ExitStack() as ctx:
        def sb(name, shape, dt):
            return ctx.enter_context(nc.sbuf_tensor(name, shape, dt))

        def sem(name):
            return ctx.enter_context(nc.semaphore(name))

        qkn = sb("qkn", [P, 2, ST, (REP + 1) * STACK], F16)
        vn = sb("vn", [P, 2, ST, VW], F16)
        qT = sb("qT", [P, REP, S], F16)
        kT = sb("kT", [P, 2, S], F16)
        probs = sb("probs", [P, 2, COLS], F32)
        p_hi = probs[:, :, :].bitcast(BF16).rearrange("p u (s c) -> p u s c", c=2)[:, :, :, 1]
        p_lo = sb("p_lo", [P, 2, COLS], F16)
        shift = sb("shift", [P, 2, ST], F16)
        part = sb("part", [P, 2, ST - TB], F16)
        sums = sb("sums", [P, 2, ST * VW], F32)
        rsum = sb("rsum", [P, ST], F32)
        o_sum = sb("o_sum", [P, ST, HD], F32)
        sc_ps = [ctx.enter_context(nc.psum_tensor(f"sc_ps{i}", [P, BANK], F32)) for i in range(SC_BANKS)]
        mx_ps = [ctx.enter_context(nc.psum_tensor(f"mx_ps{i}", [P, BANK], F32)) for i in range(MX_BANKS)]
        o_ps = ctx.enter_context(nc.psum_tensor("o_ps", [P, BANK], F32))
        tr_ps = ctx.enter_context(nc.psum_tensor("tr_ps", [P, S], F16))

        qk_loaded = [sem(f"qk_loaded{i}") for i in range(2)]
        v_loaded = [sem(f"v_loaded{i}") for i in range(2)]
        ones_set = sem("ones_set_a")
        zeros_set = sem("zeros_set_a")
        k_done = sem("k_done")
        q_done = sem("q_done")
        mx_ready = sem("mx_ready")
        mx_taken = sem("mx_taken")
        shift_turned = sem("shift_turned")
        shift_done = sem("shift_done")
        q_turned = sem("q_turned")
        k_turned = sem("k_turned")
        sc_ready = sem("sc_ready")
        exp_done = sem("exp_done")
        lo_pool = sem("lo_pool")
        lo_dve = sem("lo_dve")
        p_used = sem("p_used")
        o_copied = sem("o_copied")
        shift_ready = sem("shift_ready")
        rsum_done = sem("rsum_done")
        o_added = sem("o_added")
        o_done = sem("o_done")

        block = ctx.enter_context(nc.Block())

        def head(m, r):
            return R * m + r

        def low(eng, m, r, t, done):
            if not exists(m, r):
                return
            eng.wait_ge(exp_done, NC * head(m, r) + chunks_to(t))
            c = slice(START[t] + t * P, START[t] + S)
            eng.tensor_tensor(p_lo[:, r % 2, c], probs[:, r % 2, c], p_hi[:, r % 2, c], ALU.subtract
                              ).then_inc(done, 1)

        def chunks_to(t):
            return sum(c[0] <= t for c in SC)

        def exists(m, r):
            return inside(m, r, NH, R)

        def steps(eng, step):
            for r in range(-3, 0):
                step(*at(0, 0, r, R))
            for r in range(R):
                step(0, r)
            with eng.Fori(1, NH // R - 1) as m:
                for r in range(R):
                    step(m, r)
            for r in range(R + 2):
                step(*at(NH // R - 1, 0, r, R))

        @block.sync
        def _(sp):
            def load_qk(g, u):
                sp.dma_start(qkn[:, u, :, :], qk_d.rearrange("b g p t c -> (b g) p t c")[g]
                             ).then_inc(qk_loaded[u], 16)

            def load_v(g, u):
                sp.dma_start(vn[:, u, :, :], v_d.rearrange("b g p t c -> (b g) p t c")[g]
                             ).then_inc(v_loaded[u], 16)

            def store(g, u):
                sp.wait_ge(o_done, REP * (g + 1))
                sp.dma_start(o_d.rearrange("b g p t c -> (b g) p t c")[g], o[:, u, :, :]
                             ).then_inc(o_stored[u], 16)

            for g in range(2):
                load_qk(g, g)
                load_v(g, g)
            with sp.Fori(0, GROUPS // 2 - 1) as m:
                for u in range(2):
                    g = 2 * m + u
                    sp.wait_ge(q_turned, REP * (g + 1))
                    load_qk(g + 2, u)
                    sp.wait_ge(p_used, ST * REP * (g + 1))
                    load_v(g + 2, u)
                    store(g, u)
            for u in range(2):
                sp.wait_ge(o_stored[u], 16 * KV // 2)
            for u in range(2):
                load_attended(sp, o_d, a, a_loaded, 0, 0, u)
            for s in range(STAGE):
                load_wo(sp, wo, w_in, w_loaded, s)
            for u in range(2):
                store(GROUPS - 2 + u, u)

        @block.tensor
        def _(pe):
            def turn_key(m, r):
                if r % REP or not exists(m, r):
                    return
                h, u = head(m, r), r // REP
                if not isinstance(m, int) or h >= 2:
                    pe.wait_ge(shift_done, h - 1)
                pe.wait_ge(qk_loaded[u], 16 * (m + 1))
                for t in range(ST):
                    last = pe.transpose(tr_ps[0:STACK, t * P:(t + 1) * P],
                                        qkn[:, u, t, REP * STACK:], ident[:, :])
                last.then_inc(k_turned, 1)

            def turn(m, r):
                if not exists(m, r):
                    return
                h, u, q = head(m, r), r // REP, r % REP
                if q == 0:
                    pe.wait_ge(k_done, 2 * m + u + 1)
                elif not isinstance(m, int) or h >= 2:
                    pe.wait_ge(shift_done, h - 1)
                else:
                    pe.wait_ge(q_done, h)
                for t in range(ST):
                    last = pe.transpose(tr_ps[0:STACK, t * P:(t + 1) * P],
                                        qkn[:, u, t, q * STACK:(q + 1) * STACK], ident[:, :])
                last.then_inc(q_turned, 1)

            def turn_shifts(m, r):
                if not exists(m, r):
                    return
                h = head(m, r)
                pe.wait_ge(shift_ready, h + 1)
                pe.wait_ge(q_done, min(h + 2, NH) if isinstance(m, int) else h + 2)
                for t in range(ST):
                    last = pe.transpose(tr_ps[STACK:STACK + 1, t * P:(t + 1) * P], shift[:, r % 2, t:t + 1],
                                        ident[:, :])
                last.then_inc(shift_turned, 1)

            def maxima(m, r, slot):
                if not exists(m, r):
                    return
                h, u, q = head(m, r), r // REP, r % REP
                if slot == 0:
                    pe.wait_ge(q_done, h + 1)
                    pe.wait_ge(k_done, 2 * m + u + 1)
                for i, (t, c, e) in enumerate(MX):
                    if t != slot:
                        continue
                    if not isinstance(m, int) or NC * h + i >= MX_BANKS:
                        pe.wait_ge(mx_taken, NC * h + i + 1 - MX_BANKS)
                    bank = mx_ps[i % MX_BANKS]
                    last = pe.matmul(bank[:, 0:e - c], qT[0:STACK, q, t * P:(t + 1) * P], kT[0:STACK, u, c:e],
                                     start=True, stop=(e <= t * P))
                    if e > t * P:
                        last = pe.matmul(bank[:, t * P - c:e - c], identb[:, :], maskb[:, :],
                                         start=False, stop=True)
                    last.then_inc(mx_ready, 1)

            def scores(m, r, slot):
                if not exists(m, r):
                    return
                h, u, q = head(m, r), r // REP, r % REP
                if slot == 0:
                    pe.wait_ge(shift_done, h + 1)
                for i, (t, c, e) in enumerate(SC):
                    if t != slot:
                        continue
                    if not isinstance(m, int) or NC * h + i >= SC_BANKS:
                        pe.wait_ge(exp_done, NC * h + i + 1 - SC_BANKS)
                    bank = sc_ps[i % SC_BANKS]
                    last = pe.matmul(bank[:, 0:e - c], kT[0:STACK + 1, u, t * P:(t + 1) * P],
                                     qT[0:STACK + 1, q, c:e], start=True, stop=(c > t * P))
                    if c == t * P:
                        last = pe.matmul(bank[:, 0:P], maskb[:, :], identb[:, :], start=False, stop=True)
                    last.then_inc(sc_ready, 1)

            def outputs(m, r, k):
                if not exists(m, r):
                    return
                h, u = head(m, r), r // REP
                if k == 0:
                    if r % REP == 0:
                        pe.wait_ge(v_loaded[u], 16 * (m + 1))
                    if not isinstance(m, int) or h >= 1:
                        pe.wait_ge(o_copied, h)
                if k in POOL_TILES:
                    pe.wait_ge(lo_pool, len(POOL_TILES) * h + POOL_TILES.index(k) + 1)
                else:
                    pe.wait_ge(lo_dve, len(DVE_TILES) * h + DVE_TILES.index(k) + 1)
                for t in range(k, ST):
                    q = slice(START[k] + t * P, START[k] + (t + 1) * P)
                    hi, lo = p_hi[:, r % 2, q], p_lo[:, r % 2, q]
                    c = min(t, WIDE) * VW + max(t - WIDE, 0) * VH
                    if t < WIDE:
                        pe.matmul(o_ps[:, c:c + VW], hi, vn[:, u, k, :], start=(k + t == 0), stop=False)
                    else:
                        pe.matmul(o_ps[:, c:c + VH], hi, vn[:, u, k, 0:VH], start=False, stop=False)
                        pe.matmul(o_ps[:, c:c + HD], hi, vn[:, u, k, VH:VW], start=False, stop=False)
                    last = pe.matmul(o_ps[:, c:c + VH], lo, vn[:, u, k, 0:VH], start=False,
                                     stop=(k == ST - 1))
                last.then_inc(p_used, 1)

            pe.wait_ge(ones_set, 1)

            def step(m, r):
                for t in range(ST):
                    scores(m, r, t)
                    maxima(*at(m, r, 2, R), t)
                    if t == 1:
                        turn_shifts(*at(m, r, 1, R))
                        outputs(*at(m, r, -1, R), 0)
                    if t == 4:
                        turn_key(*at(m, r, 3, R))
                    if t == 6:
                        turn(*at(m, r, 3, R))
                    if t >= 1:
                        outputs(*at(m, r, -1, R), t)

            steps(pe, step)

        @block.scalar
        def _(act):
            def key(m, r):
                if r % REP or not exists(m, r):
                    return
                h, u = head(m, r), r // REP
                act.wait_ge(k_turned, 2 * m + u + 1)
                if not isinstance(m, int) or m >= 1:
                    act.wait_ge(sc_ready, NC * (h - REP))
                act.activation(kT[0:STACK, u, :], tr_ps[0:STACK, :], ACT.Copy).then_inc(k_done, 1)

            def queries(m, r):
                if not exists(m, r):
                    return
                h = head(m, r)
                act.wait_ge(q_turned, h + 1)
                if not isinstance(m, int) or h >= REP:
                    act.wait_ge(sc_ready, NC * (h - REP + 1))
                act.activation(qT[0:STACK, r % REP, :], tr_ps[0:STACK, :], ACT.Copy).then_inc(q_done, 1)

            def exps(m, r, slot):
                if not exists(m, r):
                    return
                h = head(m, r)
                if not isinstance(m, int) or h >= 2:
                    act.wait_ge(p_used, ST * (h - 2) + slot + 1)
                for i, (t, c, e) in enumerate(SC):
                    if t == slot:
                        act.wait_ge(sc_ready, NC * h + i + 1)
                        act.activation(probs[:, r % 2, START[t] + c:START[t] + e], sc_ps[i % SC_BANKS][:, 0:e - c], ACT.Exp,
                                       scale=float(1.0 / np.sqrt(HD))).then_inc(exp_done, 1)

            def shifts(m, r):
                if not exists(m, r):
                    return
                h = head(m, r)
                act.wait_ge(shift_turned, h + 1)
                act.activation(qT[STACK:STACK + 1, r % REP, :], tr_ps[STACK:STACK + 1, :], ACT.Copy
                               ).then_inc(shift_done, 1)

            def copy_sums(m, r):
                if not exists(m, r):
                    return
                h = head(m, r)
                act.wait_ge(p_used, ST * (h + 1))
                if not isinstance(m, int) or h >= 2:
                    act.wait_ge(o_done, h - 1)
                act.activation(sums[:, r % 2, 0:OW], o_ps[:, 0:OW], ACT.Copy).then_inc(o_copied, 1)

            def step(m, r):
                for t in range(ST):
                    exps(m, r, t)
                    if t == 0:
                        copy_sums(*at(m, r, -2, R))
                    if t == 1:
                        shifts(*at(m, r, 1, R))
                    if t == 4:
                        key(*at(m, r, 3, R))
                    if t == 6:
                        queries(*at(m, r, 3, R))

            steps(act, step)

        @block.vector
        def _(dve):
            dve.memset(kT[STACK:STACK + 1, :, :], 1.0).then_inc(ones_set, 1)
            dve.memset(sums[:, :, OW:], 0.0).then_inc(zeros_set, 1)
            dve.wait_ge(zeros_set, 1)

            def maxima(m, r, slot):
                if not exists(m, r):
                    return
                h = head(m, r)
                for i, (t, c, e) in enumerate(MX):
                    if t != slot:
                        continue
                    dve.wait_ge(mx_ready, NC * h + i + 1)
                    if i == 0 and (not isinstance(m, int) or h >= 2):
                        dve.wait_ge(shift_turned, h - 1)
                    out = shift[:, r % 2, t:t + 1] if t < TB else part[:, c // BANK, t - TB:t - TB + 1]
                    dve.tensor_reduce(out, mx_ps[i % MX_BANKS][:, 0:e - c], AX_X, ALU.max,
                                      negate=True).then_inc(mx_taken, 1)
                if slot == ST - 1:
                    dve.wait_ge(mx_taken, NC * (h + 1))
                    dve.tensor_tensor(shift[:, r % 2, TB:ST], part[:, 0, :], part[:, 1, :], ALU.min
                                      ).then_inc(shift_ready, 1)

            def normalise(m, r):
                if not exists(m, r):
                    return
                h, u, q = head(m, r), r // REP, r % REP
                all_sums = sums[:, r % 2, :].rearrange("p (t c) -> p t c", c=VW)
                dve.wait_ge(o_copied, h + 1)
                dve.reciprocal(rsum[:, :], all_sums[:, :, HD]).then_inc(rsum_done, 1)
                dve.tensor_tensor(o_sum[:, :, :], all_sums[:, :, 0:HD], all_sums[:, :, VH:VW], ALU.add
                                  ).then_inc(o_added, 1)
                if q == 0 and (not isinstance(m, int) or m >= 1):
                    dve.wait_ge(o_stored[u], 16 * m)
                dve.wait_ge(rsum_done, h + 1)
                dve.wait_ge(o_added, h + 1)
                dve.tensor_tensor(o[:, u, :, q * HD:(q + 1) * HD], o_sum[:, :, :],
                                  rsum[:, :].unsqueeze(2).to_broadcast([P, ST, HD]), ALU.mult
                                  ).then_inc(o_done, 1)

            def step(m, r):
                for t in range(ST):
                    maxima(*at(m, r, 2, R), t)
                    if t == 1:
                        normalise(*at(m, r, -2, R))
                    elif max(t - 1, 0) < len(DVE_TILES):
                        low(dve, *at(m, r, -1, R), DVE_TILES[max(t - 1, 0)], lo_dve)

            steps(dve, step)

        @block.gpsimd
        def _(pool):
            def step(m, r):
                for t in POOL_TILES:
                    low(pool, m, r, t, lo_pool)

            steps(pool, step)


def load_attended(eng, o_d, a, a_loaded, b, m, u):
    eng.dma_start(a[:, u, :].rearrange("p (g c) -> p g c", g=KV),
                  o_d.rearrange("b g p t c -> b t p g c")[b, 2 * m + u]).then_inc(a_loaded[u], 16)


def load_wo(eng, wo, w_in, w_loaded, s):
    eng.dma_start(w_in[:, s % STAGE, :], wo.rearrange("(s p) n -> p s n", p=P)[:, s, :]
                  ).then_inc(w_loaded[s % STAGE], 16)


def project_out(nc, o_d, wo, s_d, ident, o_stored, a, a_loaded, w_in, w_loaded, lanes_in, scales_gu, zeros_gu,
                scales_d, zeros_d, g_idx_gu, lanes, sc_d, z_d, scd, zd, sel_gu):
    PIECE = 688
    PIECES = 2 * INTER // PIECE
    WORDS = PIECE // NIB
    R_GU, R_D = 64 + G_GU, 64 + G_D
    with ExitStack() as ctx:
        def sb(name, shape, dt):
            return ctx.enter_context(nc.sbuf_tensor(name, shape, dt))

        def sem(name):
            return ctx.enter_context(nc.semaphore(name))

        ah = sb("ah", [P, 2, D], F16)
        al = sb("al", [P, 2, D], F16)
        aT = sb("aT", [P, 2, 2, KT, P], F16)
        w = sb("wo", [P, 2, KT, D], F16)
        s_out = sb("s_out", [P, 2, D], F32)
        out_ps = [ctx.enter_context(nc.psum_tensor(f"out_ps{i}", [P, FULL], F32)) for i in range(2)]
        tr_ps = [ctx.enter_context(nc.psum_tensor(f"tro_ps{i}", [P, KT, P], F16)) for i in range(2)]

        whi_done = sem("wohi_done")
        wlo_done = sem("wolo_done")
        ah_done = sem("ah_done")
        al_done = sem("al_done")
        ah_turned = sem("ah_turned")
        al_turned = sem("al_turned")
        aTh_done = sem("aTh_done")
        aTl_done = sem("aTl_done")
        out_ready = sem("out_ready")
        out_done = sem("out_done")
        stored = [sem(f"s_stored{i}") for i in range(2)]
        s_v = s_d.rearrange("(t p) n -> t p n", p=P)

        sc = sb("tb_sc", [R_GU, 2, PIECE], F32)
        sc_dn = sb("tb_sc_dn", [R_D, D], F32)
        rest = sb("tb_rest", [R_D, D], F32)
        hi = sb("tb_hi", [R_GU, 2, PIECE], BF16)
        mid = sb("tb_mid", [R_D, D], BF16)
        lo = sb("tb_lo", [R_D, D], BF16)
        zw = sb("tb_zw", [G_GU, 2, WORDS], U32)
        zw_dn = sb("tb_zw_dn", [G_D, D // NIB], U32)
        zn = sb("tb_zn", [G_D, NIB, D // NIB], U32)
        zt = sb("tb_zt", [R_GU, 2, PIECE], BF16)
        idx = sb("tb_idx", [R_GU, D], I32)
        idf = sb("tb_idf", [R_GU, 2, D], F32)

        tb_loaded = [sem(f"tb_loaded{i}") for i in range(2)]
        dn_loaded = sem("tb_dn_loaded")
        idx_loaded = sem("tb_idx_loaded")
        zeroed = sem("tb_zeroed")
        selecting = sem("tb_selecting")
        dn_step = sem("tb_dn_step")
        tb_step = sem("tb_step")
        built = sem("tb_built")
        tb_stored = [sem(f"tb_stored{i}") for i in range(2)]

        block = ctx.enter_context(nc.Block())

        @block.sync
        def _(sp):
            def load(b, m, u):
                sp.wait_ge(al_done, b * ST + 2 * m + u - 1)
                load_attended(sp, o_d, a, a_loaded, b, m, u)

            def load_piece(c, u):
                cols, words = bass.ds((2 * c + u) * PIECE, PIECE), bass.ds((2 * c + u) * WORDS, WORDS)
                for k in range(3):
                    sp.dma_start(sc[32 * k:32 * k + G_GU, u, :], scales_gu[:, cols]).then_inc(tb_loaded[u], 16)
                sp.dma_start(zw[:, u, :], zeros_gu[:, words]).then_inc(tb_loaded[u], 16)

            def store_piece(c, u):
                cols = bass.ds((2 * c + u) * PIECE, PIECE)
                sp.wait_ge(built, 2 * c + u + 1)
                sp.dma_start(sc_d[:, cols], hi[:, u, :]).then_inc(tb_stored[u], 16)
                sp.dma_start(z_d[:, cols], zt[:, u, :]).then_inc(tb_stored[u], 16)

            load(0, 1, 0)
            load(0, 1, 1)
            for s in range(STAGE, KT):
                sp.wait_ge(wlo_done, s - STAGE + 1)
                load_wo(sp, wo, w_in, w_loaded, s)
            sp.wait_ge(zeroed, 1)
            for u in range(2):
                load_piece(0, u)
            sp.dma_start(lanes[:, :], lanes_in).then_inc(idx_loaded, 16)
            sp.dma_start(idx[:, :], g_idx_gu.rearrange("(a i) -> a i", a=1).broadcast_to([R_GU, D])
                         ).then_inc(idx_loaded, 16)
            for k in range(3):
                sp.dma_start(sc_dn[32 * k:32 * k + G_D, :], scales_d).then_inc(dn_loaded, 16)
            sp.dma_start(zw_dn[:, :], zeros_d).then_inc(dn_loaded, 16)
            for u in range(2):
                load(0, 2, u)
            for u in range(2):
                load(0, 3, u)
                store_piece(0, u)
                load_piece(1, u)
            for u in range(2):
                sp.wait_ge(o_stored[u], 16 * GROUPS // 2)
            with sp.Fori(0, PIECES // 2 - 2) as m:
                for u in range(2):
                    load(1, m, u)
                    store_piece(m + 1, u)
                    load_piece(m + 2, u)
            for u in range(2):
                load(1, PIECES // 2 - 2, u)
                store_piece(PIECES // 2 - 1, u)
            for m in range(PIECES // 2 - 1, ST // 2):
                for u in range(2):
                    load(1, m, u)
            for u in range(2):
                sp.wait_ge(tb_stored[u], 32 * PIECES // 2)

        @block.gpsimd
        def _(pool):
            pool.memset(sc[:, :, :], 0.0)
            pool.memset(sc_dn[:, :], 0.0)
            pool.memset(zt[:, :, :], 0.0)
            pool.memset(zd[:, :], 0.0).then_inc(zeroed, 1)
            with pool.Fori(0, TT // 2) as m:
                for u in range(2):
                    pool.wait_ge(out_done, 2 * m + u + 1)
                    pool.dma_start(s_v[2 * m + u], s_out[:, u, :]).then_inc(stored[u], 16)
            for u in range(2):
                pool.wait_ge(stored[u], 16 * TT // 2)

        @block.scalar
        def _(act):
            def high(m, u):
                if not inside(m, u, TT):
                    return
                n = 2 * m + u
                act.wait_ge(a_loaded[u], 16 * (m + 1))
                if not isinstance(m, int) or m >= 1:
                    act.wait_ge(ah_turned, n - 1)
                    act.wait_ge(al_done, n - 1)
                act.activation(ah[:, u, :], a[:, u, :], ACT.Copy).then_inc(ah_done, 1)

            def turned(m, u):
                if not inside(m, u, TT):
                    return
                n = 2 * m + u
                act.wait_ge(ah_turned, n + 1)
                if not isinstance(m, int) or m >= 1:
                    act.wait_ge(out_ready, n - 1)
                act.activation(aT[:, u, 0, :, :], tr_ps[0][:, :, :], ACT.Copy).then_inc(aTh_done, 1)

            def post(m, u):
                if not inside(m, u, TT):
                    return
                n = 2 * m + u
                act.wait_ge(out_ready, n + 1)
                if not isinstance(m, int) or m >= 1:
                    act.wait_ge(stored[u], 16 * m)
                act.activation(s_out[:, u, :], out_ps[u][:, :], ACT.Copy, scale=1.0 / W_SCALE
                               ).then_inc(out_done, 1)

            def step(m, u):
                high(*at(m, u, 2))
                turned(*at(m, u, 1))
                post(m, u)

            high(0, 0)
            high(0, 1)
            for s in range(KT):
                act.wait_ge(w_loaded[s % STAGE], 16 * (s // STAGE + 1))
                act.activation(w[:, 0, s, :], w_in[:, s % STAGE, :], ACT.Copy, scale=W_SCALE
                               ).then_inc(whi_done, 1)
                if s < 2:
                    turned(0, s)
            high(1, 0)
            high(1, 1)
            turned(1, 0)
            post(0, 0)
            post(0, 1)
            with act.Fori(1, TT // 2 - 1) as m:
                step(m, 0)
                step(m, 1)
            step(TT // 2 - 1, 0)
            step(TT // 2 - 1, 1)

        @block.vector
        def _(dve):
            def low(m, u):
                if not inside(m, u, TT):
                    return
                n = 2 * m + u
                dve.wait_ge(ah_done, n + 1)
                if not isinstance(m, int) or m >= 1:
                    dve.wait_ge(al_turned, n - 1)
                dve.tensor_tensor(al[:, u, :], a[:, u, :], ah[:, u, :], ALU.subtract).then_inc(al_done, 1)

            def turned(m, u):
                if not inside(m, u, TT):
                    return
                n = 2 * m + u
                dve.wait_ge(al_turned, n + 1)
                if not isinstance(m, int) or m >= 1:
                    dve.wait_ge(out_ready, n - 1)
                dve.tensor_copy(aT[:, u, 1, :, :], tr_ps[1][:, :, :]).then_inc(aTl_done, 1)

            def step(m, u):
                low(*at(m, u, 2))
                turned(*at(m, u, 1))

            def chain(done, first, ops):
                for k, op in enumerate(ops):
                    if k:
                        dve.wait_ge(done, first + k)
                    op().then_inc(done, 1)

            def split(x, r, md, l, hold, g):
                rows = 64 + g
                return [lambda: dve.tensor_scalar(hold[0:rows, :], x, W_SCALE, None, ALU.mult),
                        lambda: dve.scalar_tensor_tensor(r, x, W_SCALE, hold[0:rows, :], ALU.mult, ALU.subtract),
                        lambda: dve.tensor_copy(md, r),
                        lambda: dve.tensor_tensor(l, r, md, ALU.subtract),
                        lambda: dve.tensor_copy(hold[32:64, :], md[32:64, :]),
                        lambda: dve.tensor_copy(hold[64:rows, :], l[64:rows, :])]

            def unpack(words, n, out):
                def values():
                    for k in range(NIB):
                        last = dve.tensor_scalar(n[:, k, :], words, 4 * k, 15,
                                                 ALU.logical_shift_right, ALU.bitwise_and)
                    return last
                return [values, lambda: dve.tensor_scalar(out.rearrange("g (c k) -> g k c", k=NIB), n, 1.0, None,
                                                          ALU.add)]

            def select():
                dve.wait_ge(idx_loaded, 32)
                chain(selecting, 0, [
                    lambda: dve.tensor_scalar(idf[:, 0, :], idx[:, :], 0.0, float(G_GU), ALU.is_lt, ALU.mult),
                    lambda: dve.tensor_tensor(idf[:, 1, :], idf[:, 0, :], idx[:, :], ALU.add),
                    lambda: dve.tensor_scalar(idf[:, 0, :], idf[:, 1, :], 0.0, float(G_GU - 1), ALU.max, ALU.min),
                    lambda: dve.tensor_scalar(sel_gu[0:R_GU, :], idf[:, 0, :], lanes[0:R_GU, 0:1], None,
                                              ALU.is_equal)])

            def down_tables():
                dve.wait_ge(dn_loaded, 64)
                chain(dn_step, 0, split(sc_dn[:, :], rest[:, :], mid[:, :], lo[:, :], scd, G_D)
                      + unpack(zw_dn[:, :], zn[:, :, :], zd[0:G_D, :]))

            def piece(c, u):
                dve.wait_ge(tb_loaded[u], 64 * (c + 1))
                if not isinstance(c, int) or c >= 1:
                    dve.wait_ge(tb_stored[u], 32 * c)
                ops = (split(sc[:, u, :], rest[0:R_GU, 0:PIECE], mid[0:R_GU, 0:PIECE], lo[0:R_GU, 0:PIECE],
                             hi[:, u, :], G_GU)
                       + unpack(zw[:, u, :], zn[0:G_GU, :, 0:WORDS], zt[0:G_GU, u, :]))
                first = len(ops) * (2 * c + u)
                chain(tb_step, first, ops[:-1])
                dve.wait_ge(tb_step, first + len(ops) - 1)
                ops[-1]().then_inc(tb_step, 1)
                dve.wait_ge(tb_step, first + len(ops))
                dve.tensor_copy(rest[0:1, 0:1], rest[0:1, 0:1]).then_inc(built, 1)

            low(0, 0)
            low(0, 1)
            for s in range(KT):
                dve.wait_ge(whi_done, s + 1)
                dve.scalar_tensor_tensor(w[:, 1, s, :], w_in[:, s % STAGE, :], W_SCALE, w[:, 0, s, :],
                                         ALU.mult, ALU.subtract).then_inc(wlo_done, 1)
                if s < 2:
                    turned(0, s)
            low(1, 0)
            low(1, 1)
            turned(1, 0)
            with dve.Fori(1, PIECES // 2 + 1) as m:
                for u in range(2):
                    step(m, u)
                    piece(m - 1, u)
            for m in range(PIECES // 2 + 1, TT // 2):
                step(m, 0)
                if m == TT // 2 - 2:
                    select()
                step(m, 1)
                if m == TT // 2 - 2:
                    down_tables()

        @block.tensor
        def _(pe):
            def turn(m, u):
                if not inside(m, u, TT):
                    return
                n = 2 * m + u
                for part, (src, done, free, out) in enumerate([(ah, ah_done, aTh_done, ah_turned),
                                                               (al, al_done, aTl_done, al_turned)]):
                    pe.wait_ge(done, n + 1)
                    if not isinstance(m, int) or n >= 1:
                        pe.wait_ge(free, n)
                    for s in range(KT):
                        last = pe.transpose(tr_ps[part][:, s, :], src[:, u, s * P:(s + 1) * P], ident[:, :])
                    last.then_inc(out, 1)

            def operands(m, u):
                n = 2 * m + u
                pe.wait_ge(aTh_done, n + 1)
                pe.wait_ge(aTl_done, n + 1)
                if not isinstance(m, int) or m >= 1:
                    pe.wait_ge(out_done, n - 1)

            def contract(u, s):
                for k, (xp, wp) in enumerate([(0, 0), (0, 1), (1, 0)]):
                    for c in range(D // BANK):
                        cols = slice(c * BANK, (c + 1) * BANK)
                        last = pe.matmul(out_ps[u][:, cols], aT[:, u, xp, s, :], w[:, wp, s, cols],
                                         start=(s == 0 and k == 0), stop=(s == KT - 1 and k == 2))
                if s == KT - 1:
                    last.then_inc(out_ready, 1)

            def products(m, u):
                operands(m, u)
                for s in range(KT):
                    contract(u, s)

            turn(0, 0)
            turn(0, 1)
            operands(0, 0)
            for s in range(KT):
                pe.wait_ge(whi_done, s + 1)
                pe.wait_ge(wlo_done, s + 1)
                contract(0, s)
                if s == KT // 2:
                    operands(0, 1)
                if s >= KT // 2:
                    contract(1, s - KT // 2)
            turn(1, 0)
            for s in range(KT // 2, KT):
                contract(1, s)
            with pe.Fori(1, TT // 2 - 1) as m:
                for u in range(2):
                    turn(*at(m, u, 1))
                    products(m, u)
            turn(TT // 2 - 1, 1)
            products(TT // 2 - 1, 0)
            products(TT // 2 - 1, 1)


def feed_forward(nc, x, qw_gu, qw_d, g_idx_d, lanes, sc_d, z_d, scd, zd, sel_gu, xT, s_d, out):
    R_GU, R_D = 64 + G_GU, 64 + G_D
    ROUNDS = NIB // 2
    PER = ROUNDS + 2
    DN = 2 * TT
    with ExitStack() as ctx:
        def sb(name, shape, dt):
            return ctx.enter_context(nc.sbuf_tensor(name, shape, dt))

        def sem(name):
            return ctx.enter_context(nc.semaphore(name))

        acc = sb("acc", [P, TT, D], F32)
        hT = sb("hT", [P, 2, CHUNK, T], F16)
        wg = sb("wg", [P, 2, 2, KT, 2 * P], F16)
        wd = sb("wd", [P, 2, CHUNK, D], F16)
        qwg = sb("qwg", [P, 2, 2, P], U32)
        qwd = sb("qwd", [P, 2, BANK], U32)
        nib = sb("nib", [P, BANK], U32)
        dif = sb("dif", [P, BANK], F32)
        wf = sb("wf", [P, 2, BANK], F32)
        h = sb("h", [P, 2, BANK], F32)
        zt = sb("zt", [R_GU, 2, 2, P], BF16)
        st = sb("st", [R_GU, 2, 2, P], BF16)
        idx = sb("idx", [R_D, 2, P], I32)
        idf = sb("idf", [R_D, 2, P], F32)
        sel = sb("sel", [R_D, 2, P], BF16)
        x_in = sb("x_in", [P, 2, BANK], F32)
        s_in = sb("s_in", [P, 2, BANK], F32)
        gate_ps = [ctx.enter_context(nc.psum_tensor(f"gate_ps{i}", [P, BANK], F32)) for i in range(2)]
        up_ps = [ctx.enter_context(nc.psum_tensor(f"up_ps{i}", [P, BANK], F32)) for i in range(2)]
        dn_ps = [ctx.enter_context(nc.psum_tensor(f"dn_ps{i}", [P, BANK], F32)) for i in range(2)]
        z_ps = ctx.enter_context(nc.psum_tensor("z_ps", [P, BANK], F32))
        s_ps = ctx.enter_context(nc.psum_tensor("s_ps", [P, BANK], F32))

        gu_loaded = [sem(f"gu_loaded{i}") for i in range(2)]
        dn_loaded = [sem(f"dn_loaded{i}") for i in range(2)]
        idx_loaded = [sem(f"idx_loaded{i}") for i in range(2)]
        acc_zeroed = sem("acc_zeroed")
        sel_step = sem("sel_step")
        sel_done = sem("sel_done")
        zs_ready = sem("zs_ready")
        nib_done = sem("nib_done")
        dif_done = sem("dif_done")
        wf_done = sem("wf_done")
        whi_done = sem("fwhi_done")
        wlo_done = sem("fwlo_done")
        gu_ready = sem("gu_ready")
        silu_done = sem("silu_done")
        h_done = sem("h_done")
        hhi_done = sem("hhi_done")
        hlo_done = sem("hlo_done")
        dn_ready = sem("dn_ready")
        dn_taken = sem("dn_taken")
        g_done = sem("g_done")
        xs_loaded = [sem(f"xs_loaded{i}") for i in range(2)]
        prod_done = sem("prod_done")
        sum_done = sem("sum_done")
        out_stored = sem("out_stored")

        qwg_v = qw_gu.rearrange("p (h f) -> p h f", h=2)
        z_v = z_d.rearrange("p (h f) -> p h f", h=2)
        sc_v = sc_d.rearrange("p (h f) -> p h f", h=2)
        x_v = x.rearrange("b (t p) d -> (b t) p d", p=P)
        s_v = s_d.rearrange("(t p) d -> t p d", p=P)
        out_v = out.rearrange("b (t p) d -> (b t) p d", p=P)

        def width(j):
            return FLAST if isinstance(j, int) and j == FTILES - 1 else P

        def first_round(j, kind):
            if kind == "g":
                return 0 if isinstance(j, int) and j == 0 else ROUNDS + PER * (j - 1)
            return ROUNDS + PER * j + (0 if isinstance(j, int) and j == FTILES - 1 else ROUNDS)

        def places(j):
            nxt = [("g", k) for k in range(ROUNDS)] if not (isinstance(j, int) and j == FTILES - 1) else []
            return (nxt + [("d", 0), ("d", 1)] + [None] * 8)[:8]

        def store(sp, k):
            t, n = k // 2, k % 2
            cols = slice(n * BANK, (n + 1) * BANK)
            sp.wait_ge(sum_done, k + 1)
            sp.dma_start(out_v[t][:, cols], acc[:, t, cols]).then_inc(out_stored, 16)

        block = ctx.enter_context(nc.Block())

        @block.sync
        def _(sp):
            def load_gu(j, u):
                w = width(j)
                f = bass.ds(j * P, w)
                sp.dma_start(qwg[:, u, :, 0:w], qwg_v[:, :, f]).then_inc(gu_loaded[u], 16)
                sp.dma_start(zt[:, u, :, 0:w], z_v[:, :, f]).then_inc(gu_loaded[u], 16)
                sp.dma_start(st[:, u, :, 0:w], sc_v[:, :, f]).then_inc(gu_loaded[u], 16)

            def load_dn(j, u):
                w = width(j)
                rows = qw_d[bass.ds(j * (P // NIB), w // NIB), :]
                for n in range(2):
                    sp.dma_start(qwd[0:w, n, :],
                                 rows[:, n * BANK:(n + 1) * BANK].unsqueeze(1).broadcast_to([w // NIB, NIB, BANK])
                                 ).then_inc(dn_loaded[n], 16)
                sp.dma_start(idx[:, u, 0:w],
                             g_idx_d.rearrange("(a i) -> a i", a=1)[:, bass.ds(j * P, w)].broadcast_to([R_D, w])
                             ).then_inc(idx_loaded[u], 16)

            def step(j, u):
                if not isinstance(j, int) or j + 2 < FTILES:
                    sp.wait_ge(wf_done, first_round(j, "g") + ROUNDS)
                    load_gu(j + 2, u)
                if not isinstance(j, int) or j + 1 < FTILES:
                    sp.wait_ge(wf_done, first_round(j, "d") + 2)
                    load_dn(j + 1, 1 - u)

            load_gu(0, 0)
            load_gu(1, 1)
            load_dn(0, 0)
            step(0, 0)
            step(1, 1)
            with sp.Fori(1, CHUNKS - 2) as c:
                for u in range(2):
                    step(CHUNK * c + u, u)
            for j in range(CHUNK * (CHUNKS - 2), FTILES):
                step(j, j % 2)
            for k in range(DN):
                t, n, u = k // 2, k % 2, k % 2
                cols = slice(n * BANK, (n + 1) * BANK)
                if k >= 2:
                    sp.wait_ge(sum_done, k - 1)
                sp.dma_start(x_in[:, u, :], x_v[t][:, cols]).then_inc(xs_loaded[u], 16)
                sp.dma_start(s_in[:, u, :], s_v[t][:, cols]).then_inc(xs_loaded[u], 16)
                if k >= 2:
                    store(sp, k - 2)
            store(sp, DN - 2)
            store(sp, DN - 1)
            sp.wait_ge(out_stored, 16 * DN)

        @block.tensor
        def _(pe):
            def rebuild(j, u, place):
                if place is None:
                    return
                kind, k = place
                if kind == "g":
                    n, w, s_u = first_round(j + 1, "g") + k, width(j + 1), 1 - u
                    if k == 0:
                        slot_load = gu_loaded[s_u]
                        pe.wait_ge(slot_load, 48 * ((j + 1 - s_u) // 2 + 1))
                    if not isinstance(n, int) or n >= 1:
                        pe.wait_ge(wf_done, n)
                    for b in range(2):
                        rows = sel_gu[0:R_GU, :].rearrange("g (p s) -> g s p", s=KT)[:, 2 * k + b, :]
                        for src, dst in ((zt, z_ps), (st, s_ps)):
                            last = pe.matmul(dst[:, b * 2 * P:b * 2 * P + 2 * w], rows, src[:, s_u, :, 0:w],
                                             start=True, stop=True)
                else:
                    n, w = first_round(j, "d") + k, width(j)
                    pe.wait_ge(wf_done, n)
                    if k == 0:
                        pe.wait_ge(sel_done, j + 1)
                    for src, dst in ((zd, z_ps), (scd, s_ps)):
                        last = pe.matmul(dst[0:w, :], sel[:, u, 0:w], src[0:R_D, k * BANK:(k + 1) * BANK],
                                         start=True, stop=True)
                last.then_inc(zs_ready, 1)

            def gate_up(j, u):
                w = width(j)
                for t in range(TC):
                    e = TC * j + t
                    if t == 0:
                        pe.wait_ge(whi_done, first_round(j, "g") + ROUNDS)
                        pe.wait_ge(wlo_done, first_round(j, "g") + ROUNDS)
                    if not isinstance(j, int) or e >= 2:
                        pe.wait_ge(h_done, e - 1)
                    for s in range(KT):
                        if s % (KT // 2) == 0:
                            rebuild(j, u, places(j)[2 * t + s // (KT // 2)])
                        for k, (wp, xp) in enumerate([(0, 0), (0, 1), (1, 0)]):
                            for g, ps in ((0, gate_ps), (1, up_ps)):
                                last = pe.matmul(ps[t % 2][0:w, :], wg[:, u, wp, s, g * w:(g + 1) * w],
                                                 xT[:, xp, s, t * BANK:(t + 1) * BANK],
                                                 start=(s == 0 and k == 0), stop=(s == KT - 1 and k == 2))
                    last.then_inc(gu_ready, 1)

            def down(c):
                j = CHUNK * c + CHUNK - 1
                pe.wait_ge(whi_done, first_round(j, "d") + 2)
                pe.wait_ge(wlo_done, first_round(j, "d") + 2)
                for t in range(TT):
                    if t % (TT // TC) == 0:
                        pe.wait_ge(hlo_done, TC * j + t // (TT // TC) + 1)
                        pe.wait_ge(hhi_done, TC * j + t // (TT // TC) + 1)
                    for n in range(2):
                        i = DN * c + 2 * t + n
                        if not isinstance(c, int) or i >= 2:
                            pe.wait_ge(dn_taken, i - 1)
                        for e in range(CHUNK):
                            w = width(CHUNK * c + e)
                            for k, (hp, wp) in enumerate([(0, 0), (0, 1), (1, 0)]):
                                last = pe.matmul(dn_ps[n][:, :], hT[0:w, hp, e, t * P:(t + 1) * P],
                                                 wd[0:w, wp, e, n * BANK:(n + 1) * BANK],
                                                 start=(e == 0 and k == 0), stop=(e == CHUNK - 1 and k == 2))
                        last.then_inc(dn_ready, 1)

            for k in range(ROUNDS):
                rebuild(-1, 1, ("g", k))
            for u in range(2):
                gate_up(u, u)
            down(0)
            with pe.Fori(1, CHUNKS - 1) as c:
                for u in range(2):
                    gate_up(CHUNK * c + u, u)
                down(c)
            for u in range(2):
                gate_up(CHUNK * (CHUNKS - 1) + u, u)
            down(CHUNKS - 1)

        @block.vector
        def _(dve):
            def select(j, u):
                w = width(j)
                steps = [lambda: dve.tensor_scalar(idf[:, 0, 0:w], idx[:, u, 0:w], 0.0, float(G_D),
                                                   ALU.is_lt, ALU.mult),
                         lambda: dve.tensor_tensor(idf[:, 1, 0:w], idf[:, 0, 0:w], idx[:, u, 0:w], ALU.add),
                         lambda: dve.tensor_scalar(idf[:, 0, 0:w], idf[:, 1, 0:w], 0.0, float(G_D - 1),
                                                   ALU.max, ALU.min)]
                dve.wait_ge(idx_loaded[u], 16 * ((j - u) // 2 + 1))
                for k, op in enumerate(steps):
                    op().then_inc(sel_step, 1)
                    dve.wait_ge(sel_step, 3 * j + k + 1)
                dve.tensor_scalar(sel[:, u, 0:w], idf[:, 0, 0:w], lanes[0:R_D, 0:1], None, ALU.is_equal
                                  ).then_inc(sel_done, 1)

            def rebuild(j, u, place):
                if place is None:
                    return
                kind, k = place
                if kind == "g":
                    n, w, s_u = first_round(j + 1, "g") + k, width(j + 1), 1 - u
                    p, view = P, [slice(b * 2 * P, b * 2 * P + 2 * w) for b in range(2)]
                    if k == 0:
                        dve.wait_ge(gu_loaded[s_u], 48 * ((j + 1 - s_u) // 2 + 1))
                    for b in range(2):
                        last = dve.tensor_scalar(nib[:, view[b]].rearrange("p (h f) -> p h f", h=2),
                                                 qwg[:, s_u, :, 0:w], 4 * (2 * k + b), 15,
                                                 ALU.logical_shift_right, ALU.bitwise_and)
                    if w == P:
                        view = [slice(0, BANK)]
                else:
                    n, p, view = first_round(j, "d") + k, width(j), [slice(0, BANK)]
                    dve.wait_ge(dn_loaded[k], 16 * (j + 1))
                    last = dve.tensor_scalar(nib[0:p, :], qwd[0:p, k, :], lanes[0:p, 1:2].bitcast(U32), 15,
                                             ALU.logical_shift_right, ALU.bitwise_and)
                last.then_inc(nib_done, 1)
                dve.wait_ge(zs_ready, n + 1)
                dve.wait_ge(nib_done, n + 1)
                for v in view:
                    last = dve.tensor_tensor(dif[0:p, v], nib[0:p, v], z_ps[0:p, v], ALU.subtract)
                last.then_inc(dif_done, 1)
                dve.wait_ge(dif_done, n + 1)
                if not isinstance(n, int) or n >= 2:
                    dve.wait_ge(wlo_done, n - 1)
                for v in view:
                    last = dve.tensor_tensor(wf[0:p, k % 2, v], dif[0:p, v], s_ps[0:p, v], ALU.mult)
                last.then_inc(wf_done, 1)

            def gated(j, t):
                w, e = width(j), TC * j + t
                dve.wait_ge(silu_done, e + 1)
                dve.scalar_tensor_tensor(h[0:w, t % 2, :], up_ps[t % 2][0:w, :], H_SCALE / W_SCALE,
                                         h[0:w, t % 2, :], ALU.mult, ALU.mult).then_inc(h_done, 1)

            def tile(j, u):
                select(j, u)
                for t in range(TC):
                    for half in range(2):
                        rebuild(j, u, places(j)[2 * t + half])
                    gated(j, t)

            def add(c, t, n):
                i = DN * c + 2 * t + n
                cols = slice(n * BANK, (n + 1) * BANK)
                dve.wait_ge(dn_ready, i + 1)
                dve.tensor_tensor(acc[:, t, cols], acc[:, t, cols], dn_ps[n][:, :], ALU.add).then_inc(dn_taken, 1)

            def weigh(k):
                t, n, u = k // 2, k % 2, k % 2
                cols = slice(n * BANK, (n + 1) * BANK)
                dve.wait_ge(g_done, k + 1)
                dve.wait_ge(xs_loaded[u], 32 * (k // 2 + 1))
                dve.tensor_tensor(acc[:, t, cols], acc[:, t, cols], s_in[:, u, :], ALU.mult).then_inc(prod_done, 1)

            for k in range(ROUNDS):
                rebuild(-1, 1, ("g", k))
            for u in range(2):
                tile(u, u)
            dve.wait_ge(acc_zeroed, 1)
            for k in range(DN):
                add(0, k // 2, k % 2)
            with dve.Fori(1, CHUNKS - 1) as c:
                for u in range(2):
                    tile(CHUNK * c + u, u)
                dve.wait_ge(dn_taken, DN * c)
                for k in range(DN):
                    add(c, k // 2, k % 2)
            for u in range(2):
                tile(CHUNK * (CHUNKS - 1) + u, u)
            dve.wait_ge(dn_taken, DN * (CHUNKS - 1))
            for k in range(DN + 2):
                if k < DN:
                    add(CHUNKS - 1, k // 2, k % 2)
                if k >= 2:
                    weigh(k - 2)

        @block.scalar
        def _(act):
            def high(j, u, place):
                if place is None:
                    return
                kind, k = place
                if kind == "g":
                    n, w = first_round(j + 1, "g") + k, width(j + 1)
                    act.wait_ge(wf_done, n + 1)
                    act.activation(wg[:, 1 - u, 0, 2 * k:2 * k + 2, 0:2 * w],
                                   wf[:, k % 2, :].rearrange("p (s f) -> p s f", s=2)[:, :, 0:2 * w],
                                   ACT.Copy).then_inc(whi_done, 1)
                else:
                    n, w = first_round(j, "d") + k, width(j)
                    act.wait_ge(wf_done, n + 1)
                    act.activation(wd[0:w, 0, u, k * BANK:(k + 1) * BANK], wf[0:w, k % 2, :],
                                   ACT.Copy).then_inc(whi_done, 1)

            def gated(j, u, t):
                w, e = width(j), TC * j + t
                act.wait_ge(gu_ready, e + 1)
                if not isinstance(e, int) or e >= 2:
                    act.wait_ge(hlo_done, e - 1)
                act.activation(h[0:w, t % 2, :], gate_ps[t % 2][0:w, :], ACT.Silu, scale=1.0 / W_SCALE
                               ).then_inc(silu_done, 1)
                act.wait_ge(h_done, e + 1)
                act.activation(hT[0:w, 0, u, t * BANK:(t + 1) * BANK], h[0:w, t % 2, :], ACT.Copy
                               ).then_inc(hhi_done, 1)

            def tile(j, u):
                for t in range(TC):
                    for half in range(2):
                        high(j, u, places(j)[2 * t + half])
                    gated(j, u, t)

            for k in range(ROUNDS):
                high(-1, 1, ("g", k))
            for u in range(2):
                tile(u, u)
            with act.Fori(1, CHUNKS - 1) as c:
                for u in range(2):
                    tile(CHUNK * c + u, u)
            for u in range(2):
                tile(CHUNK * (CHUNKS - 1) + u, u)
            for k in range(DN):
                t, n = k // 2, k % 2
                cols = slice(n * BANK, (n + 1) * BANK)
                act.wait_ge(dn_taken, DN * (CHUNKS - 1) + k + 1)
                act.activation(acc[:, t, cols], acc[:, t, cols], ACT.Silu, scale=1.0 / (W_SCALE * H_SCALE)
                               ).then_inc(g_done, 1)

        @block.gpsimd
        def _(pool):
            def low(j, u, place):
                if place is None:
                    return
                kind, k = place
                if kind == "g":
                    n, w = first_round(j + 1, "g") + k, width(j + 1)
                    s = slice(2 * k, 2 * k + 2)
                    pool.wait_ge(whi_done, n + 1)
                    pool.tensor_tensor(wg[:, 1 - u, 1, s, 0:2 * w],
                                       wf[:, k % 2, :].rearrange("p (s f) -> p s f", s=2)[:, :, 0:2 * w],
                                       wg[:, 1 - u, 0, s, 0:2 * w], ALU.subtract).then_inc(wlo_done, 1)
                else:
                    n, w = first_round(j, "d") + k, width(j)
                    cols = slice(k * BANK, (k + 1) * BANK)
                    pool.wait_ge(whi_done, n + 1)
                    pool.tensor_tensor(wd[0:w, 1, u, cols], wf[0:w, k % 2, :], wd[0:w, 0, u, cols],
                                       ALU.subtract).then_inc(wlo_done, 1)

            def gated(j, u, t):
                w, e = width(j), TC * j + t
                cols = slice(t * BANK, (t + 1) * BANK)
                pool.wait_ge(hhi_done, e + 1)
                pool.tensor_tensor(hT[0:w, 1, u, cols], h[0:w, t % 2, :], hT[0:w, 0, u, cols],
                                   ALU.subtract).then_inc(hlo_done, 1)

            def tile(j, u):
                for t in range(TC):
                    for half in range(2):
                        low(j, u, places(j)[2 * t + half])
                    gated(j, u, t)

            pool.memset(acc[:, :, :], 0.0).then_inc(acc_zeroed, 1)
            for k in range(ROUNDS):
                low(-1, 1, ("g", k))
            for u in range(2):
                tile(u, u)
            with pool.Fori(1, CHUNKS - 1) as c:
                for u in range(2):
                    tile(CHUNK * c + u, u)
            for u in range(2):
                tile(CHUNK * (CHUNKS - 1) + u, u)
            for k in range(DN):
                t, n, u = k // 2, k % 2, k % 2
                cols = slice(n * BANK, (n + 1) * BANK)
                pool.wait_ge(prod_done, k + 1)
                pool.tensor_tensor(acc[:, t, cols], acc[:, t, cols], x_in[:, u, :], ALU.add).then_inc(sum_done, 1)


def build(nc, x, wq, wk, wv, wo, qw_gu, qz_gu, sc_gu, gi_gu, qw_d, qz_d, sc_dn, gi_d, rope, lanes_in, out):
    qk_d = nc.dram_tensor("qk_scratch", (B, KV, P, ST, (REP + 1) * STACK), F16, kind="Internal").ap()
    v_d = nc.dram_tensor("v_scratch", (B, KV, P, ST, VW), F16, kind="Internal").ap()
    o_d = nc.dram_tensor("o_scratch", (B, KV, P, ST, REP * HD), F32, kind="Internal").ap()
    s_d = nc.dram_tensor("s_scratch", (T, D), F32, kind="Internal").ap()
    sc_d = nc.dram_tensor("scale_scratch", (64 + G_GU, 2 * INTER), BF16, kind="Internal").ap()
    z_d = nc.dram_tensor("zero_scratch", (64 + G_GU, 2 * INTER), BF16, kind="Internal").ap()
    with ExitStack() as ctx:
        def sb(name, shape, dt):
            return ctx.enter_context(nc.sbuf_tensor(name, shape, dt))

        xT = sb("xT", [P, 2, KT, T], F16)
        ident = sb("ident", [P, P], F16)
        identb = sb("identb", [P, P], BF16)
        maskb = sb("maskb", [P, P], BF16)
        project_qkv(nc, x, wq, wk, wv, rope, qk_d, v_d, xT, ident, identb, maskb)
        lanes = sb("lanes", [P, 2], I32)
        scd = sb("scd", [64 + G_D, D], BF16)
        zd = sb("zd", [64 + G_D, D], BF16)
        sel_gu = sb("sel_gu", [64 + G_GU, D], BF16)
        with ExitStack() as both:
            o = both.enter_context(nc.sbuf_tensor("o", [P, 2, ST, REP * HD], F32))
            a = both.enter_context(nc.sbuf_tensor("a", [P, 2, D], F32))
            w_in = both.enter_context(nc.sbuf_tensor("wo_in", [P, STAGE, D], F32))
            o_stored = [both.enter_context(nc.semaphore(f"o_stored{i}")) for i in range(2)]
            a_loaded = [both.enter_context(nc.semaphore(f"a_loaded{i}")) for i in range(2)]
            w_loaded = [both.enter_context(nc.semaphore(f"wo_loaded{i}")) for i in range(STAGE)]
            attend(nc, qk_d, v_d, o_d, wo, ident, identb, maskb, o, o_stored, a, a_loaded, w_in, w_loaded)
            project_out(nc, o_d, wo, s_d, ident, o_stored, a, a_loaded, w_in, w_loaded, lanes_in, sc_gu, qz_gu,
                        sc_dn, qz_d, gi_gu, lanes, sc_d, z_d, scd, zd, sel_gu)
        feed_forward(nc, x, qw_gu, qw_d, gi_d, lanes, sc_d, z_d, scd, zd, sel_gu, xT, s_d, out)


def rope_table():
    f32 = np.float32
    freqs = (f32(1.0) / np.power(f32(THETA), np.arange(0, HD, 2, dtype=f32) / f32(HD))).astype(f32)
    ang = np.outer(np.arange(S, dtype=f32), freqs).astype(f32)
    both = np.stack([np.cos(ang), np.sin(ang)], axis=1).astype(f32) / f32(W_SCALE)
    both = np.tile(both.reshape(ST, P, 2, HALF), (B, 1, 1, 1))
    return np.ascontiguousarray(both.transpose(1, 0, 2, 3).reshape(P, -1))


def lane_table():
    p = np.arange(P)
    return np.stack([p % 32, 4 * (p % NIB)], axis=1).astype(np.int32)


def kernel(L0_attn_x, L0_attn_wq, L0_attn_wk, L0_attn_wv, L0_attn_wo, L0_ffn_qweight_gu, L0_ffn_qzeros_gu,
           L0_ffn_scales_gu, L0_ffn_g_idx_gu, L0_ffn_qweight_down, L0_ffn_qzeros_down, L0_ffn_scales_down,
           L0_ffn_g_idx_down):
    import concourse.bacc as bacc
    from concourse.bass_utils import run_bass_kernel_spmd

    given = {"x": L0_attn_x, "wq": L0_attn_wq, "wk": L0_attn_wk, "wv": L0_attn_wv, "wo": L0_attn_wo,
             "qw_gu": L0_ffn_qweight_gu, "qz_gu": L0_ffn_qzeros_gu, "sc_gu": L0_ffn_scales_gu,
             "gi_gu": L0_ffn_g_idx_gu, "qw_d": L0_ffn_qweight_down, "qz_d": L0_ffn_qzeros_down,
             "sc_dn": L0_ffn_scales_down, "gi_d": L0_ffn_g_idx_down, "rope": rope_table(), "lanes": lane_table()}
    nc = bacc.Bacc("TRN2", target_bir_lowering=False, num_devices=1)
    arrays, args = {}, []
    for name, a in given.items():
        a = np.ascontiguousarray(a)
        arrays[f"in_{name}"] = a
        args.append(nc.dram_tensor(f"in_{name}", a.shape, mybir.dt.from_np(a.dtype), kind="ExternalInput").ap())
    out = nc.dram_tensor("out", (B, S, D), F32, kind="ExternalOutput").ap()
    build(nc, *args, out)
    r = run_bass_kernel_spmd(nc, [arrays], core_ids=[0])
    return r.results[0]["out"]
```

```python
from contextlib import ExitStack

import numpy as np

import concourse.bass as bass
from concourse import mybir

ALU = mybir.AluOpType
ACT = mybir.ActivationFunctionType
AX_X = mybir.AxisListType.X
F32 = mybir.dt.float32
F16 = mybir.dt.float16
BF16 = mybir.dt.bfloat16
I32 = mybir.dt.int32
U32 = mybir.dt.uint32

P = 128
B, S, D = 2, 1024, 1024
T = B * S
TT = T // P
ST = S // P
KT = D // P
HEADS, KV, HD = 32, 8, 32
REP = HEADS // KV
GROUPS = B * KV
QKV = (HEADS + 2 * KV) * HD
QK = HEADS + KV
HALF = HD // 2
STACK = 3 * HD
VH = HD + 1
VW = VH + HD
EPS = 1e-5
THETA = 10000.0
BANK = 512
FULL = 1024

INTER = 2752
G_GU, G_D = 8, 21
NIB = 8
HALF_NIB = NIB // 2
FTILES = (INTER + P - 1) // P
FLAST = INTER - (FTILES - 1) * P
CHUNK = 2
CHUNKS = FTILES // CHUNK
TC = T // BANK
STAGE = 4

W_SCALE = 64.0
H_SCALE = 1.0 / 16.0
MASKED = -1e30


def at(m, u, off, unroll=2):
    k = u + off
    return m + k // unroll, k % unroll


def inside(m, u, n, unroll=2):
    return not isinstance(m, int) or 0 <= unroll * m + u < n


def wait_alone(eng, sem, count, seen):
    eng.wait_ge(sem, count)
    eng.sem_inc(seen, 1)


def make_masks(pool, ident, identb, maskb, zeros_done, masks_done):
    pool.memset(ident[:, :], 1.0)
    pool.memset(identb[:, :], 1.0)
    pool.memset(maskb[:, :], 0.0).then_inc(zeros_done, 1)
    pool.wait_ge(zeros_done, 1)
    pool.affine_select(out=ident[:, :], in_=ident[:, :], pattern=[[-1, P]], compare_op=ALU.is_equal,
                       fill=0.0, base=0, channel_multiplier=1)
    pool.affine_select(out=identb[:, :], in_=identb[:, :], pattern=[[-1, P]], compare_op=ALU.is_equal,
                       fill=0.0, base=0, channel_multiplier=1)
    pool.affine_select(out=maskb[:, :], in_=maskb[:, :], pattern=[[-1, P]], compare_op=ALU.is_ge,
                       fill=MASKED, base=0, channel_multiplier=1).then_inc(masks_done, 1)


def load_heads(eng, qk_d, qkn, qk_loaded, g, u):
    eng.dma_start(qkn[:, u, :, :], qk_d.rearrange("b g p t c -> (b g) p t c")[g]).then_inc(qk_loaded[u], 16)


def load_values(eng, v_d, vn, v_loaded, g, u):
    eng.dma_start(vn[:, u, :, :], v_d.rearrange("b g p t c -> (b g) p t c")[g]).then_inc(v_loaded[u], 16)


def project_qkv(nc, x, wq, wk, wv, rope, qk_d, v_d, xT, ident, identb, maskb, qkn, qk_loaded, vn, v_loaded):
    with ExitStack() as ctx:
        def sb(name, shape, dt):
            return ctx.enter_context(nc.sbuf_tensor(name, shape, dt))

        def sem(name):
            return ctx.enter_context(nc.semaphore(name))

        xin = sb("xin", [P, 2, D], F32)
        xn = sb("xn", [P, 2, D], F32)
        xh = sb("xh", [P, 2, D], F16)
        xl = sb("xl", [P, 2, D], F16)
        bn = sb("bn", [P, 2, 6], F32)
        mv = sb("mv", [P, 2, 2], F32)
        std = sb("std", [P, 2, 1], F32)
        rstd = sb("rstd", [P, 2, 1], F32)
        eps = sb("eps", [P, 1], F32)
        xTc = sb("xTc", [P, 2, 2, KT, P], F16)
        w_in = sb("w_in", [P, STAGE, QKV], F32)
        w = sb("w", [P, 2, KT, QKV], F16)
        cs = sb("cs", [P, TT, 2, HALF], F32)
        staged = w_in[:, :, :].rearrange("p s n -> p (s n)")
        rot_t = staged[:, 0:4 * QK * HALF].rearrange("p (k h f) -> p k h f", k=4, h=QK)
        rot = staged[:, 4 * QK * HALF:6 * QK * HALF].rearrange("p (h c f) -> p h c f", h=QK, c=2)
        stack = sb("stack", [P, 2, QK, STACK], F16)
        v = sb("v", [P, 2, KV, VW], F16)
        qkv_ps = [ctx.enter_context(nc.psum_tensor(f"qkv_ps{i}", [P, QKV], F32)) for i in range(2)]
        tr_ps = [ctx.enter_context(nc.psum_tensor(f"tr_ps{i}", [P, KT, P], F16)) for i in range(2)]

        x_loaded = [sem(f"x_loaded{i}") for i in range(2)]
        w_loaded = [sem(f"w_loaded{i}") for i in range(STAGE)]
        cs_loaded = sem("cs_loaded")
        whi_done = sem("whi_done")
        wlo_done = sem("wlo_done")
        zeros_done = sem("zeros_done")
        masks_done = sem("masks_done")
        ones_set = sem("ones_set")
        eps_set = sem("eps_set")
        bn_done = sem("bn_done")
        bn_seen = sem("bn_seen")
        mv_done = sem("mv_done")
        std_done = sem("std_done")
        rstd_done = sem("rstd_done")
        xn_done = sem("xn_done")
        xh_done = sem("xh_done")
        xl_done = sem("xl_done")
        xh_turned = sem("xh_turned")
        xl_turned = sem("xl_turned")
        xTh_done = sem("xTh_done")
        xTl_done = sem("xTl_done")
        xT_kept = sem("xT_kept")
        qkv_done = sem("qkv_done")
        mult_done = sem("mult_done")
        rot_done = sem("rot_done")
        v_done = sem("v_done")
        vlo_done = sem("vlo_done")
        hi_done = sem("hi_done")
        lo_done = sem("lo_done")
        stored = [sem(f"stored{i}") for i in range(2)]
        qk_v = qk_d.rearrange("b g p t c -> b t p g c")
        v_v = v_d.rearrange("b g p t c -> b t p g c")

        w_parts = [(wq.rearrange("(p s) n -> p s n", s=KT), 0, HEADS * HD),
                   (wk.rearrange("(p s) n -> p s n", s=KT), HEADS * HD, KV * HD),
                   (wv.rearrange("(p s) n -> p s n", s=KT), QK * HD, KV * HD)]
        x_v = x.rearrange("b (t p) d -> (b t) p d", p=P)

        block = ctx.enter_context(nc.Block())

        @block.sync
        def _(sp):
            def load_x(m, u):
                if not inside(m, u, TT):
                    return
                if not isinstance(m, int) or m >= 1:
                    sp.wait_ge(xn_done, 2 * m + u - 1)
                sp.dma_start(xin[:, u, :], x_v[2 * m + u]).then_inc(x_loaded[u], 16)

            load_x(0, 0)
            load_x(0, 1)
            for s in range(KT):
                if s >= STAGE:
                    sp.wait_ge(wlo_done, s - STAGE + 1)
                for w_dram, c0, n in w_parts:
                    sp.dma_start(w_in[:, s % STAGE, c0:c0 + n], w_dram[:, s, :]).then_inc(w_loaded[s % STAGE], 16)
                if s >= KT - 2:
                    load_x(1, s - KT + 2)
            sp.dma_start(cs[:, :, :, :], rope.rearrange("p (t c f) -> p t c f", t=TT, c=2)).then_inc(cs_loaded, 16)

            def step(b, m, u):
                n = b * ST + 2 * m + u
                sp.wait_ge(lo_done, n + 1)
                sp.wait_ge(hi_done, n + 1)
                sp.wait_ge(vlo_done, n + 1)
                sp.dma_start(qk_v[b, 2 * m + u, :, :, 0:REP * STACK],
                             stack[:, u, 0:HEADS, :].rearrange("p (g r) c -> p g (r c)", r=REP)
                             ).then_inc(stored[u], 16)
                sp.dma_start(qk_v[b, 2 * m + u, :, :, REP * STACK:],
                             stack[:, u, HEADS:QK, :]).then_inc(stored[u], 16)
                sp.dma_start(v_v[b, 2 * m + u], v[:, u, :, :]).then_inc(stored[u], 16)

            half = ST // 2
            with sp.Fori(0, half) as m:
                for u in range(2):
                    load_x(m + 2, u)
                    step(0, m, u)
            with sp.Fori(0, half - 2) as m:
                for u in range(2):
                    load_x(m + 2 + half, u)
                    step(1, m, u)
            for u in range(2):
                sp.wait_ge(stored[u], 16 * 3 * (TT // 2 - 2))
            for g in range(2):
                load_heads(sp, qk_d, qkn, qk_loaded, g, g)
                load_values(sp, v_d, vn, v_loaded, g, g)
            for m in range(half - 2, half):
                for u in range(2):
                    step(1, m, u)
            for u in range(2):
                sp.wait_ge(stored[u], 16 * 3 * TT // 2)

        @block.gpsimd
        def _(pool):
            pool.memset(v[:, :, :, HD:VH], 1.0).then_inc(ones_set, 1)
            make_masks(pool, ident, identb, maskb, zeros_done, masks_done)

            def low(m, u):
                if not inside(m, u, TT):
                    return
                n = 2 * m + u
                pool.wait_ge(xh_done, n + 1)
                if not isinstance(m, int) or m >= 1:
                    pool.wait_ge(xl_turned, n - 1)
                pool.tensor_tensor(xl[:, u, :], xn[:, u, :], xh[:, u, :], ALU.subtract).then_inc(xl_done, 1)

            def keep(m, u):
                if not inside(m, u, TT):
                    return
                n = 2 * m + u
                pool.wait_ge(xTh_done, n + 1)
                pool.wait_ge(xTl_done, n + 1)
                for part in range(2):
                    last = pool.tensor_copy(xT[:, part, :, bass.ds(n * P, P)], xTc[:, u, part, :, :])
                last.then_inc(xT_kept, 1)

            def step(m, u):
                low(*at(m, u, 2))
                keep(*at(m, u, 1))

            for m in range(2):
                low(m, 0)
                low(m, 1)
                if m == 0:
                    keep(0, 0)
                    keep(0, 1)
            keep(1, 0)
            with pool.Fori(1, TT // 2 - 1) as m:
                step(m, 0)
                step(m, 1)
            step(TT // 2 - 1, 0)
            step(TT // 2 - 1, 1)

        @block.scalar
        def _(act):
            def deviation(m, u):
                n = 2 * m + u
                act.wait_ge(mv_done, n + 1)
                act.activation(std[:, u, :], mv[:, u, 1:2], ACT.Sqrt, bias=eps[:, :]).then_inc(std_done, 1)

            def norm(m, u):
                if not inside(m, u, TT):
                    return
                n = 2 * m + u
                deviation(m, u)
                act.wait_ge(xn_done, n + 1)
                if not isinstance(m, int) or m >= 1:
                    act.wait_ge(xh_turned, n - 1)
                    act.wait_ge(xl_done, n - 1)
                act.activation(xh[:, u, :], xn[:, u, :], ACT.Copy).then_inc(xh_done, 1)

            def turned(m, u):
                if not inside(m, u, TT):
                    return
                n = 2 * m + u
                act.wait_ge(xh_turned, n + 1)
                if not isinstance(m, int) or m >= 1:
                    act.wait_ge(qkv_done, n - 1)
                    act.wait_ge(xT_kept, n - 1)
                act.activation(xTc[:, u, 0, :, :], tr_ps[0][:, :, :], ACT.Copy).then_inc(xTh_done, 1)

            def post(m, u):
                if not inside(m, u, TT):
                    return
                n = 2 * m + u
                act.wait_ge(mult_done, n + 1)
                if not isinstance(m, int) or m >= 1:
                    act.wait_ge(stored[u], 48 * m)
                act.activation(v[:, u, :, 0:HD],
                               qkv_ps[u][:, QK * HD:QKV].rearrange("p (h c) -> p h c", h=KV),
                               ACT.Copy, scale=1.0 / W_SCALE).then_inc(v_done, 1)
                act.wait_ge(rot_done, n + 1)
                full = rot[:, :, :, :].rearrange("p h c f -> p h (c f)").unsqueeze(2)
                parts = stack[:, u, :, :].rearrange("p h (a c) -> p h a c", c=HD)
                act.activation(parts[:, 0:HEADS, 0:2, :], full[:, 0:HEADS, :, :].to_broadcast([P, HEADS, 2, HD]),
                               ACT.Copy)
                act.activation(parts[:, HEADS:QK, 0:3:2, :], full[:, HEADS:QK, :, :].to_broadcast([P, KV, 2, HD]),
                               ACT.Copy).then_inc(hi_done, 1)

            def step(m, u):
                norm(*at(m, u, 2))
                turned(*at(m, u, 1))
                post(m, u)

            act.wait_ge(eps_set, 1)
            act.wait_ge(ones_set, 1)
            norm(0, 0)
            norm(0, 1)
            for s in range(KT):
                act.wait_ge(w_loaded[s % STAGE], 48 * (s // STAGE + 1))
                act.activation(w[:, 0, s, :], w_in[:, s % STAGE, :], ACT.Copy, scale=W_SCALE
                               ).then_inc(whi_done, 1)
                if s < 2:
                    turned(0, s)
                if s >= KT - 2:
                    norm(1, s - KT + 2)
            turned(1, 0)
            post(0, 0)
            post(0, 1)
            with act.Fori(1, TT // 2 - 1) as m:
                step(m, 0)
                step(m, 1)
            step(TT // 2 - 1, 0)
            step(TT // 2 - 1, 1)

        @block.vector
        def _(dve):
            def norm(m, u):
                if not inside(m, u, TT):
                    return
                n = 2 * m + u
                dve.wait_ge(x_loaded[u], 16 * (m + 1))
                for h in range(2):
                    last = dve.bn_stats(bn[:, h, :], xin[:, u, h * BANK:(h + 1) * BANK])
                last.then_inc(bn_done, 1)
                wait_alone(dve, bn_done, n + 1, bn_seen)
                dve.bn_aggr(mv[:, u, :], bn[:, :, :]).then_inc(mv_done, 1)
                dve.wait_ge(std_done, n + 1)
                dve.reciprocal(rstd[:, u, :], std[:, u, :]).then_inc(rstd_done, 1)
                dve.wait_ge(rstd_done, n + 1)
                if not isinstance(m, int) or m >= 1:
                    dve.wait_ge(xl_done, n - 1)
                dve.tensor_scalar(xn[:, u, :], xin[:, u, :], mv[:, u, 0:1], rstd[:, u, :],
                                  ALU.subtract, ALU.mult).then_inc(xn_done, 1)

            def turned(m, u):
                if not inside(m, u, TT):
                    return
                n = 2 * m + u
                dve.wait_ge(xl_turned, n + 1)
                if not isinstance(m, int) or m >= 1:
                    dve.wait_ge(qkv_done, n - 1)
                    dve.wait_ge(xT_kept, n - 1)
                dve.tensor_copy(xTc[:, u, 1, :, :], tr_ps[1][:, :, :]).then_inc(xTl_done, 1)

            def post(m, u):
                if not inside(m, u, TT):
                    return
                n = 2 * m + u
                dve.wait_ge(qkv_done, n + 1)
                pairs = qkv_ps[u][:, 0:QK * HD].rearrange("p (h f c) -> p c h f", h=QK, c=2)
                trig = cs[:, bass.ds(n, 1), :, :].rearrange("p t c f -> p c t f")
                for k, (c, q) in enumerate([(0, 0), (1, 1), (0, 1), (1, 0)]):
                    last = dve.tensor_tensor(rot_t[:, k, :, :], pairs[:, c, :, :],
                                             trig[:, q, :, :].to_broadcast([P, QK, HALF]), ALU.mult)
                last.then_inc(mult_done, 1)
                dve.wait_ge(mult_done, n + 1)
                if not isinstance(m, int) or 2 * m + u >= 1:
                    dve.wait_ge(hi_done, n)
                dve.tensor_tensor(rot[:, :, 0, :], rot_t[:, 0, :, :], rot_t[:, 1, :, :], ALU.subtract)
                dve.tensor_tensor(rot[:, :, 1, :], rot_t[:, 2, :, :], rot_t[:, 3, :, :],
                                  ALU.add).then_inc(rot_done, 1)
                dve.wait_ge(v_done, n + 1)
                dve.scalar_tensor_tensor(v[:, u, :, VH:VW],
                                         qkv_ps[u][:, QK * HD:QKV].rearrange("p (h c) -> p h c", h=KV),
                                         1.0 / W_SCALE, v[:, u, :, 0:HD], ALU.mult, ALU.subtract
                                         ).then_inc(vlo_done, 1)
                dve.wait_ge(hi_done, n + 1)
                full = rot[:, :, :, :].rearrange("p h c f -> p h (c f)")
                dve.tensor_tensor(stack[:, u, 0:HEADS, 2 * HD:STACK], full[:, 0:HEADS, :],
                                  stack[:, u, 0:HEADS, 0:HD], ALU.subtract)
                dve.tensor_tensor(stack[:, u, HEADS:QK, HD:2 * HD], full[:, HEADS:QK, :],
                                  stack[:, u, HEADS:QK, 0:HD], ALU.subtract).then_inc(lo_done, 1)

            def step(m, u):
                norm(*at(m, u, 2))
                turned(*at(m, u, 1))
                post(m, u)

            dve.memset(eps[:, :], EPS).then_inc(eps_set, 1)
            norm(0, 0)
            norm(0, 1)
            for s in range(KT):
                dve.wait_ge(whi_done, s + 1)
                dve.scalar_tensor_tensor(w[:, 1, s, :], w_in[:, s % STAGE, :], W_SCALE, w[:, 0, s, :],
                                         ALU.mult, ALU.subtract).then_inc(wlo_done, 1)
                if s < 2:
                    turned(0, s)
                if s >= KT - 2:
                    norm(1, s - KT + 2)
            turned(1, 0)
            dve.wait_ge(cs_loaded, 16)
            post(0, 0)
            post(0, 1)
            with dve.Fori(1, TT // 2 - 1) as m:
                step(m, 0)
                step(m, 1)
            step(TT // 2 - 1, 0)
            step(TT // 2 - 1, 1)

        @block.tensor
        def _(pe):
            def turn(m, u):
                if not inside(m, u, TT):
                    return
                n = 2 * m + u
                for part, (src, done, free, out) in enumerate([(xh, xh_done, xTh_done, xh_turned),
                                                               (xl, xl_done, xTl_done, xl_turned)]):
                    pe.wait_ge(done, n + 1)
                    if not isinstance(m, int) or n >= 1:
                        pe.wait_ge(free, n)
                    cols = src[:, u, :].rearrange("p (d s) -> p s d", s=KT)
                    for s in range(KT):
                        last = pe.transpose(tr_ps[part][:, s, :], cols[:, s, :], ident[:, :])
                    last.then_inc(out, 1)

            def operands(m, u):
                n = 2 * m + u
                pe.wait_ge(xTh_done, n + 1)
                pe.wait_ge(xTl_done, n + 1)
                if not isinstance(m, int) or m >= 1:
                    pe.wait_ge(vlo_done, n - 1)
                    pe.wait_ge(mult_done, n - 1)

            def contract(u, s):
                for k, (xp, wp) in enumerate([(0, 0), (0, 1), (1, 0)]):
                    for c in range(QKV // BANK):
                        cols = slice(c * BANK, (c + 1) * BANK)
                        last = pe.matmul(qkv_ps[u][:, cols], xTc[:, u, xp, s, :], w[:, wp, s, cols],
                                         start=(s == 0 and k == 0), stop=(s == KT - 1 and k == 2))
                if s == KT - 1:
                    last.then_inc(qkv_done, 1)

            def products(m, u):
                operands(m, u)
                for s in range(KT):
                    contract(u, s)

            pe.wait_ge(masks_done, 1)
            turn(0, 0)
            turn(0, 1)
            operands(0, 0)
            for s in range(KT):
                pe.wait_ge(whi_done, s + 1)
                pe.wait_ge(wlo_done, s + 1)
                contract(0, s)
                if s == KT // 2:
                    operands(0, 1)
                if s >= KT // 2:
                    contract(1, s - KT // 2)
            turn(1, 0)
            for s in range(KT // 2, KT):
                contract(1, s)
            with pe.Fori(1, TT // 2 - 1) as m:
                for u in range(2):
                    turn(*at(m, u, 1))
                    products(m, u)
            turn(TT // 2 - 1, 1)
            products(TT // 2 - 1, 0)
            products(TT // 2 - 1, 1)


def attend(nc, qk_d, v_d, o_d, wo, ident, identb, maskb, qkn, qk_loaded, vn, v_loaded, o, o_stored,
           a, a_loaded, w_in, w_loaded):
    NH = B * HEADS
    R = 2 * REP
    POOL_TILES = [0, 1, 2, 3, 6]
    DVE_TILES = [4, 5, 7]
    TB = BANK // P
    SC = [(t, max(c, t * P), c + BANK) for t in range(ST) for c in range(t * P // BANK * BANK, S, BANK)]
    MX = [(t, c, min(c + BANK, (t + 1) * P)) for t in range(ST) for c in range(0, (t + 1) * P, BANK)]
    NC = len(SC)
    SC_BANKS, MX_BANKS = 3, 3
    WIDE = BANK // VW
    START = [sum(S - k * P for k in range(t)) - t * P for t in range(ST)]
    COLS = START[-1] + S
    OW = WIDE * VW + (ST - WIDE) * VH
    with ExitStack() as ctx:
        def sb(name, shape, dt):
            return ctx.enter_context(nc.sbuf_tensor(name, shape, dt))

        def sem(name):
            return ctx.enter_context(nc.semaphore(name))

        qT = sb("qT", [P, REP, S], F16)
        kT = sb("kT", [P, 2, S], F16)
        probs = sb("probs", [P, 2, COLS], F32)
        p_hi = probs[:, :, :].bitcast(BF16).rearrange("p u (s c) -> p u s c", c=2)[:, :, :, 1]
        p_lo = sb("p_lo", [P, 2, COLS], F16)
        shift = sb("shift", [P, 2, ST], F16)
        part = sb("part", [P, 2, ST - TB], F16)
        sums = sb("sums", [P, 2, ST * VW], F32)
        rsum = sb("rsum", [P, ST], F32)
        sc_ps = [ctx.enter_context(nc.psum_tensor(f"sc_ps{i}", [P, BANK], F32)) for i in range(SC_BANKS)]
        mx_ps = [ctx.enter_context(nc.psum_tensor(f"mx_ps{i}", [P, BANK], F32)) for i in range(MX_BANKS)]
        o_ps = ctx.enter_context(nc.psum_tensor("o_ps", [P, BANK], F32))
        tr_ps = ctx.enter_context(nc.psum_tensor("tr_ps", [P, S], F16))

        ones_set = sem("ones_set_a")
        zeros_set = sem("zeros_set_a")
        k_done = sem("k_done")
        q_done = sem("q_done")
        mx_ready = sem("mx_ready")
        mx_taken = sem("mx_taken")
        shift_turned = sem("shift_turned")
        shift_done = sem("shift_done")
        q_turned = sem("q_turned")
        k_turned = sem("k_turned")
        sc_ready = sem("sc_ready")
        exp_done = sem("exp_done")
        lo_pool = sem("lo_pool")
        lo_dve = sem("lo_dve")
        p_used = sem("p_used")
        o_copied = sem("o_copied")
        shift_ready = sem("shift_ready")
        rsum_done = sem("rsum_done")
        o_added = sem("o_added")
        o_done = sem("o_done")

        block = ctx.enter_context(nc.Block())

        def head(m, r):
            return R * m + r

        def low(eng, m, r, t, done):
            if not exists(m, r):
                return
            eng.wait_ge(exp_done, NC * head(m, r) + chunks_to(t))
            c = slice(START[t] + t * P, START[t] + S)
            eng.tensor_tensor(p_lo[:, r % 2, c], probs[:, r % 2, c], p_hi[:, r % 2, c], ALU.subtract
                              ).then_inc(done, 1)

        def chunks_to(t):
            return sum(c[0] <= t for c in SC)

        def exists(m, r):
            return inside(m, r, NH, R)

        def steps(eng, step):
            for r in range(-3, 0):
                step(*at(0, 0, r, R))
            for r in range(R):
                step(0, r)
            with eng.Fori(1, NH // R - 1) as m:
                for r in range(R):
                    step(m, r)
            for r in range(R + 2):
                step(*at(NH // R - 1, 0, r, R))

        @block.sync
        def _(sp):
            def store(g, u):
                sp.wait_ge(o_done, REP * (g + 1))
                sp.dma_start(o_d.rearrange("b g p t c -> (b g) p t c")[g], o[:, u, :, :]
                             ).then_inc(o_stored[u], 16)

            with sp.Fori(0, GROUPS // 2 - 1) as m:
                for u in range(2):
                    g = 2 * m + u
                    sp.wait_ge(q_turned, REP * (g + 1))
                    load_heads(sp, qk_d, qkn, qk_loaded, g + 2, u)
                    sp.wait_ge(p_used, ST * REP * (g + 1))
                    load_values(sp, v_d, vn, v_loaded, g + 2, u)
                    store(g, u)
            for u in range(2):
                sp.wait_ge(o_stored[u], 16 * KV // 2)
            for u in range(2):
                load_attended(sp, o_d, a, a_loaded, 0, 0, u)
            for s in range(STAGE):
                load_wo(sp, wo, w_in, w_loaded, s)
            for u in range(2):
                store(GROUPS - 2 + u, u)

        @block.tensor
        def _(pe):
            def turn_key(m, r):
                if r % REP or not exists(m, r):
                    return
                h, u = head(m, r), r // REP
                if not isinstance(m, int) or h >= 2:
                    pe.wait_ge(shift_done, h - 1)
                pe.wait_ge(qk_loaded[u], 16 * (m + 1))
                for t in range(ST):
                    last = pe.transpose(tr_ps[0:STACK, t * P:(t + 1) * P],
                                        qkn[:, u, t, REP * STACK:], ident[:, :])
                last.then_inc(k_turned, 1)

            def turn(m, r):
                if not exists(m, r):
                    return
                h, u, q = head(m, r), r // REP, r % REP
                if q == 0:
                    pe.wait_ge(k_done, 2 * m + u + 1)
                elif not isinstance(m, int) or h >= 2:
                    pe.wait_ge(shift_done, h - 1)
                else:
                    pe.wait_ge(q_done, h)
                for t in range(ST):
                    last = pe.transpose(tr_ps[0:STACK, t * P:(t + 1) * P],
                                        qkn[:, u, t, q * STACK:(q + 1) * STACK], ident[:, :])
                last.then_inc(q_turned, 1)

            def turn_shifts(m, r):
                if not exists(m, r):
                    return
                h = head(m, r)
                pe.wait_ge(shift_ready, h + 1)
                pe.wait_ge(q_done, min(h + 2, NH) if isinstance(m, int) else h + 2)
                for t in range(ST):
                    last = pe.transpose(tr_ps[STACK:STACK + 1, t * P:(t + 1) * P], shift[:, r % 2, t:t + 1],
                                        ident[:, :])
                last.then_inc(shift_turned, 1)

            def maxima(m, r, slot):
                if not exists(m, r):
                    return
                h, u, q = head(m, r), r // REP, r % REP
                if slot == 0:
                    pe.wait_ge(q_done, h + 1)
                    pe.wait_ge(k_done, 2 * m + u + 1)
                for i, (t, c, e) in enumerate(MX):
                    if t != slot:
                        continue
                    if not isinstance(m, int) or NC * h + i >= MX_BANKS:
                        pe.wait_ge(mx_taken, NC * h + i + 1 - MX_BANKS)
                    bank = mx_ps[i % MX_BANKS]
                    last = pe.matmul(bank[:, 0:e - c], qT[0:STACK, q, t * P:(t + 1) * P], kT[0:STACK, u, c:e],
                                     start=True, stop=(e <= t * P))
                    if e > t * P:
                        last = pe.matmul(bank[:, t * P - c:e - c], identb[:, :], maskb[:, :],
                                         start=False, stop=True)
                    last.then_inc(mx_ready, 1)

            def scores(m, r, slot):
                if not exists(m, r):
                    return
                h, u, q = head(m, r), r // REP, r % REP
                if slot == 0:
                    pe.wait_ge(shift_done, h + 1)
                for i, (t, c, e) in enumerate(SC):
                    if t != slot:
                        continue
                    if not isinstance(m, int) or NC * h + i >= SC_BANKS:
                        pe.wait_ge(exp_done, NC * h + i + 1 - SC_BANKS)
                    bank = sc_ps[i % SC_BANKS]
                    last = pe.matmul(bank[:, 0:e - c], kT[0:STACK + 1, u, t * P:(t + 1) * P],
                                     qT[0:STACK + 1, q, c:e], start=True, stop=(c > t * P))
                    if c == t * P:
                        last = pe.matmul(bank[:, 0:P], maskb[:, :], identb[:, :], start=False, stop=True)
                    last.then_inc(sc_ready, 1)

            def outputs(m, r, k):
                if not exists(m, r):
                    return
                h, u = head(m, r), r // REP
                if k == 0:
                    if r % REP == 0:
                        pe.wait_ge(v_loaded[u], 16 * (m + 1))
                    if not isinstance(m, int) or h >= 1:
                        pe.wait_ge(o_copied, h)
                if k in POOL_TILES:
                    pe.wait_ge(lo_pool, len(POOL_TILES) * h + POOL_TILES.index(k) + 1)
                else:
                    pe.wait_ge(lo_dve, len(DVE_TILES) * h + DVE_TILES.index(k) + 1)
                for t in range(k, ST):
                    q = slice(START[k] + t * P, START[k] + (t + 1) * P)
                    hi, lo = p_hi[:, r % 2, q], p_lo[:, r % 2, q]
                    c = min(t, WIDE) * VW + max(t - WIDE, 0) * VH
                    if t < WIDE:
                        pe.matmul(o_ps[:, c:c + VW], hi, vn[:, u, k, :], start=(k + t == 0), stop=False)
                    else:
                        pe.matmul(o_ps[:, c:c + VH], hi, vn[:, u, k, 0:VH], start=False, stop=False)
                        pe.matmul(o_ps[:, c:c + HD], hi, vn[:, u, k, VH:VW], start=False, stop=False)
                    last = pe.matmul(o_ps[:, c:c + VH], lo, vn[:, u, k, 0:VH], start=False,
                                     stop=(k == ST - 1))
                last.then_inc(p_used, 1)

            pe.wait_ge(ones_set, 1)

            def step(m, r):
                for t in range(ST):
                    scores(m, r, t)
                    maxima(*at(m, r, 2, R), t)
                    if t == 1:
                        turn_shifts(*at(m, r, 1, R))
                        outputs(*at(m, r, -1, R), 0)
                    if t == 4:
                        turn_key(*at(m, r, 3, R))
                    if t == 6:
                        turn(*at(m, r, 3, R))
                    if t >= 1:
                        outputs(*at(m, r, -1, R), t)

            steps(pe, step)

        @block.scalar
        def _(act):
            def key(m, r):
                if r % REP or not exists(m, r):
                    return
                h, u = head(m, r), r // REP
                act.wait_ge(k_turned, 2 * m + u + 1)
                if not isinstance(m, int) or m >= 1:
                    act.wait_ge(sc_ready, NC * (h - REP))
                act.activation(kT[0:STACK, u, :], tr_ps[0:STACK, :], ACT.Copy).then_inc(k_done, 1)

            def queries(m, r):
                if not exists(m, r):
                    return
                h = head(m, r)
                act.wait_ge(q_turned, h + 1)
                if not isinstance(m, int) or h >= REP:
                    act.wait_ge(sc_ready, NC * (h - REP + 1))
                act.activation(qT[0:STACK, r % REP, :], tr_ps[0:STACK, :], ACT.Copy).then_inc(q_done, 1)

            def exps(m, r, slot):
                if not exists(m, r):
                    return
                h = head(m, r)
                if not isinstance(m, int) or h >= 2:
                    act.wait_ge(p_used, ST * (h - 2) + slot + 1)
                for i, (t, c, e) in enumerate(SC):
                    if t == slot:
                        act.wait_ge(sc_ready, NC * h + i + 1)
                        act.activation(probs[:, r % 2, START[t] + c:START[t] + e],
                                       sc_ps[i % SC_BANKS][:, 0:e - c], ACT.Exp,
                                       scale=float(1.0 / np.sqrt(HD))).then_inc(exp_done, 1)

            def shifts(m, r):
                if not exists(m, r):
                    return
                h = head(m, r)
                act.wait_ge(shift_turned, h + 1)
                act.activation(qT[STACK:STACK + 1, r % REP, :], tr_ps[STACK:STACK + 1, :], ACT.Copy
                               ).then_inc(shift_done, 1)

            def copy_sums(m, r):
                if not exists(m, r):
                    return
                h = head(m, r)
                act.wait_ge(p_used, ST * (h + 1))
                if not isinstance(m, int) or h >= 2:
                    act.wait_ge(o_done, h - 1)
                act.activation(sums[:, r % 2, 0:OW], o_ps[:, 0:OW], ACT.Copy).then_inc(o_copied, 1)

            def step(m, r):
                for t in range(ST):
                    exps(m, r, t)
                    if t == 0:
                        copy_sums(*at(m, r, -2, R))
                    if t == 2:
                        shifts(*at(m, r, 1, R))
                    if t == 4:
                        key(*at(m, r, 3, R))
                    if t == 6:
                        queries(*at(m, r, 3, R))

            steps(act, step)

        @block.vector
        def _(dve):
            dve.memset(kT[STACK:STACK + 1, :, :], 1.0).then_inc(ones_set, 1)
            dve.memset(sums[:, :, OW:], 0.0).then_inc(zeros_set, 1)
            dve.wait_ge(zeros_set, 1)

            def maxima(m, r, slot):
                if not exists(m, r):
                    return
                h = head(m, r)
                for i, (t, c, e) in enumerate(MX):
                    if t != slot:
                        continue
                    dve.wait_ge(mx_ready, NC * h + i + 1)
                    if i == 0 and (not isinstance(m, int) or h >= 2):
                        dve.wait_ge(shift_turned, h - 1)
                    out = shift[:, r % 2, t:t + 1] if t < TB else part[:, c // BANK, t - TB:t - TB + 1]
                    dve.tensor_reduce(out, mx_ps[i % MX_BANKS][:, 0:e - c], AX_X, ALU.max,
                                      negate=True).then_inc(mx_taken, 1)

            def merge(m, r):
                if not exists(m, r):
                    return
                dve.wait_ge(mx_taken, NC * (head(m, r) + 1))
                dve.tensor_tensor(shift[:, r % 2, TB:ST], part[:, 0, :], part[:, 1, :], ALU.min
                                  ).then_inc(shift_ready, 1)

            def all_sums(r):
                return sums[:, r % 2, :].rearrange("p (t c) -> p t c", c=VW)

            def total(m, r):
                if not exists(m, r):
                    return
                dve.wait_ge(o_copied, head(m, r) + 1)
                dve.reciprocal(rsum[:, :], all_sums(r)[:, :, HD]).then_inc(rsum_done, 1)
                dve.tensor_tensor(all_sums(r)[:, :, 0:HD], all_sums(r)[:, :, 0:HD], all_sums(r)[:, :, VH:VW],
                                  ALU.add).then_inc(o_added, 1)

            def normalise(m, r):
                if not exists(m, r):
                    return
                h, u, q = head(m, r), r // REP, r % REP
                if q == 0 and (not isinstance(m, int) or m >= 1):
                    dve.wait_ge(o_stored[u], 16 * m)
                dve.wait_ge(rsum_done, h + 1)
                dve.wait_ge(o_added, h + 1)
                dve.tensor_tensor(o[:, u, :, q * HD:(q + 1) * HD], all_sums(r)[:, :, 0:HD],
                                  rsum[:, :].unsqueeze(2).to_broadcast([P, ST, HD]), ALU.mult
                                  ).then_inc(o_done, 1)

            def step(m, r):
                for t in range(ST):
                    maxima(*at(m, r, 2, R), t)
                    if t == 0 and len(DVE_TILES) > 1:
                        low(dve, *at(m, r, -1, R), DVE_TILES[1], lo_dve)
                    if t == 1:
                        total(*at(m, r, -2, R))
                    if t == 2:
                        normalise(*at(m, r, -2, R))
                    if t == 3 and len(DVE_TILES) > 2:
                        low(dve, *at(m, r, -1, R), DVE_TILES[2], lo_dve)
                low(dve, m, r, DVE_TILES[0], lo_dve)
                merge(*at(m, r, 2, R))

            steps(dve, step)

        @block.gpsimd
        def _(pool):
            def step(m, r):
                for t in POOL_TILES:
                    low(pool, m, r, t, lo_pool)

            steps(pool, step)


def load_attended(eng, o_d, a, a_loaded, b, m, u):
    eng.dma_start(a[:, u, :].rearrange("p (g c) -> p g c", g=KV),
                  o_d.rearrange("b g p t c -> b t p g c")[b, 2 * m + u]).then_inc(a_loaded[u], 16)


def load_wo(eng, wo, w_in, w_loaded, s):
    eng.dma_start(w_in[:, s % STAGE, :], wo.rearrange("(s p) n -> p s n", p=P)[:, s, :]
                  ).then_inc(w_loaded[s % STAGE], 16)


def project_out(nc, o_d, wo, s_d, ident, o_stored, a, a_loaded, w_in, w_loaded, lanes_in, scales_gu, zeros_gu,
                scales_d, zeros_d, g_idx_gu, lanes, sc_d, z_d, scd, zd, sel_gu, s_out, stored, load_ffn):
    PIECE = 688
    PIECES = 2 * INTER // PIECE
    WORDS = PIECE // NIB
    R_GU, R_D = 64 + G_GU, 64 + G_D
    with ExitStack() as ctx:
        def sb(name, shape, dt):
            return ctx.enter_context(nc.sbuf_tensor(name, shape, dt))

        def sem(name):
            return ctx.enter_context(nc.semaphore(name))

        ah = sb("ah", [P, 2, D], F16)
        al = sb("al", [P, 2, D], F16)
        aT = sb("aT", [P, 2, 2, KT, P], F16)
        w = sb("wo", [P, 2, KT, D], F16)
        out_ps = [ctx.enter_context(nc.psum_tensor(f"out_ps{i}", [P, FULL], F32)) for i in range(2)]
        tr_ps = [ctx.enter_context(nc.psum_tensor(f"tro_ps{i}", [P, KT, P], F16)) for i in range(2)]

        whi_done = sem("wohi_done")
        wlo_done = sem("wolo_done")
        ah_done = sem("ah_done")
        al_done = sem("al_done")
        ah_turned = sem("ah_turned")
        al_turned = sem("al_turned")
        aTh_done = sem("aTh_done")
        aTl_done = sem("aTl_done")
        out_ready = sem("out_ready")
        out_done = sem("out_done")
        s_v = s_d.rearrange("(t p) n -> t p n", p=P)

        sc = sb("tb_sc", [R_GU, 2, PIECE], F32)
        sc_dn = sb("tb_sc_dn", [R_D, D], F32)
        rest = sb("tb_rest", [R_D, D], F32)
        hi = sb("tb_hi", [R_GU, 2, PIECE], BF16)
        mid = sb("tb_mid", [R_D, D], BF16)
        lo = sb("tb_lo", [R_D, D], BF16)
        zw = sb("tb_zw", [32 + G_GU, 2, WORDS], U32)
        zw_dn = sb("tb_zw_dn", [32 + G_D, D // NIB], U32)
        zn = sb("tb_zn", [32 + G_D, D // NIB, 2], U32)
        zt = sb("tb_zt", [R_GU, 2, PIECE // HALF_NIB], BF16)
        idx = sb("tb_idx", [R_GU, D], I32)
        idf = sb("tb_idf", [R_GU, D], F32)

        tb_loaded = [sem(f"tb_loaded{i}") for i in range(2)]
        dn_loaded = sem("tb_dn_loaded")
        idx_loaded = sem("tb_idx_loaded")
        zeroed = sem("tb_zeroed")
        selecting = sem("tb_selecting")
        dn_step = sem("tb_dn_step")
        tb_step = sem("tb_step")
        built = sem("tb_built")
        tb_stored = [sem(f"tb_stored{i}") for i in range(2)]

        block = ctx.enter_context(nc.Block())

        @block.sync
        def _(sp):
            def load(b, m, u):
                sp.wait_ge(al_done, b * ST + 2 * m + u - 1)
                load_attended(sp, o_d, a, a_loaded, b, m, u)

            def load_piece(c, u):
                cols, words = bass.ds((2 * c + u) * PIECE, PIECE), bass.ds((2 * c + u) * WORDS, WORDS)
                for k in range(3):
                    sp.dma_start(sc[32 * k:32 * k + G_GU, u, :], scales_gu[:, cols]).then_inc(tb_loaded[u], 16)
                for k in range(2):
                    sp.dma_start(zw[32 * k:32 * k + G_GU, u, :], zeros_gu[:, words]).then_inc(tb_loaded[u], 16)

            def store_piece(c, u):
                cols = bass.ds((2 * c + u) * PIECE, PIECE)
                sp.wait_ge(built, 2 * c + u + 1)
                sp.dma_start(sc_d[:, cols], hi[:, u, :]).then_inc(tb_stored[u], 16)
                sp.dma_start(z_d[:, bass.ds((2 * c + u) * (PIECE // HALF_NIB), PIECE // HALF_NIB)], zt[:, u, :]
                             ).then_inc(tb_stored[u], 16)

            load(0, 1, 0)
            load(0, 1, 1)
            for s in range(STAGE, KT):
                sp.wait_ge(wlo_done, s - STAGE + 1)
                load_wo(sp, wo, w_in, w_loaded, s)
            sp.wait_ge(zeroed, 1)
            for u in range(2):
                load_piece(0, u)
            sp.dma_start(lanes[:, :], lanes_in).then_inc(idx_loaded, 16)
            sp.dma_start(idx[:, :], g_idx_gu.rearrange("(a i) -> a i", a=1).broadcast_to([R_GU, D])
                         ).then_inc(idx_loaded, 16)
            for k in range(3):
                sp.dma_start(sc_dn[32 * k:32 * k + G_D, :], scales_d).then_inc(dn_loaded, 16)
            for k in range(2):
                sp.dma_start(zw_dn[32 * k:32 * k + G_D, :], zeros_d).then_inc(dn_loaded, 16)
            for u in range(2):
                load(0, 2, u)
            for u in range(2):
                load(0, 3, u)
                store_piece(0, u)
                load_piece(1, u)
            for u in range(2):
                sp.wait_ge(o_stored[u], 16 * GROUPS // 2)
            with sp.Fori(0, PIECES // 2 - 2) as m:
                for u in range(2):
                    load(1, m, u)
                    store_piece(m + 1, u)
                    load_piece(m + 2, u)
            for u in range(2):
                load(1, PIECES // 2 - 2, u)
                store_piece(PIECES // 2 - 1, u)
            for m in range(PIECES // 2 - 1, ST // 2):
                for u in range(2):
                    load(1, m, u)
            for u in range(2):
                sp.wait_ge(tb_stored[u], 32 * PIECES // 2)
            load_ffn(sp)

        @block.gpsimd
        def _(pool):
            pool.memset(sc[:, :, :], 0.0)
            pool.memset(sc_dn[:, :], 0.0)
            pool.memset(zt[:, :, :], 0.0)
            pool.memset(zd[:, :], 0.0).then_inc(zeroed, 1)

        @block.scalar
        def _(act):
            def high(m, u):
                if not inside(m, u, TT):
                    return
                n = 2 * m + u
                act.wait_ge(a_loaded[u], 16 * (m + 1))
                if not isinstance(m, int) or m >= 1:
                    act.wait_ge(ah_turned, n - 1)
                    act.wait_ge(al_done, n - 1)
                act.activation(ah[:, u, :], a[:, u, :], ACT.Copy).then_inc(ah_done, 1)

            def turned(m, u):
                if not inside(m, u, TT):
                    return
                n = 2 * m + u
                act.wait_ge(ah_turned, n + 1)
                if not isinstance(m, int) or m >= 1:
                    act.wait_ge(out_ready, n - 1)
                act.activation(aT[:, u, 0, :, :], tr_ps[0][:, :, :], ACT.Copy).then_inc(aTh_done, 1)

            def post(m, u):
                if not inside(m, u, TT):
                    return
                n = 2 * m + u
                act.wait_ge(out_ready, n + 1)
                if not isinstance(m, int) or m >= 1:
                    act.wait_ge(stored[u], 16 * m)
                act.activation(s_out[:, u, :], out_ps[u][:, :], ACT.Copy, scale=1.0 / W_SCALE
                               ).then_inc(out_done, 1)
                act.wait_ge(out_done, n + 1)
                act.dma_start(s_v[n], s_out[:, u, :]).then_inc(stored[u], 16)

            def step(m, u):
                high(*at(m, u, 2))
                turned(*at(m, u, 1))
                post(m, u)

            high(0, 0)
            high(0, 1)
            for s in range(KT):
                act.wait_ge(w_loaded[s % STAGE], 16 * (s // STAGE + 1))
                act.activation(w[:, 0, s, :], w_in[:, s % STAGE, :], ACT.Copy, scale=W_SCALE
                               ).then_inc(whi_done, 1)
                if s < 2:
                    turned(0, s)
            high(1, 0)
            high(1, 1)
            turned(1, 0)
            post(0, 0)
            post(0, 1)
            with act.Fori(1, TT // 2 - 1) as m:
                step(m, 0)
                step(m, 1)
            step(TT // 2 - 1, 0)
            step(TT // 2 - 1, 1)

        @block.vector
        def _(dve):
            def low(m, u):
                if not inside(m, u, TT):
                    return
                n = 2 * m + u
                dve.wait_ge(ah_done, n + 1)
                if not isinstance(m, int) or m >= 1:
                    dve.wait_ge(al_turned, n - 1)
                dve.tensor_tensor(al[:, u, :], a[:, u, :], ah[:, u, :], ALU.subtract).then_inc(al_done, 1)

            def turned(m, u):
                if not inside(m, u, TT):
                    return
                n = 2 * m + u
                dve.wait_ge(al_turned, n + 1)
                if not isinstance(m, int) or m >= 1:
                    dve.wait_ge(out_ready, n - 1)
                dve.tensor_copy(aT[:, u, 1, :, :], tr_ps[1][:, :, :]).then_inc(aTl_done, 1)

            def step(m, u):
                low(*at(m, u, 2))
                turned(*at(m, u, 1))

            def chain(done, first, ops):
                for k, op in enumerate(ops):
                    if k:
                        dve.wait_ge(done, first + k)
                    op().then_inc(done, 1)

            def split(x, r, md, l, hold, g):
                rows = 64 + g
                return [lambda: dve.tensor_scalar(hold[0:rows, :], x, W_SCALE, None, ALU.mult),
                        lambda: dve.scalar_tensor_tensor(r, x, W_SCALE, hold[0:rows, :], ALU.mult, ALU.subtract),
                        lambda: dve.tensor_copy(md, r),
                        lambda: dve.tensor_tensor(l, r, md, ALU.subtract),
                        lambda: dve.tensor_copy(hold[32:64, :], md[32:64, :]),
                        lambda: dve.tensor_copy(hold[64:rows, :], l[64:rows, :])]

            def unpack(words, n, out, g):
                def values():
                    for k in range(2):
                        for b, rows in ((8, slice(0, g)), (0, slice(32, 32 + g))):
                            last = dve.tensor_scalar(n[rows, :, k], words[rows, :], 16 * k + b, 255,
                                                     ALU.logical_shift_right, ALU.bitwise_and)
                    return last

                def parts():
                    for scale, rows in ((256.0, slice(0, g)), (1.0, slice(32, 32 + g))):
                        last = dve.tensor_scalar(out[rows, :].rearrange("g (c k) -> g c k", k=2),
                                                 n[rows, :, :], scale, None, ALU.mult)
                    return last
                return [values, parts]

            def select():
                dve.wait_ge(idx_loaded, 32)
                chain(selecting, 0, [
                    lambda: dve.tensor_scalar(idf[:, :], idx[:, :], 0.0, float(G_GU), ALU.is_lt, ALU.mult),
                    lambda: dve.tensor_tensor(rest[0:R_GU, :], idf[:, :], idx[:, :], ALU.add),
                    lambda: dve.tensor_scalar(idf[:, :], rest[0:R_GU, :], 0.0, float(G_GU - 1), ALU.max, ALU.min),
                    lambda: dve.tensor_scalar(sel_gu[0:R_GU, :], idf[:, :], lanes[0:R_GU, 0:1], None,
                                              ALU.is_equal)])

            def down_tables():
                dve.wait_ge(dn_loaded, 80)
                chain(dn_step, 0, split(sc_dn[:, :], rest[:, :], mid[:, :], lo[:, :], scd, G_D)
                      + unpack(zw_dn, zn, zd, G_D))

            def piece(c, u):
                dve.wait_ge(tb_loaded[u], 80 * (c + 1))
                if not isinstance(c, int) or c >= 1:
                    dve.wait_ge(tb_stored[u], 32 * c)
                ops = (split(sc[:, u, :], rest[0:R_GU, 0:PIECE], mid[0:R_GU, 0:PIECE], lo[0:R_GU, 0:PIECE],
                             hi[:, u, :], G_GU)
                       + unpack(zw[:, u, :], zn[:, 0:WORDS, :], zt[:, u, :], G_GU))
                first = len(ops) * (2 * c + u)
                chain(tb_step, first, ops[:-1])
                dve.wait_ge(tb_step, first + len(ops) - 1)
                ops[-1]().then_inc(tb_step, 1)
                dve.wait_ge(tb_step, first + len(ops))
                dve.tensor_copy(rest[0:1, 0:1], rest[0:1, 0:1]).then_inc(built, 1)

            low(0, 0)
            low(0, 1)
            for s in range(KT):
                dve.wait_ge(whi_done, s + 1)
                dve.scalar_tensor_tensor(w[:, 1, s, :], w_in[:, s % STAGE, :], W_SCALE, w[:, 0, s, :],
                                         ALU.mult, ALU.subtract).then_inc(wlo_done, 1)
                if s < 2:
                    turned(0, s)
            low(1, 0)
            low(1, 1)
            turned(1, 0)
            with dve.Fori(1, PIECES // 2 + 1) as m:
                for u in range(2):
                    step(m, u)
                    piece(m - 1, u)
            for m in range(PIECES // 2 + 1, TT // 2):
                step(m, 0)
                if m == TT // 2 - 2:
                    select()
                step(m, 1)
                if m == TT // 2 - 2:
                    down_tables()

        @block.tensor
        def _(pe):
            def turn(m, u):
                if not inside(m, u, TT):
                    return
                n = 2 * m + u
                for part, (src, done, free, out) in enumerate([(ah, ah_done, aTh_done, ah_turned),
                                                               (al, al_done, aTl_done, al_turned)]):
                    pe.wait_ge(done, n + 1)
                    if not isinstance(m, int) or n >= 1:
                        pe.wait_ge(free, n)
                    for s in range(KT):
                        last = pe.transpose(tr_ps[part][:, s, :], src[:, u, s * P:(s + 1) * P], ident[:, :])
                    last.then_inc(out, 1)

            def operands(m, u):
                n = 2 * m + u
                pe.wait_ge(aTh_done, n + 1)
                pe.wait_ge(aTl_done, n + 1)
                if not isinstance(m, int) or m >= 1:
                    pe.wait_ge(out_done, n - 1)

            def contract(u, s):
                for k, (xp, wp) in enumerate([(0, 0), (0, 1), (1, 0)]):
                    for c in range(D // BANK):
                        cols = slice(c * BANK, (c + 1) * BANK)
                        last = pe.matmul(out_ps[u][:, cols], aT[:, u, xp, s, :], w[:, wp, s, cols],
                                         start=(s == 0 and k == 0), stop=(s == KT - 1 and k == 2))
                if s == KT - 1:
                    last.then_inc(out_ready, 1)

            def products(m, u):
                operands(m, u)
                for s in range(KT):
                    contract(u, s)

            turn(0, 0)
            turn(0, 1)
            operands(0, 0)
            for s in range(KT):
                pe.wait_ge(whi_done, s + 1)
                pe.wait_ge(wlo_done, s + 1)
                contract(0, s)
                if s == KT // 2:
                    operands(0, 1)
                if s >= KT // 2:
                    contract(1, s - KT // 2)
            turn(1, 0)
            for s in range(KT // 2, KT):
                contract(1, s)
            with pe.Fori(1, TT // 2 - 1) as m:
                for u in range(2):
                    turn(*at(m, u, 1))
                    products(m, u)
            turn(TT // 2 - 1, 1)
            products(TT // 2 - 1, 0)
            products(TT // 2 - 1, 1)


def tile_width(j):
    return FLAST if isinstance(j, int) and j == FTILES - 1 else P


def load_gate_up(sp, qw_gu, z_d, sc_d, qwg, zt, st, gu_loaded, j, u):
    for src, dst, per in ((qw_gu, qwg, 1), (z_d, zt, HALF_NIB), (sc_d, st, 1)):
        w = tile_width(j) // per
        sp.dma_start(dst[:, u, :, 0:w], src.rearrange("p (h f) -> p h f", h=2)[:, :, bass.ds(j * (P // per), w)]
                     ).then_inc(gu_loaded[u], 16)


def load_down(sp, qw_d, qwd, dn_loaded, j, n):
    w = tile_width(j)
    rows = qw_d[bass.ds(j * (P // NIB), w // NIB), n * BANK:(n + 1) * BANK]
    sp.dma_start(qwd[0:w, n, :], rows.unsqueeze(1).broadcast_to([w // NIB, NIB, BANK])).then_inc(dn_loaded[n], 16)


def load_groups(sp, g_idx_d, idx, idx_loaded, j, u):
    w = tile_width(j)
    sp.dma_start(idx[:, u, 0:w],
                 g_idx_d.rearrange("(a i) -> a i", a=1)[:, bass.ds(j * P, w)].broadcast_to([64 + G_D, w])
                 ).then_inc(idx_loaded[u], 16)


def feed_forward(nc, x, qw_gu, qw_d, g_idx_d, lanes, sc_d, z_d, scd, zd, sel_gu, xT, s_d, s_stored, out,
                 qwg, zt, st, gu_loaded, qwd, idx, dn_loaded, idx_loaded):
    R_GU, R_D = 64 + G_GU, 64 + G_D
    ROUNDS = NIB // 2
    PER = ROUNDS + 2
    DN = 2 * TT
    DT = DN // TC
    RING = 8
    J0 = FTILES - CHUNK
    J1 = FTILES - 1
    LAST = [(J0, 0), (J0, 1), (J1, 0), (J1, 1), 0, (J0, 2), (J1, 2), 1, (J0, 3), (J1, 3), 2, 3]
    LAST_GU = [step for step in LAST if isinstance(step, tuple)]
    with ExitStack() as ctx:
        def sb(name, shape, dt):
            return ctx.enter_context(nc.sbuf_tensor(name, shape, dt))

        def sem(name):
            return ctx.enter_context(nc.semaphore(name))

        acc = sb("acc", [P, TT, D], F32)
        hT = sb("hT", [P, 2, CHUNK, T], F16)
        wg = sb("wg", [P, 2, 2, KT, 2 * P], F16)
        wd = sb("wd", [P, 2, CHUNK, D], F16)
        nib = sb("nib", [P, BANK], U32)
        zhalf = sb("zhalf", [P, BANK // HALF_NIB], U32)
        zero = sb("zero", [P, BANK], U32)
        dif = sb("dif", [P, BANK], F32)
        wf = sb("wf", [P, 2, BANK], F32)
        h = sb("h", [P, 2, BANK], F32)
        idf = sb("idf", [R_D, 2, P], F32)
        sel = sb("sel", [R_D, 2, P], BF16)
        gate_ps = [ctx.enter_context(nc.psum_tensor(f"gate_ps{i}", [P, BANK], F32)) for i in range(2)]
        up_ps = [ctx.enter_context(nc.psum_tensor(f"up_ps{i}", [P, BANK], F32)) for i in range(2)]
        dn_ps = [ctx.enter_context(nc.psum_tensor(f"dn_ps{i}", [P, BANK], F32)) for i in range(2)]
        z_ps = ctx.enter_context(nc.psum_tensor("z_ps", [P, BANK], F32))
        s_ps = ctx.enter_context(nc.psum_tensor("s_ps", [P, BANK], F32))

        sel_step = sem("sel_step")
        sel_done = sem("sel_done")
        zs_ready = sem("zs_ready")
        nib_done = sem("nib_done")
        zhalf_done = sem("zhalf_done")
        zero_done = sem("zero_done")
        dif_done = sem("dif_done")
        wf_done = sem("wf_done")
        whi_done = sem("fwhi_done")
        wlo_done = sem("fwlo_done")
        gu_ready = sem("gu_ready")
        silu_done = sem("silu_done")
        h_done = sem("h_done")
        hhi_done = sem("hhi_done")
        hlo_done = sem("hlo_done")
        dn_ready = sem("dn_ready")
        dn_taken = sem("dn_taken")
        g_done = sem("g_done")
        xs_loaded = [sem(f"xs_loaded{i}") for i in range(RING)]
        prod_done = sem("prod_done")
        sum_done = sem("sum_done")
        out_stored = sem("out_stored")

        x_v = x.rearrange("b (t p) d -> (b t) p d", p=P)
        s_v = s_d.rearrange("(t p) d -> t p d", p=P)
        out_v = out.rearrange("b (t p) d -> (b t) p d", p=P)

        width = tile_width
        spent = xT[:, :, :, :].bitcast(F32)
        HALF_BANK = BANK // 2

        def ring(k, part):
            i = k % RING
            rows, c = 2 * (i % (KT // 2)), i // (KT // 2) * HALF_BANK
            return spent[:, part, rows:rows + 2, c:c + HALF_BANK]

        def unit(k):
            n = k % 2
            return acc[:, k // 2, n * BANK:(n + 1) * BANK].rearrange("p (r c) -> p r c", c=HALF_BANK)

        def first_round(j, kind):
            if kind == "g":
                return 0 if isinstance(j, int) and j == 0 else ROUNDS + PER * (j - 1)
            return ROUNDS + PER * j + (0 if isinstance(j, int) and j == FTILES - 1 else ROUNDS)

        def places(j):
            nxt = [("g", k) for k in range(ROUNDS)] if not (isinstance(j, int) and j == FTILES - 1) else []
            return (nxt + [("d", 0), ("d", 1)] + [None] * 8)[:8]

        def rounds_at(j, t):
            if isinstance(j, int) and j == 0 and t < 2:
                first = [(max(2 * k - 2, 0), 1, ("g", k)) for k in range(ROUNDS)] + [(KT - 1, 0, places(0)[0])]
                return first if t == 0 else [(3 * k, 0, places(0)[k + 1]) for k in range(3)]
            if isinstance(j, int) and j >= J0:
                per = 3
                return [(3 * n, 0, place) for n, place in enumerate(places(j)[per * t:per * (t + 1)]) if place]
            return [(n * KT // 2, 0, place) for n, place in enumerate(places(j)[2 * t:2 * t + 2]) if place]

        def order(j, t):
            if isinstance(j, int) and j >= J0:
                return TC * J0 + LAST_GU.index((j, t))
            return TC * j + t

        def slot(j, t):
            return order(j, t) % 2 if isinstance(j, int) else t % 2

        block = ctx.enter_context(nc.Block())

        @block.sync
        def _(sp):
            def step(j, u):
                more = not isinstance(j, int) or j + 1 < FTILES
                sp.wait_ge(wf_done, first_round(j, "g") + ROUNDS)
                if not isinstance(j, int) or j + 2 < FTILES:
                    load_gate_up(sp, qw_gu, z_d, sc_d, qwg, zt, st, gu_loaded, j + 2, u)
                if more:
                    load_groups(sp, g_idx_d, idx, idx_loaded, j + 1, 1 - u)
                    for n in range(2):
                        sp.wait_ge(wf_done, first_round(j, "d") + n + 1)
                        load_down(sp, qw_d, qwd, dn_loaded, j + 1, n)

            def load_unit(k):
                n = k % 2
                cols = slice(n * BANK, (n + 1) * BANK)
                for part, src in ((0, x_v), (1, s_v)):
                    sp.dma_start(ring(k, part), src[k // 2][:, cols].rearrange("p (r c) -> p r c", c=HALF_BANK)
                                 ).then_inc(xs_loaded[k % RING], 16)

            def store_unit(k):
                n = k % 2
                cols = slice(n * BANK, (n + 1) * BANK)
                sp.wait_ge(sum_done, k + 1)
                sp.dma_start(out_v[k // 2][:, cols], acc[:, k // 2, cols]).then_inc(out_stored, 16)

            step(0, 0)
            step(1, 1)
            with sp.Fori(1, CHUNKS - 2) as c:
                for u in range(2):
                    step(CHUNK * c + u, u)
            for j in range(CHUNK * (CHUNKS - 2), FTILES):
                step(j, j % 2)
            for u in range(2):
                sp.wait_ge(s_stored[u], 16 * TT // 2)
            for k in range(RING):
                if k % (KT // 2) == 0:
                    sp.wait_ge(gu_ready, order(J1, k // (KT // 2)) + 1)
                load_unit(k)
            for k in range(DN):
                store_unit(k)
                if k + RING < DN:
                    load_unit(k + RING)
            sp.wait_ge(out_stored, 16 * DN)

        @block.tensor
        def _(pe):
            def rebuild(j, u, place):
                if place is None:
                    return
                kind, k = place
                if kind == "g":
                    n, w, s_u = first_round(j + 1, "g") + k, width(j + 1), 1 - u
                    if k == 0:
                        slot_load = gu_loaded[s_u]
                        pe.wait_ge(slot_load, 48 * ((j + 1 - s_u) // 2 + 1))
                    if not isinstance(n, int) or n >= 1:
                        pe.wait_ge(wf_done, n)
                    for b in range(2):
                        rows = sel_gu[0:R_GU, :].rearrange("g (p s) -> g s p", s=KT)[:, 2 * k + b, :]
                        for src, dst, per in ((zt, z_ps, HALF_NIB), (st, s_ps, 1)):
                            c, v = b * 2 * P // per, w // per
                            last = pe.matmul(dst[:, c:c + 2 * v], rows, src[:, s_u, :, 0:v], start=True, stop=True)
                else:
                    n, w = first_round(j, "d") + k, width(j)
                    pe.wait_ge(wf_done, n)
                    if k == 0:
                        pe.wait_ge(sel_done, j + 1)
                    for src, dst, per in ((zd, z_ps, HALF_NIB), (scd, s_ps, 1)):
                        v = BANK // per
                        last = pe.matmul(dst[0:w, 0:v], sel[:, u, 0:w], src[0:R_D, k * v:(k + 1) * v],
                                         start=True, stop=True)
                last.then_inc(zs_ready, 1)

            def gate_up(j, u, t):
                w, e, q = width(j), order(j, t), slot(j, t)
                first = isinstance(j, int) and j == 0 and t == 0
                if t == 0 and not first:
                    pe.wait_ge(whi_done, first_round(j, "g") + ROUNDS)
                    pe.wait_ge(wlo_done, first_round(j, "g") + ROUNDS)
                if not isinstance(j, int) or e >= 2:
                    pe.wait_ge(h_done, e - 1)
                ps = [gate_ps, up_ps] if w == P else [gate_ps]
                for s in range(KT):
                    for before, back, place in rounds_at(j, t):
                        if before == s:
                            rebuild(j - back, (u + back) % 2, place)
                    if first and s % 2 == 0:
                        pe.wait_ge(whi_done, s // 2 + 1)
                        pe.wait_ge(wlo_done, s // 2 + 1)
                    for k, (wp, xp) in enumerate([(0, 0), (0, 1), (1, 0)]):
                        for g, to in enumerate(ps):
                            last = pe.matmul(to[q][:, :], wg[:, u, wp, s, g * P:(g + 1) * P],
                                             xT[:, xp, s, t * BANK:(t + 1) * BANK],
                                             start=(s == 0 and k == 0), stop=(s == KT - 1 and k == 2))
                last.then_inc(gu_ready, 1)

            def down(c, t):
                j = CHUNK * c + CHUNK - 1
                if t == 0:
                    pe.wait_ge(whi_done, first_round(j, "d") + 2)
                    pe.wait_ge(wlo_done, first_round(j, "d") + 2)
                pe.wait_ge(hlo_done, order(j, t) + 1)
                pe.wait_ge(hhi_done, order(j, t) + 1)
                for k in range(DT * t, DT * (t + 1)):
                    i, n, tokens = DN * c + k, k % 2, slice(k // 2 * P, (k // 2 + 1) * P)
                    if not isinstance(c, int) or i >= 2:
                        pe.wait_ge(dn_taken, i - 1)
                    for e in range(CHUNK):
                        w = width(CHUNK * c + e)
                        for p, (hp, wp) in enumerate([(0, 0), (0, 1), (1, 0)]):
                            last = pe.matmul(dn_ps[n][:, :], hT[0:w, hp, e, tokens],
                                             wd[0:w, wp, e, n * BANK:(n + 1) * BANK],
                                             start=(e == 0 and p == 0), stop=(e == CHUNK - 1 and p == 2))
                    last.then_inc(dn_ready, 1)

            def chunk(c):
                for u in range(CHUNK):
                    for t in range(TC):
                        gate_up(CHUNK * c + u, u, t)
                for t in range(TC):
                    down(c, t)

            chunk(0)
            with pe.Fori(1, CHUNKS - 1) as c:
                chunk(c)
            for step in LAST:
                if isinstance(step, tuple):
                    gate_up(step[0], step[0] - J0, step[1])
                else:
                    down(CHUNKS - 1, step)

        @block.vector
        def _(dve):
            def select(j, u):
                w = width(j)
                steps = [lambda: dve.tensor_scalar(idf[:, 0, 0:w], idx[:, u, 0:w], 0.0, float(G_D),
                                                   ALU.is_lt, ALU.mult),
                         lambda: dve.tensor_tensor(idf[:, 1, 0:w], idf[:, 0, 0:w], idx[:, u, 0:w], ALU.add),
                         lambda: dve.tensor_scalar(idf[:, 0, 0:w], idf[:, 1, 0:w], 0.0, float(G_D - 1),
                                                   ALU.max, ALU.min)]
                dve.wait_ge(idx_loaded[u], 16 * ((j - u) // 2 + 1))
                for k, op in enumerate(steps):
                    op().then_inc(sel_step, 1)
                    dve.wait_ge(sel_step, 3 * j + k + 1)
                dve.tensor_scalar(sel[:, u, 0:w], idf[:, 0, 0:w], lanes[0:R_D, 0:1], None, ALU.is_equal
                                  ).then_inc(sel_done, 1)

            def rebuild(j, u, place):
                if place is None:
                    return
                kind, k = place
                if kind == "g":
                    n, w, s_u = first_round(j + 1, "g") + k, width(j + 1), 1 - u
                    p, view = P, [slice(b * 2 * P, b * 2 * P + 2 * w) for b in range(2)]
                    if k == 0:
                        dve.wait_ge(gu_loaded[s_u], 48 * ((j + 1 - s_u) // 2 + 1))
                    for b in range(2):
                        last = dve.tensor_scalar(nib[:, view[b]].rearrange("p (h f) -> p h f", h=2),
                                                 qwg[:, s_u, :, 0:w], 4 * (2 * k + b), 15,
                                                 ALU.logical_shift_right, ALU.bitwise_and)
                    if w == P:
                        view = [slice(0, BANK)]
                else:
                    n, p, view = first_round(j, "d") + k, width(j), [slice(0, BANK)]
                    dve.wait_ge(dn_loaded[k], 16 * (j + 1))
                    last = dve.tensor_scalar(nib[0:p, :], qwd[0:p, k, :], lanes[0:p, 1:2].bitcast(U32), 15,
                                             ALU.logical_shift_right, ALU.bitwise_and)
                last.then_inc(nib_done, 1)
                halves = [slice(v.start // HALF_NIB, v.stop // HALF_NIB) for v in view]
                dve.wait_ge(zs_ready, n + 1)
                for v in halves:
                    last = dve.tensor_copy(zhalf[0:p, v], z_ps[0:p, v])
                last.then_inc(zhalf_done, 1)
                dve.wait_ge(zhalf_done, n + 1)
                for i in range(HALF_NIB):
                    for v in halves:
                        last = dve.tensor_scalar(zero[0:p, :].rearrange("p (c k) -> p c k", k=HALF_NIB)[:, v, i],
                                                 zhalf[0:p, v], 4 * i, 15, ALU.logical_shift_right, ALU.bitwise_and)
                last.then_inc(zero_done, 1)
                dve.wait_ge(nib_done, n + 1)
                dve.wait_ge(zero_done, n + 1)
                for v in view:
                    last = dve.tensor_tensor(dif[0:p, v], nib[0:p, v], zero[0:p, v], ALU.subtract)
                last.then_inc(dif_done, 1)
                dve.wait_ge(dif_done, n + 1)
                if not isinstance(n, int) or n >= 2:
                    dve.wait_ge(wlo_done, n - 1)
                for v in view:
                    last = dve.scalar_tensor_tensor(wf[0:p, k % 2, v], dif[0:p, v], 1.0, s_ps[0:p, v],
                                                    ALU.subtract, ALU.mult)
                last.then_inc(wf_done, 1)

            def gated(j, t):
                w, e, q = width(j), order(j, t), slot(j, t)
                up = up_ps[q][:, :] if w == P else gate_ps[q][w:2 * w, :]
                dve.wait_ge(silu_done, e + 1)
                dve.scalar_tensor_tensor(h[0:w, q, :], up, H_SCALE / W_SCALE, h[0:w, q, :], ALU.mult, ALU.mult
                                         ).then_inc(h_done, 1)

            def products(j, u, t):
                if t == 0:
                    select(j, u)
                for _, back, place in rounds_at(j, t):
                    rebuild(j - back, (u + back) % 2, place)
                gated(j, t)

            def add(c, k):
                i, n = DN * c + k, k % 2
                cols = slice(n * BANK, (n + 1) * BANK)
                dve.wait_ge(dn_ready, i + 1)
                if isinstance(c, int) and c == 0:
                    dve.tensor_copy(acc[:, k // 2, cols], dn_ps[n][:, :]).then_inc(dn_taken, 1)
                else:
                    dve.tensor_tensor(acc[:, k // 2, cols], acc[:, k // 2, cols], dn_ps[n][:, :], ALU.add
                                      ).then_inc(dn_taken, 1)

            def weigh(k):
                dve.wait_ge(g_done, k + 1)
                dve.wait_ge(xs_loaded[k % RING], 32 * (k // RING + 1))
                dve.tensor_tensor(unit(k), unit(k), ring(k, 1), ALU.mult).then_inc(prod_done, 1)

            def chunk(c):
                for u in range(CHUNK):
                    for t in range(TC):
                        products(CHUNK * c + u, u, t)
                if not isinstance(c, int) or c >= 1:
                    dve.wait_ge(dn_taken, DN * c)
                for k in range(DN):
                    add(c, k)

            chunk(0)
            with dve.Fori(1, CHUNKS - 1) as c:
                chunk(c)
            for step in LAST:
                if isinstance(step, tuple):
                    products(step[0], step[0] - J0, step[1])
                else:
                    if step == 0:
                        dve.wait_ge(dn_taken, DN * (CHUNKS - 1))
                    for k in range(DT * step, DT * (step + 1)):
                        add(CHUNKS - 1, k)
                        if k >= DT * step + 2:
                            weigh(k - 2)
                    weigh(DT * (step + 1) - 2)
                    weigh(DT * (step + 1) - 1)

        @block.scalar
        def _(act):
            def high(j, u, place):
                if place is None:
                    return
                kind, k = place
                if kind == "g":
                    n, w = first_round(j + 1, "g") + k, width(j + 1)
                    act.wait_ge(wf_done, n + 1)
                    act.activation(wg[:, 1 - u, 0, 2 * k:2 * k + 2, 0:2 * w],
                                   wf[:, k % 2, :].rearrange("p (s f) -> p s f", s=2)[:, :, 0:2 * w],
                                   ACT.Copy).then_inc(whi_done, 1)
                else:
                    n, w = first_round(j, "d") + k, width(j)
                    act.wait_ge(wf_done, n + 1)
                    act.activation(wd[0:w, 0, u, k * BANK:(k + 1) * BANK], wf[0:w, k % 2, :],
                                   ACT.Copy).then_inc(whi_done, 1)

            def gated(j, u, t):
                w, e, q = width(j), order(j, t), slot(j, t)
                act.wait_ge(gu_ready, e + 1)
                if not isinstance(e, int) or e >= 2:
                    act.wait_ge(hlo_done, e - 1)
                act.activation(h[0:w, q, :], gate_ps[q][0:w, :], ACT.Silu, scale=1.0 / W_SCALE
                               ).then_inc(silu_done, 1)
                act.wait_ge(h_done, e + 1)
                act.activation(hT[0:w, 0, u, t * BANK:(t + 1) * BANK], h[0:w, q, :], ACT.Copy
                               ).then_inc(hhi_done, 1)

            def products(j, u, t):
                for _, back, place in rounds_at(j, t):
                    high(j - back, (u + back) % 2, place)
                gated(j, u, t)

            def chunk(c):
                for u in range(CHUNK):
                    for t in range(TC):
                        products(CHUNK * c + u, u, t)

            chunk(0)
            with act.Fori(1, CHUNKS - 1) as c:
                chunk(c)
            for step in LAST:
                if isinstance(step, tuple):
                    products(step[0], step[0] - J0, step[1])
                    continue
                for k in range(DT * step, DT * (step + 1)):
                    n = k % 2
                    cols = slice(n * BANK, (n + 1) * BANK)
                    act.wait_ge(dn_taken, DN * (CHUNKS - 1) + k + 1)
                    act.activation(acc[:, k // 2, cols], acc[:, k // 2, cols], ACT.Silu,
                                   scale=1.0 / (W_SCALE * H_SCALE)).then_inc(g_done, 1)

        @block.gpsimd
        def _(pool):
            def low(j, u, place):
                if place is None:
                    return
                kind, k = place
                if kind == "g":
                    n, w = first_round(j + 1, "g") + k, width(j + 1)
                    s = slice(2 * k, 2 * k + 2)
                    pool.wait_ge(whi_done, n + 1)
                    pool.tensor_tensor(wg[:, 1 - u, 1, s, 0:2 * w],
                                       wf[:, k % 2, :].rearrange("p (s f) -> p s f", s=2)[:, :, 0:2 * w],
                                       wg[:, 1 - u, 0, s, 0:2 * w], ALU.subtract).then_inc(wlo_done, 1)
                else:
                    n, w = first_round(j, "d") + k, width(j)
                    cols = slice(k * BANK, (k + 1) * BANK)
                    pool.wait_ge(whi_done, n + 1)
                    pool.tensor_tensor(wd[0:w, 1, u, cols], wf[0:w, k % 2, :], wd[0:w, 0, u, cols],
                                       ALU.subtract).then_inc(wlo_done, 1)

            def gated(j, u, t):
                w, e, q = width(j), order(j, t), slot(j, t)
                cols = slice(t * BANK, (t + 1) * BANK)
                pool.wait_ge(hhi_done, e + 1)
                pool.tensor_tensor(hT[0:w, 1, u, cols], h[0:w, q, :], hT[0:w, 0, u, cols],
                                   ALU.subtract).then_inc(hlo_done, 1)

            def products(j, u, t):
                for _, back, place in rounds_at(j, t):
                    low(j - back, (u + back) % 2, place)
                gated(j, u, t)

            def chunk(c):
                for u in range(CHUNK):
                    for t in range(TC):
                        products(CHUNK * c + u, u, t)

            chunk(0)
            with pool.Fori(1, CHUNKS - 1) as c:
                chunk(c)
            for step in LAST:
                if isinstance(step, tuple):
                    products(step[0], step[0] - J0, step[1])
                    continue
                for k in range(DT * step, DT * (step + 1)):
                    pool.wait_ge(prod_done, k + 1)
                    pool.tensor_tensor(unit(k), unit(k), ring(k, 0), ALU.add).then_inc(sum_done, 1)


def build(nc, x, wq, wk, wv, wo, qw_gu, qz_gu, sc_gu, gi_gu, qw_d, qz_d, sc_dn, gi_d, rope, lanes_in, out):
    qk_d = nc.dram_tensor("qk_scratch", (B, KV, P, ST, (REP + 1) * STACK), F16, kind="Internal").ap()
    v_d = nc.dram_tensor("v_scratch", (B, KV, P, ST, VW), F16, kind="Internal").ap()
    o_d = nc.dram_tensor("o_scratch", (B, KV, P, ST, REP * HD), F32, kind="Internal").ap()
    s_d = nc.dram_tensor("s_scratch", (T, D), F32, kind="Internal").ap()
    sc_d = nc.dram_tensor("scale_scratch", (64 + G_GU, 2 * INTER), BF16, kind="Internal").ap()
    z_d = nc.dram_tensor("zero_scratch", (64 + G_GU, 2 * INTER // HALF_NIB), BF16, kind="Internal").ap()
    with ExitStack() as ctx:
        def sb(name, shape, dt):
            return ctx.enter_context(nc.sbuf_tensor(name, shape, dt))

        xT = sb("xT", [P, 2, KT, T], F16)
        ident = sb("ident", [P, P], F16)
        identb = sb("identb", [P, P], BF16)
        maskb = sb("maskb", [P, P], BF16)
        arena = sb("arena", [P, 2 * ST * ((REP + 1) * STACK + VW) // 2], F32)

        def shape(ap, dt, pattern, **sizes):
            return ap.bitcast(dt).rearrange(pattern, **sizes)

        n = ST * (REP + 1) * STACK
        qkn = shape(arena[:, 0:n], F16, "p (u t c) -> p u t c", u=2, t=ST)
        vn = shape(arena[:, n:n + ST * VW], F16, "p (u t c) -> p u t c", u=2, t=ST)
        qk_loaded = [ctx.enter_context(nc.semaphore(f"qk_loaded{i}")) for i in range(2)]
        v_loaded = [ctx.enter_context(nc.semaphore(f"v_loaded{i}")) for i in range(2)]
        project_qkv(nc, x, wq, wk, wv, rope, qk_d, v_d, xT, ident, identb, maskb, qkn, qk_loaded, vn, v_loaded)

        lanes = sb("lanes", [P, 2], I32)
        scd = sb("scd", [64 + G_D, D], BF16)
        zd = sb("zd", [64 + G_D, D // HALF_NIB], BF16)
        sel_gu = sb("sel_gu", [64 + G_GU, D], BF16)
        parts = np.cumsum([0, 2 * D, 2 * BANK, 4 * P, 2 * P, 2 * P]).tolist()
        places = [slice(c, e) for c, e in zip(parts, parts[1:])]
        s_out = shape(arena[:, places[0]], F32, "p (u d) -> p u d", u=2)
        qwd = shape(arena[:, places[1]], U32, "p (n c) -> p n c", n=2)
        qwg = shape(arena[:, places[2]], U32, "p (u h f) -> p u h f", u=2, h=2)
        st = shape(arena[0:64 + G_GU, places[3]], BF16, "p (u h f) -> p u h f", u=2, h=2)
        idx = shape(arena[0:64 + G_D, places[4]], I32, "p (u f) -> p u f", u=2)
        zt = sb("zt", [64 + G_GU, 2, 2, P // HALF_NIB], BF16)
        s_stored = [ctx.enter_context(nc.semaphore(f"s_stored{i}")) for i in range(2)]
        gu_loaded = [ctx.enter_context(nc.semaphore(f"gu_loaded{i}")) for i in range(2)]
        dn_loaded = [ctx.enter_context(nc.semaphore(f"dn_loaded{i}")) for i in range(2)]
        idx_loaded = [ctx.enter_context(nc.semaphore(f"idx_loaded{i}")) for i in range(2)]

        def load_ffn(sp):
            for u in range(2):
                load_gate_up(sp, qw_gu, z_d, sc_d, qwg, zt, st, gu_loaded, u, u)
            load_groups(sp, gi_d, idx, idx_loaded, 0, 0)
            for n in range(2):
                load_down(sp, qw_d, qwd, dn_loaded, 0, n)

        with ExitStack() as both:
            o = both.enter_context(nc.sbuf_tensor("o", [P, 2, ST, REP * HD], F32))
            a = both.enter_context(nc.sbuf_tensor("a", [P, 2, D], F32))
            w_in = both.enter_context(nc.sbuf_tensor("wo_in", [P, STAGE, D], F32))
            o_stored = [both.enter_context(nc.semaphore(f"o_stored{i}")) for i in range(2)]
            a_loaded = [both.enter_context(nc.semaphore(f"a_loaded{i}")) for i in range(2)]
            w_loaded = [both.enter_context(nc.semaphore(f"wo_loaded{i}")) for i in range(STAGE)]
            attend(nc, qk_d, v_d, o_d, wo, ident, identb, maskb, qkn, qk_loaded, vn, v_loaded, o, o_stored, a,
                   a_loaded, w_in, w_loaded)
            project_out(nc, o_d, wo, s_d, ident, o_stored, a, a_loaded, w_in, w_loaded, lanes_in, sc_gu, qz_gu,
                        sc_dn, qz_d, gi_gu, lanes, sc_d, z_d, scd, zd, sel_gu, s_out, s_stored, load_ffn)
        feed_forward(nc, x, qw_gu, qw_d, gi_d, lanes, sc_d, z_d, scd, zd, sel_gu, xT, s_d, s_stored, out,
                     qwg, zt, st, gu_loaded, qwd, idx, dn_loaded, idx_loaded)


def rope_table():
    f32 = np.float32
    freqs = (f32(1.0) / np.power(f32(THETA), np.arange(0, HD, 2, dtype=f32) / f32(HD))).astype(f32)
    ang = np.outer(np.arange(S, dtype=f32), freqs).astype(f32)
    both = np.stack([np.cos(ang), np.sin(ang)], axis=1).astype(f32) / f32(W_SCALE)
    both = np.tile(both.reshape(ST, P, 2, HALF), (B, 1, 1, 1))
    return np.ascontiguousarray(both.transpose(1, 0, 2, 3).reshape(P, -1))


def lane_table():
    p = np.arange(P)
    return np.stack([p % 32, 4 * (p % NIB)], axis=1).astype(np.int32)


def kernel(L0_attn_x, L0_attn_wq, L0_attn_wk, L0_attn_wv, L0_attn_wo, L0_ffn_qweight_gu, L0_ffn_qzeros_gu,
           L0_ffn_scales_gu, L0_ffn_g_idx_gu, L0_ffn_qweight_down, L0_ffn_qzeros_down, L0_ffn_scales_down,
           L0_ffn_g_idx_down):
    import concourse.bacc as bacc
    from concourse.bass_utils import run_bass_kernel_spmd

    given = {"x": L0_attn_x, "wq": L0_attn_wq, "wk": L0_attn_wk, "wv": L0_attn_wv, "wo": L0_attn_wo,
             "qw_gu": L0_ffn_qweight_gu, "qz_gu": L0_ffn_qzeros_gu, "sc_gu": L0_ffn_scales_gu,
             "gi_gu": L0_ffn_g_idx_gu, "qw_d": L0_ffn_qweight_down, "qz_d": L0_ffn_qzeros_down,
             "sc_dn": L0_ffn_scales_down, "gi_d": L0_ffn_g_idx_down, "rope": rope_table(), "lanes": lane_table()}
    nc = bacc.Bacc("TRN2", target_bir_lowering=False, num_devices=1)
    arrays, args = {}, []
    for name, a in given.items():
        a = np.ascontiguousarray(a)
        arrays[f"in_{name}"] = a
        args.append(nc.dram_tensor(f"in_{name}", a.shape, mybir.dt.from_np(a.dtype), kind="ExternalInput").ap())
    out = nc.dram_tensor("out", (B, S, D), F32, kind="ExternalOutput").ap()
    build(nc, *args, out)
    r = run_bass_kernel_spmd(nc, [arrays], core_ids=[0])
    return r.results[0]["out"]
```
